# Optimizing a Trainium2 kernel written in Bass

```python
import numpy as np
import jax
import jax.numpy as jnp

def _softmax(x, axis=-1):
    return jax.nn.softmax(x, axis=axis)

def _gelu(x):
    return jax.nn.gelu(x, approximate=True)

def _silu(x):
    return jax.nn.silu(x)

def _sigmoid(x):
    return jax.nn.sigmoid(x)

def _layernorm(x, axis=-1, eps=1e-05):
    m = jnp.mean(x, axis=axis, keepdims=True)
    v = jnp.var(x, axis=axis, keepdims=True)
    return (x - m) / jnp.sqrt(v + eps)

def _scatter_add(tgt, idx, src, axis=0):
    return tgt.at[idx].add(src)

def _segment_sum(src, seg, n):
    return jax.ops.segment_sum(src, seg, n)
kernel_name = 'mk_adaln_ffn_d1_seqx_r8_59e4d1'

def setup_inputs(seed: int=0):
    np.random.seed(seed)
    _w = jnp.asarray

    def _rec_inputs():
        import jax
        import jax.numpy as jnp
        _rk = jax.random.key(seed)
        x = 7.22e-05 + 1 * jax.random.normal(jax.random.fold_in(_rk, 1), (16, 128, 256), jnp.float32)
        _lenS = 128 - jax.random.randint(jax.random.fold_in(_rk, 7), (16,), 0, max(1, 128 // 4) + 1, jnp.int32)
        _lenS2 = 128 - jax.random.randint(jax.random.fold_in(_rk, 8), (16,), 0, max(1, 128 // 4) + 1, jnp.int32)
        cond_2048 = 0.0061147 + 1.02565 * jax.random.normal(jax.random.fold_in(_rk, 11), (16, 256), jnp.float32)
        return (x, cond_2048)
    x, cond_2048 = _rec_inputs()

    def _L0_cond_setup():
        import jax, jax.numpy as jnp
        import numpy as np
        DIM = 256
        H = 16
        DH = 128
        INNER = H * DH
        MLP = 4 * DIM
        B, T = (2, 256)
        EPS = 1e-06

        def _ln(x):
            mu = jnp.mean(x, axis=-1, keepdims=True)
            var = jnp.var(x, axis=-1, keepdims=True)
            return (x - mu) * jax.lax.rsqrt(var + EPS)
        key = jax.random.key(seed)
        ks = jax.random.split(key, 12)
        s = 0.02
        return {'x': jax.random.normal(ks[0], (B, T, DIM), jnp.float32), 'timestep_embed': jax.random.normal(ks[1], (B, DIM), jnp.float32), 'ada_w': jax.random.normal(ks[2], (DIM, 6 * DIM), jnp.float32) * s, 'ada_b': jnp.zeros((6 * DIM,), jnp.float32), 'qkv_w': jax.random.normal(ks[3], (DIM, 3 * INNER), jnp.float32) * s, 'qkv_b': jnp.zeros((3 * INNER,), jnp.float32), 'out_w': jax.random.normal(ks[4], (INNER, DIM), jnp.float32) * s, 'out_b': jnp.zeros((DIM,), jnp.float32), 'ffn_w1': jax.random.normal(ks[5], (DIM, MLP), jnp.float32) * s, 'ffn_b1': jnp.zeros((MLP,), jnp.float32), 'ffn_w2': jax.random.normal(ks[6], (MLP, DIM), jnp.float32) * s, 'ffn_b2': jnp.zeros((DIM,), jnp.float32)}
    _L0_cond_all = _L0_cond_setup()
    _L0_cond_in = {k: v for k, v in _L0_cond_all.items() if k in ('ada_w', 'ada_b', 'qkv_w', 'qkv_b', 'out_w', 'out_b', 'ffn_w1', 'ffn_b1', 'ffn_w2', 'ffn_b2')}
    del _L0_cond_all

    def _L0_ffn_setup():
        import jax, jax.numpy as jnp
        import numpy as np
        ROPE_THETA = 1000000.0
        TOP_K = 2

        def rmsnorm(x, w, eps=1e-06):
            xf = x.astype(jnp.float32)
            n = jax.lax.rsqrt(jnp.mean(xf * xf, axis=-1, keepdims=True) + eps)
            return (xf * n).astype(x.dtype) * w

        def rope_tables(seq_len, head_dim):
            freqs = 1.0 / ROPE_THETA ** (jnp.arange(0, head_dim, 2, dtype=jnp.float32) / head_dim)
            t = jnp.arange(seq_len, dtype=jnp.float32)
            f = jnp.outer(t, freqs)
            return (jnp.cos(f), jnp.sin(f))

        def apply_rope(x, cos, sin):
            half = x.shape[-1] // 2
            x1, x2 = (x[..., :half], x[..., half:])
            c = cos[None, None]
            s = sin[None, None]
            return jnp.concatenate([x1 * c - x2 * s, x2 * c + x1 * s], axis=-1)
        key = jax.random.key(seed)
        ks = jax.random.split(key, 8)
        B, S, D = (2, 256, 256)
        Hq, Hkv, hd = (16, 4, 128)
        E, I = (8, 176)
        sc = 0.02
        return {'hidden': jax.random.normal(ks[0], (B, S, D), jnp.float32), 'attn_norm_w': jnp.ones((D,), jnp.float32), 'q_w': jax.random.normal(ks[1], (Hq * hd, D), jnp.float32) * sc, 'k_w': jax.random.normal(ks[2], (Hkv * hd, D), jnp.float32) * sc, 'v_w': jax.random.normal(ks[3], (Hkv * hd, D), jnp.float32) * sc, 'o_w': jax.random.normal(ks[4], (D, Hq * hd), jnp.float32) * sc, 'q_norm_w': jnp.ones((hd,), jnp.float32), 'k_norm_w': jnp.ones((hd,), jnp.float32), 'ffn_norm_w': jnp.ones((D,), jnp.float32), 'gate_w': jax.random.normal(ks[5], (E, D), jnp.float32) * sc, 'wg': jax.random.normal(ks[6], (E, I, D), jnp.float32) * sc, 'wu': jax.random.normal(ks[7], (E, I, D), jnp.float32) * sc, 'wd': jax.random.normal(jax.random.fold_in(key, 99), (E, D, I), jnp.float32) * sc}
    _L0_ffn_all = _L0_ffn_setup()
    _L0_ffn_in = {k: v for k, v in _L0_ffn_all.items() if k in ('attn_norm_w', 'q_w', 'k_w', 'v_w', 'o_w', 'q_norm_w', 'k_norm_w', 'ffn_norm_w', 'gate_w', 'wg', 'wu', 'wd')}
    del _L0_ffn_all
    return {'x': x, 'cond_2048': cond_2048, 'L0_cond_ada_w': _L0_cond_in['ada_w'], 'L0_cond_ada_b': _L0_cond_in['ada_b'], 'L0_cond_qkv_w': _L0_cond_in['qkv_w'], 'L0_cond_qkv_b': _L0_cond_in['qkv_b'], 'L0_cond_out_w': _L0_cond_in['out_w'], 'L0_cond_out_b': _L0_cond_in['out_b'], 'L0_cond_ffn_w1': _L0_cond_in['ffn_w1'], 'L0_cond_ffn_b1': _L0_cond_in['ffn_b1'], 'L0_cond_ffn_w2': _L0_cond_in['ffn_w2'], 'L0_cond_ffn_b2': _L0_cond_in['ffn_b2'], 'L0_ffn_attn_norm_w': _L0_ffn_in['attn_norm_w'], 'L0_ffn_q_w': _L0_ffn_in['q_w'], 'L0_ffn_k_w': _L0_ffn_in['k_w'], 'L0_ffn_v_w': _L0_ffn_in['v_w'], 'L0_ffn_o_w': _L0_ffn_in['o_w'], 'L0_ffn_q_norm_w': _L0_ffn_in['q_norm_w'], 'L0_ffn_k_norm_w': _L0_ffn_in['k_norm_w'], 'L0_ffn_ffn_norm_w': _L0_ffn_in['ffn_norm_w'], 'L0_ffn_gate_w': _L0_ffn_in['gate_w'], 'L0_ffn_wg': _L0_ffn_in['wg'], 'L0_ffn_wu': _L0_ffn_in['wu'], 'L0_ffn_wd': _L0_ffn_in['wd']}

def reference(x, cond_2048, L0_cond_ada_w, L0_cond_ada_b, L0_cond_qkv_w, L0_cond_qkv_b, L0_cond_out_w, L0_cond_out_b, L0_cond_ffn_w1, L0_cond_ffn_b1, L0_cond_ffn_w2, L0_cond_ffn_b2, L0_ffn_attn_norm_w, L0_ffn_q_w, L0_ffn_k_w, L0_ffn_v_w, L0_ffn_o_w, L0_ffn_q_norm_w, L0_ffn_k_norm_w, L0_ffn_ffn_norm_w, L0_ffn_gate_w, L0_ffn_wg, L0_ffn_wu, L0_ffn_wd):
    import jax
    import jax.numpy as jnp

    def _L0_cond_ref(x, timestep_embed, ada_w, ada_b, qkv_w, qkv_b, out_w, out_b, ffn_w1, ffn_b1, ffn_w2, ffn_b2):
        import jax, jax.numpy as jnp
        import numpy as np
        DIM = 256
        H = 16
        DH = 128
        INNER = H * DH
        MLP = 4 * DIM
        B, T = (2, 256)
        EPS = 1e-06

        def _ln(x):
            mu = jnp.mean(x, axis=-1, keepdims=True)
            var = jnp.var(x, axis=-1, keepdims=True)
            return (x - mu) * jax.lax.rsqrt(var + EPS)
        Bc, Tc, D = x.shape
        ada = (timestep_embed @ ada_w + ada_b)[:, None, :]
        shift1, scale1, gate1, shift2, scale2, gate2 = jnp.split(ada, 6, axis=-1)
        x1 = _ln(x) * (1.0 + scale1) + shift1
        qkv = (x1 @ qkv_w + qkv_b).reshape(Bc, Tc, 3, H, DH)
        q, k, v = (qkv[:, :, 0], qkv[:, :, 1], qkv[:, :, 2])
        scale = DH ** (-0.5)
        attn = jnp.einsum('bthd,bshd->bhts', q, k) * scale
        attn = jax.nn.softmax(attn, axis=-1)
        attn_out = jnp.einsum('bhts,bshd->bthd', attn, v).reshape(Bc, Tc, INNER)
        attn_out = attn_out @ out_w + out_b
        x = x + gate1 * attn_out
        x2 = _ln(x) * (1.0 + scale2) + shift2
        h = jax.nn.gelu(x2 @ ffn_w1 + ffn_b1, approximate=False)
        x = x + gate2 * (h @ ffn_w2 + ffn_b2)
        return x

    def _L0_ffn_ref(hidden, attn_norm_w, q_w, k_w, v_w, o_w, q_norm_w, k_norm_w, ffn_norm_w, gate_w, wg, wu, wd):
        import jax, jax.numpy as jnp
        import numpy as np
        ROPE_THETA = 1000000.0
        TOP_K = 2

        def rmsnorm(x, w, eps=1e-06):
            xf = x.astype(jnp.float32)
            n = jax.lax.rsqrt(jnp.mean(xf * xf, axis=-1, keepdims=True) + eps)
            return (xf * n).astype(x.dtype) * w

        def rope_tables(seq_len, head_dim):
            freqs = 1.0 / ROPE_THETA ** (jnp.arange(0, head_dim, 2, dtype=jnp.float32) / head_dim)
            t = jnp.arange(seq_len, dtype=jnp.float32)
            f = jnp.outer(t, freqs)
            return (jnp.cos(f), jnp.sin(f))

        def apply_rope(x, cos, sin):
            half = x.shape[-1] // 2
            x1, x2 = (x[..., :half], x[..., half:])
            c = cos[None, None]
            s = sin[None, None]
            return jnp.concatenate([x1 * c - x2 * s, x2 * c + x1 * s], axis=-1)
        B, S, D = hidden.shape
        hd = q_norm_w.shape[0]
        Hq = q_w.shape[0] // hd
        Hkv = k_w.shape[0] // hd
        n_rep = Hq // Hkv
        h = rmsnorm(hidden, attn_norm_w)
        q = (h @ q_w.T).reshape(B, S, Hq, hd)
        k = (h @ k_w.T).reshape(B, S, Hkv, hd)
        v = (h @ v_w.T).reshape(B, S, Hkv, hd)
        q = rmsnorm(q, q_norm_w).transpose(0, 2, 1, 3)
        k = rmsnorm(k, k_norm_w).transpose(0, 2, 1, 3)
        v = v.transpose(0, 2, 1, 3)
        cos, sin = rope_tables(S, hd)
        q = apply_rope(q, cos, sin)
        k = apply_rope(k, cos, sin)
        k = jnp.repeat(k, n_rep, axis=1)
        v = jnp.repeat(v, n_rep, axis=1)
        scale = 1.0 / jnp.sqrt(jnp.float32(hd))
        scores = jnp.einsum('bhqd,bhkd->bhqk', q, k) * scale
        causal = jnp.tril(jnp.ones((S, S), bool))
        scores = jnp.where(causal[None, None], scores, jnp.finfo(scores.dtype).min)
        attn = jnp.einsum('bhqk,bhkd->bhqd', jax.nn.softmax(scores, axis=-1), v)
        attn = attn.transpose(0, 2, 1, 3).reshape(B, S, Hq * hd)
        hidden = hidden + attn @ o_w.T
        h2 = rmsnorm(hidden, ffn_norm_w)
        T = B * S
        E = gate_w.shape[0]
        tok = h2.reshape(T, D)
        probs = jax.nn.softmax(tok @ gate_w.T, axis=-1)
        topv, topi = jax.lax.top_k(probs, TOP_K)
        topw = topv / (jnp.sum(topv, axis=-1, keepdims=True) + 1e-09)
        combine = jnp.zeros((T, E), tok.dtype).at[jnp.arange(T)[:, None], topi].set(topw)
        eg = jnp.einsum('td,eid->eti', tok, wg)
        eu = jnp.einsum('td,eid->eti', tok, wu)
        eo = jnp.einsum('eti,edi->etd', jax.nn.silu(eg) * eu, wd)
        moe_out = jnp.einsum('te,etd->td', combine, eo).reshape(B, S, D)
        return hidden + moe_out
    x = x + _L0_ffn_ref(_L0_cond_ref(x, cond_2048, L0_cond_ada_w, L0_cond_ada_b, L0_cond_qkv_w, L0_cond_qkv_b, L0_cond_out_w, L0_cond_out_b, L0_cond_ffn_w1, L0_cond_ffn_b1, L0_cond_ffn_w2, L0_cond_ffn_b2), L0_ffn_attn_norm_w, L0_ffn_q_w, L0_ffn_k_w, L0_ffn_v_w, L0_ffn_o_w, L0_ffn_q_norm_w, L0_ffn_k_norm_w, L0_ffn_ffn_norm_w, L0_ffn_gate_w, L0_ffn_wg, L0_ffn_wu, L0_ffn_wd)
    return x

_drawn_inputs = setup_inputs


def setup_inputs(seed=0):
    import zlib

    import numpy as np

    out = dict(_drawn_inputs(seed))
    spreads = {'L0_cond_ada_b': (0.0, 0.593),
     'L0_cond_qkv_b': (0.0, 0.504),
     'L0_cond_out_b': (0.0, 0.419),
     'L0_cond_ffn_b1': (0.0, 0.8),
     'L0_cond_ffn_b2': (0.0, 0.407),
     'L0_ffn_attn_norm_w': (1.0, 0.6),
     'L0_ffn_q_norm_w': (1.0, 0.6),
     'L0_ffn_k_norm_w': (1.0, 0.6),
     'L0_ffn_ffn_norm_w': (1.0, 0.6)}
    factors = {'L0_cond_qkv_w': 3.074,
     'L0_cond_ffn_w1': 2.693,
     'L0_ffn_gate_w': 8.0,
     'L0_ffn_wg': 8.0,
     'L0_ffn_wu': 8.0,
     'L0_ffn_wd': 8.0}
    for name, (base, spread) in spreads.items():
        noise = np.random.default_rng([zlib.crc32(name.encode()), seed]).standard_normal(out[name].shape)
        drawn = base * np.exp(spread * noise) if base else spread * noise
        out[name] = jnp.asarray(drawn.astype(out[name].dtype))
    for name, factor in factors.items():
        out[name] = (out[name] * factor).astype(out[name].dtype)
    return out
```

```python
import concourse.bass as bass
from concourse import mybir
from contextlib import ExitStack

F32 = mybir.dt.float32
F32R = mybir.dt.float32r
BF16 = mybir.dt.bfloat16
ALU = mybir.AluOpType
ACT = mybir.ActivationFunctionType
X = mybir.AxisListType.X

B, T, D = 16, 128, 256
P = 128
KD = D // P
GB = 4
NG = B // GB
GT = GB * T
H, DH = 16, 128
HKV = 4
REP = H // HKV
F1 = 1024
NF = F1 // P
E, I = 8, 176
NR = E * I // P
SCALE = DH ** -0.5
EPS = 1e-6
KB = 1024


def program(nc, ins, out):
    ctx = ExitStack()
    with ctx:
        place = {}
        cursor = [16512]

        def sb(name, shape, dtype=F32, at=None):
            size = 4 if dtype in (F32, F32R) else 2
            for n in shape[1:]:
                size *= n
            size = -(-size // 32) * 32
            if at is None:
                at = cursor[0]
                cursor[0] += size
            place[name] = (at, at + size)
            return nc.alloc_sbuf_tensor_at(name, shape, dtype, offset=at)

        def sem(name):
            return ctx.enter_context(nc.semaphore(name))

        xres = sb("xres", [P, B, D])
        act_t = sb("act_t", [P, KD, B * T])
        cur_hi = sb("cur_hi", [P, KD, GT], F32R)
        cur_lo = sb("cur_lo", [P, KD, GT], F32R)
        gate = sb("gate", [P, GB, D])
        xn = sb("xn", [P, GB, D], at=place["gate"][0])
        obias = sb("obias", [P, D])
        ident = sb("ident", [P, P])
        ada_t = sb("ada_t", [P, 4, KD, B])
        ada_bt = sb("ada_bt", [P, 12])
        bqkv = sb("bqkv", [P, 3, H])
        b1 = sb("b1", [P, NF])
        norm_w = sb("norm_w", [P, 2, KD])
        bn = sb("bn", [P, GB, 6])
        mv = sb("mv", [P, GB, 2])
        vare = sb("vare", [P, GB])
        rstd = sb("rstd", [P, GB])
        mean2 = sb("mean2", [P, GB])
        neg_half = sb("neg_half", [P, 8])
        eps = sb("eps", [P, 8])
        nmax = sb("nmax", [P, 2, GB])
        rsum = sb("rsum", [P, 2, GB])
        rinv = sb("rinv", [P, 2, GB])
        W = cursor[0]
        WORK = W + 128 * KB

        wqk_hi = sb("wqk_hi", [P, H, 2, KD, DH], F32R, at=W)
        wqk_lo = sb("wqk_lo", [P, H, 2, KD, DH], F32R, at=W + 32 * KB)
        wqk_raw = sb("wqk_raw", [P, H, 2, KD, DH], at=W + 32 * KB)
        wv_hi = sb("wv_hi", [P, KD, H * DH], F32R, at=W + 64 * KB)
        wv_lo = sb("wv_lo", [P, KD, H * DH], F32R, at=W + 80 * KB)
        wv_raw = sb("wv_raw", [P, KD, H * DH], at=W + 80 * KB)
        wo_hi = sb("wo_hi", [P, H, D], F32R, at=W + 96 * KB)
        wo_lo = sb("wo_lo", [P, H, D], F32R, at=W + 112 * KB)
        wo_raw = sb("wo_raw", [P, H, D], at=W + 112 * KB)
        q1 = sb("q1", [P, 2, GT], at=WORK)
        k1 = sb("k1", [P, 2, GT], at=WORK + 4 * KB)
        v1 = sb("v1", [P, 2, GB, 2 * DH], at=WORK + 8 * KB)
        p1 = sb("p1", [P, 2, GB, T], at=WORK + 16 * KB)
        pt1 = sb("pt1", [P, GT], at=WORK + 20 * KB)
        o1_hi = sb("o1_hi", [P, 2, GT], F32R, at=WORK + 22 * KB)
        o1_lo = sb("o1_lo", [P, 2, GT], F32R, at=WORK + 26 * KB)
        ada_w = sb("ada_w", [P, KD, 6 * D], at=WORK)
        cond_t = sb("cond_t", [P, KD, B], at=WORK + 12 * KB)
        ada_bg = sb("ada_bg", [B, 2, D], at=WORK + 13 * KB)
        gates = sb("gates", [B, 2, D], at=WORK + 15 * KB)
        w1_hi = sb("w1_hi", [P, NF, KD, P], F32R, at=W + 16 * KB)
        w1_lo = sb("w1_lo", [P, NF, KD, P], F32R, at=W)
        w1_raw = sb("w1_raw", [P, NF, KD, P], at=W)
        w2_hi = sb("w2_hi", [P, NF, D], F32R, at=W + 24 * KB)
        w2_lo = sb("w2_lo", [P, NF, D], F32R, at=W + 8 * KB)
        w2_raw = sb("w2_raw", [P, NF, D], at=W + 8 * KB)
        hf = sb("hf", [P, 2, GT], at=WORK)
        h_hi = sb("h_hi", [P, 2, GT], F32R, at=WORK + 4 * KB)
        h_lo = sb("h_lo", [P, 2, GT], F32R, at=WORK + 8 * KB)

        wq_hi = sb("wq_hi", [P, KD, H * DH], F32R, at=W + 32 * KB)
        wq_lo = sb("wq_lo", [P, KD, H * DH], F32R, at=W + 48 * KB)
        wq_raw = sb("wq_raw", [P, KD, H * DH], at=W + 48 * KB)
        wkv_hi = sb("wkv_hi", [P, KD, 2 * HKV * DH], F32R, at=W + 64 * KB)
        wkv_lo = sb("wkv_lo", [P, KD, 2 * HKV * DH], F32R, at=W + 72 * KB)
        wkv_raw = sb("wkv_raw", [P, KD, 2 * HKV * DH], at=W + 72 * KB)
        wo2_hi = sb("wo2_hi", [P, H, D], F32R, at=W + 80 * KB)
        wo2_lo = sb("wo2_lo", [P, H, D], F32R, at=W + 96 * KB)
        wo2_raw = sb("wo2_raw", [P, H, D], at=W + 96 * KB)
        W2 = W + 112 * KB
        qr = sb("qr", [P, 2, REP * DH], at=W2)
        rb = sb("rb", [P, REP * DH], at=W2 + 4 * KB)
        sq = sb("sq", [P, REP * DH], at=W2 + 6 * KB)
        kr = sb("kr", [P, HKV * DH], at=W2 + 8 * KB)
        kb = sb("kb", [P, HKV * DH], at=W2 + 10 * KB)
        ksq = sb("ksq", [P, HKV * DH], at=W2 + 12 * KB)
        q_t = sb("q_t", [P, REP * T], at=W2 + 14 * KB)
        k_t = sb("k_t", [P, 2, HKV * T], at=W2 + 16 * KB)
        v_hi = sb("v_hi", [P, 2, HKV * DH], F32R, at=W2 + 20 * KB)
        v_lo = sb("v_lo", [P, 2, HKV * DH], F32R, at=W2 + 24 * KB)
        p2 = sb("p2", [P, 2, REP, T], at=W2 + 28 * KB)
        pt_hi = sb("pt_hi", [P, REP * T], F32R, at=W2 + 32 * KB)
        pt_lo = sb("pt_lo", [P, REP * T], F32R, at=W2 + 34 * KB)
        o2_hi = sb("o2_hi", [P, REP * T], F32R, at=W2 + 36 * KB)
        o2_lo = sb("o2_lo", [P, REP * T], F32R, at=W2 + 38 * KB)
        rope = sb("rope", [P, 4, DH], at=W2 + 40 * KB)
        cos_sin = sb("cos_sin", [P, 2, DH], at=W2 + 42 * KB)
        mask = sb("mask", [P, REP * T], BF16, at=W2 + 43 * KB)
        ident_b = sb("ident_b", [P, P], BF16, at=W2 + 44 * KB)
        mask_f = sb("mask_f", [P, T], at=W2 + 44 * KB + 256)
        small = W2 + 44 * KB + 768
        q_ms = sb("q_ms", [P, 2, REP], at=small)
        q_ve = sb("q_ve", [P, 2, REP], at=small + 32)
        rq = sb("rq", [P, 4, REP], at=small + 64)
        k_ms = sb("k_ms", [P, HKV], at=small + 128)
        k_ve = sb("k_ve", [P, HKV], at=small + 160)
        rk = sb("rk", [P, HKV], at=small + 192)
        nb = sb("nb", [P, 2, REP], at=small + 224)
        wg_hi = sb("wg_hi", [P, NR, KD, P], F32R, at=W)
        wg_lo = sb("wg_lo", [P, NR, KD, P], F32R, at=W + 11 * KB)
        wg_raw = sb("wg_raw", [P, NR, KD, P], at=W + 11 * KB)
        sel = sb("sel", [E, NR, P], F32R, at=W + 22 * KB)
        sel_f = sb("sel_f", [E, NR, P], at=W + 22 * KB)
        rw_raw = sb("rw_raw", [P, KD, E], at=W + 28 * KB)
        rw_hi = sb("rw_hi", [P, KD, E], F32R, at=W + 28 * KB + 64)
        rw_lo = sb("rw_lo", [P, KD, E], F32R, at=W + 28 * KB + 128)
        before = sb("before", [P, E, E], at=W + 28 * KB + 256)
        wu_hi = sb("wu_hi", [P, NR, KD, P], F32R, at=W + 32 * KB)
        wu_lo = sb("wu_lo", [P, NR, KD, P], F32R, at=W + 43 * KB)
        wu_raw = sb("wu_raw", [P, NR, KD, P], at=W + 43 * KB)
        wd_hi = sb("wd_hi", [P, NR, D], F32R, at=W + 54 * KB)
        wd_lo = sb("wd_lo", [P, NR, D], F32R, at=W + 65 * KB)
        wd_raw = sb("wd_raw", [P, NR, D], at=W + 65 * KB)
        sg = sb("sg", [P, 2, GT], at=W2)
        em = sb("em", [P, 2, GT], at=W2 + 4 * KB)
        e_hi = sb("e_hi", [P, 2, GT], F32R, at=W2 + 8 * KB)
        e_lo = sb("e_lo", [P, 2, GT], F32R, at=W2 + 12 * KB)
        x0 = sb("x0", [P, GB, D], at=W2 + 16 * KB)
        y = sb("y", [P, GB, D], at=W2 + 20 * KB)
        ct_hi = sb("ct_hi", [E, GT], F32R, at=W2 + 24 * KB)
        ct_lo = sb("ct_lo", [E, GT], F32R, at=W2 + 26 * KB)
        gt = sb("gt", [P, GB, E, E], at=W2 + 28 * KB)
        eq = sb("eq", [P, GB, E, E], at=W2 + 29 * KB)
        probs = sb("probs", [P, GB, E], at=W2 + 30 * KB)
        pick = sb("pick", [P, GB, E], at=W2 + 30 * KB + 128)
        comb = sb("comb", [P, GB, E], at=W2 + 30 * KB + 256)
        r4 = sb("r4", [P, 4, GB], at=W2 + 30 * KB + 384)

        bank = [ctx.enter_context(nc.psum_tensor(f"bank{i}", [P, 512], F32)) for i in range(8)]
        gates_dram = nc.dram_tensor("gates_scratch", (B, 2, D), F32).ap()

        d_x = [sem(f"d_x{g}") for g in range(NG)]
        d_small = sem("d_small")
        d_adaw = sem("d_adaw")
        d_wqk = [sem(f"d_wqk{c}") for c in range(4)]
        d_wv = [sem(f"d_wv{c}") for c in range(4)]
        d_wo = [sem(f"d_wo{c}") for c in range(4)]
        d_gout = sem("d_gout")
        d_gate = sem("d_gate")
        d_wq, d_wkv, d_oproj, d_rope = sem("d_wq"), sem("d_wkv"), sem("d_oproj"), sem("d_rope")
        d_wg, d_wu, d_wd, d_rw, d_xin = sem("d_wg"), sem("d_wu"), sem("d_wd"), sem("d_rw"), sem("d_xin")
        d_w1, d_w2, d_b2 = sem("d_w1"), sem("d_w2"), sem("d_b2")
        d_out = sem("d_out")
        consts, ada_p, ada_s, bq_s = sem("consts"), sem("ada_p"), sem("ada_s"), sem("bq_s")
        w_hi1, w_lo1 = sem("w_hi1"), sem("w_lo1")
        w_hi2, w_lo2 = sem("w_hi2"), sem("w_lo2")
        n_bn, n_mv, n_st, n_ve, n_rs, n_xn, n_tp, n_ev = (
            sem(f"n_{x}") for x in ("bn", "mv", "st", "ve", "rs", "xn", "tp", "ev"))
        n_m2 = sem("n_m2")
        c_hi, c_lo = sem("c_hi"), sem("c_lo")
        a_qp, a_kp, a_vp, a_sp, a_tp, a_pvp, a_op = (
            sem(f"a_{x}") for x in ("qp", "kp", "vp", "sp", "tp", "pvp", "op"))
        a_q, a_k, a_v, a_mx, a_ex, a_ri, a_pn, a_pt, a_oh, a_ol = (
            sem(f"a_{x}") for x in ("q", "k", "v", "mx", "ex", "ri", "pn", "pt", "oh", "ol"))
        r_add, r_mul, r_x = sem("r_add"), sem("r_mul"), sem("r_x")
        f_up, f_dp, f_g, f_h, f_l = (sem(f"f_{x}") for x in ("up", "dp", "g", "h", "l"))

        w_hi3, w_lo3, g_tab, g_mask = sem("w_hi3"), sem("w_lo3"), sem("g_tab"), sem("g_mask")
        g_kp, g_vp, g_qp, g_tp, g_qtp, g_op, g_pvp, g_ktp, g_sp = (
            sem(f"g_{x}") for x in ("kp", "vp", "qp", "tp", "qtp", "op", "pvp", "ktp", "sp"))
        g_ex, g_ksq, g_sq, g_ph, g_vh, g_qt, g_oh, g_kt = (
            sem(f"g_{x}") for x in ("ex", "ksq", "sq", "ph", "vh", "qt", "oh", "kt"))
        g_x, g_mx, g_nb, g_kb, g_qb, g_ks, g_kr, g_pl, g_ss, g_ri, g_vl, g_ol = (
            sem(f"g_{x}") for x in ("x", "mx", "nb", "kb", "qb", "ks", "kr", "pl", "ss", "ri", "vl", "ol"))
        g_ka, g_rk, g_kv, g_qr, g_rq, g_qv, g_pn = (
            sem(f"g_{x}") for x in ("ka", "rk", "kv", "qr", "rq", "qv", "pn"))
        w_hi4, w_lo4, m_sel = sem("w_hi4"), sem("w_lo4"), sem("m_sel")
        m_gp, m_up, m_cp, m_dp, m_sg, m_su, m_em, m_h, m_l, m_y, m_o = (
            sem(f"m_{x}") for x in ("gp", "up", "cp", "dp", "sg", "su", "em", "h", "l", "y", "o"))
        t_lp, t_ctp, t_ex, t_h, t_l, t_v, t_c = (sem(f"t_{x}") for x in ("lp", "ctp", "ex", "h", "l", "v", "c"))
        RV = 13

        block = ctx.enter_context(nc.Block())

        class Step:

            def __init__(self, g, u, first):
                self.g, self.u, self.first = g, u, first
                self.n, self.b, self.kv = g * 4 * GB + u, u // HKV, u % HKV
                self.seq = g * GB + self.b

            def new(self):
                return self.u < 4 * GB

            def live(self, k):
                return self.had(k) and self.u - k < 4 * GB

            def had(self, k):
                return self.u >= k or not self.first

        def attention2(eng, step):
            for u in range(4 * GB):
                step(Step(0, u, True))
            with eng.Fori(1, NG) as g:
                for u in range(4 * GB):
                    step(Step(g, u, False))
            for u in range(4 * GB, 5 * GB + 1):
                step(Step(NG - 1, u, False))

        def span(t, k, g, b0=0, nb=GB):
            return t[:, k, bass.ds((g * GB + b0) * T, nb * T)]

        def split_products(hi_l, lo_l, hi_r, lo_r):
            return ((hi_l, hi_r), (hi_l, lo_r), (lo_l, hi_r))

        @block.sync
        def _(sp):
            for g in range(NG):
                sp.dma_start(xres[:, g * GB:(g + 1) * GB, :],
                             ins["x"][g * GB:(g + 1) * GB].rearrange("b t d -> t b d")).then_inc(d_x[g], 16)
                if g == 0:
                    sp.dma_start(cond_t[:], ins["cond_t"]).then_inc(d_small, 16)
                    sp.dma_start(ada_bt[:], ins["ada_bt"]).then_inc(d_small, 16)
                    sp.dma_start(ada_bg[:], ins["ada_bg"]).then_inc(d_small, 16)
                    sp.dma_start(bqkv[:], ins["bqkv"]).then_inc(d_small, 16)
                    sp.dma_start(b1[:], ins["b1"]).then_inc(d_small, 16)
                    sp.dma_start(norm_w[:], ins["norm_w"]).then_inc(d_small, 16)
                    sp.dma_start(obias[:], ins["out_b"].partition_broadcast(P)).then_inc(d_small, 16)
                    sp.dma_start(ada_w[:], ins["ada_w"]).then_inc(d_adaw, 16)
            for c in range(4):
                hs = slice(4 * c, 4 * c + 4)
                sp.dma_start(wqk_raw[:, hs], ins["wqk"][:, hs]).then_inc(d_wqk[c], 16)
                cs = slice(512 * c, 512 * c + 512)
                sp.dma_start(wv_raw[:, :, cs], ins["wv"][:, :, cs]).then_inc(d_wv[c], 16)
                sp.dma_start(wo_raw[:, hs], ins["wo"][:, hs]).then_inc(d_wo[c], 16)
            sp.wait_ge(d_gout, 16)
            sp.wait_ge(n_tp, 2 * NG)
            sp.dma_start(gate[:], gates_dram[0:GB, 0, :].partition_broadcast(P)).then_inc(d_gate, 16)
            with sp.Fori(1, NG) as g:
                sp.wait_ge(n_tp, 2 * (NG + g))
                sp.dma_start(gate[:], gates_dram[bass.ds(g * GB, GB), 0, :].partition_broadcast(P)).then_inc(d_gate, 16)
            sp.wait_ge(a_kp, 3 * H + 8)
            sp.dma_start(w1_raw[:], ins["w1"]).then_inc(d_w1, 16)
            sp.dma_start(w2_raw[:], ins["w2"]).then_inc(d_w2, 16)
            sp.wait_ge(a_vp, NG * H)
            sp.dma_start(wkv_raw[:], ins["wkv"]).then_inc(d_wkv, 16)
            sp.dma_start(wq_raw[:], ins["wq"]).then_inc(d_wq, 16)
            sp.wait_ge(a_op, NG * H)
            sp.dma_start(wo2_raw[:], ins["wo2"]).then_inc(d_oproj, 16)
            sp.dma_start(rope[:], ins["qk_norm"].partition_broadcast(P)).then_inc(d_rope, 16)
            sp.dma_start(cos_sin[:], ins["cos_sin"]).then_inc(d_rope, 16)
            sp.wait_ge(r_add, 2 * NG)
            sp.dma_start(obias[:], ins["b2"].partition_broadcast(P)).then_inc(d_b2, 16)
            sp.wait_ge(n_tp, 2 * (2 * NG))
            sp.dma_start(gate[:], gates_dram[0:GB, 1, :].partition_broadcast(P)).then_inc(d_gate, 16)
            with sp.Fori(1, NG) as g:
                sp.wait_ge(n_tp, 2 * (2 * NG + g))
                sp.dma_start(gate[:], gates_dram[bass.ds(g * GB, GB), 1, :].partition_broadcast(P)).then_inc(d_gate, 16)
            sp.wait_ge(f_up, NG * NF)
            sp.wait_ge(f_dp, NG * NF)
            sp.dma_start(wg_raw[:], ins["wg"]).then_inc(d_wg, 16)
            sp.dma_start(rw_raw[:], ins["rw"]).then_inc(d_rw, 16)
            sp.wait_ge(g_qp, NG * 4 * GB)
            sp.wait_ge(g_vp, B)
            sp.dma_start(wu_raw[:], ins["wu"]).then_inc(d_wu, 16)
            sp.dma_start(wd_raw[:], ins["wd"]).then_inc(d_wd, 16)
            sp.wait_ge(g_x, B)
            sp.dma_start(x0[:], ins["x"][0:GB].rearrange("b t d -> t b d")).then_inc(d_xin, 16)
            sp.wait_ge(m_y, 4)
            sp.dma_start(out[0:GB].rearrange("b t d -> t b d"), y[:]).then_inc(d_out, 16)
            with sp.Fori(1, NG) as g:
                sp.dma_start(x0[:], ins["x"][bass.ds(g * GB, GB)].rearrange("b t d -> t b d")).then_inc(d_xin, 16)
                sp.wait_ge(m_y, 4 * g + 4)
                sp.dma_start(out[bass.ds(g * GB, GB)].rearrange("b t d -> t b d"), y[:]).then_inc(d_out, 16)
            sp.wait_ge(d_out, 16 * NG)

        @block.gpsimd
        def _(pool):
            nc.gpsimd.memset(neg_half[:], -0.5).then_inc(consts, 1)
            nc.gpsimd.memset(ident[:], 0.0).then_inc(consts, 1)
            nc.gpsimd.memset(eps[:], EPS).then_inc(consts, 1)
            pool.wait_ge(consts, 3)
            nc.gpsimd.affine_select(out=ident[:], in_=ident[:], compare_op=ALU.not_equal, fill=1.0, base=0,
                                    pattern=[[-1, P]], channel_multiplier=1).then_inc(consts, 1)

            def norm(n, rms=False):
                pool.wait_ge(n_st, n + 1)
                nc.gpsimd.tensor_tensor(vare[:], mv[:, :, 1], eps[:, 0:GB], ALU.add).then_inc(n_ve, 1)
                if rms:
                    nc.gpsimd.tensor_tensor(mean2[:], mv[:, :, 0], mv[:, :, 0], ALU.mult).then_inc(n_m2, 1)
                    pool.wait_ge(n_m2, 2 * (n - 2 * NG) + 1)
                    pool.wait_ge(n_ve, n + 1)
                    nc.gpsimd.tensor_tensor(vare[:], vare[:], mean2[:], ALU.add).then_inc(n_m2, 1)
                    pool.wait_ge(n_m2, 2 * (n - 2 * NG) + 2)
                pool.wait_ge(n_ve, n + 1)
                nc.gpsimd.tensor_tensor(rstd[:], vare[:], neg_half[:, 0:GB], ALU.pow).then_inc(n_rs, 1)

            for g in range(NG):
                norm(g)

            def normalise(n, h):
                pool.wait_ge(a_ri, n + 1)
                nc.gpsimd.tensor_tensor(p1[:, h % 2], p1[:, h % 2],
                                        rinv[:, h % 2].unsqueeze(2).broadcast_to([P, GB, T]),
                                        ALU.mult).then_inc(a_pn, 1)

            def attention1(g, first):
                for h in range(H):
                    if h >= 1 or not first:
                        normalise(g * H + h - 1, (h - 1) % 2)
                    if h == 3 and not first:
                        norm(NG + g - 1)

            attention1(0, True)
            with pool.Fori(1, NG) as g:
                attention1(g, False)
            normalise(NG * H - 1, 1)
            norm(2 * NG - 1)

            pool.wait_ge(a_op, NG * H)
            nc.gpsimd.memset(mask_f[:], 0.0).then_inc(g_mask, 1)
            pool.wait_ge(g_mask, 1)
            nc.gpsimd.affine_select(out=mask_f[:], in_=mask_f[:], compare_op=ALU.is_ge, fill=-1e30, base=0,
                                    pattern=[[-1, T]], channel_multiplier=1).then_inc(g_mask, 1)

            for g in range(NG):
                norm(2 * NG + g, True)
            pool.wait_ge(f_dp, NG * NF)
            nc.gpsimd.memset(sel_f[:], 1.0).then_inc(m_sel, 1)
            nc.gpsimd.memset(before[:], 1.0).then_inc(m_sel, 1)
            pool.wait_ge(m_sel, 2)
            nc.gpsimd.affine_select(out=sel_f[:], in_=sel_f[:], compare_op=ALU.is_ge, fill=0.0, base=0,
                                    pattern=[[P, NR], [1, P]], channel_multiplier=-I).then_inc(m_sel, 1)
            nc.gpsimd.affine_select(out=before[:], in_=before[:], compare_op=ALU.is_gt, fill=0.0, base=0,
                                    pattern=[[1, E], [-1, E]], channel_multiplier=0).then_inc(m_sel, 1)
            pool.wait_ge(m_sel, 4)
            nc.gpsimd.affine_select(out=sel_f[:], in_=sel_f[:], compare_op=ALU.is_ge, fill=0.0, base=I - 1,
                                    pattern=[[-P, NR], [-1, P]], channel_multiplier=I).then_inc(m_sel, 1)

            def step(s):
                n, new_seq = s.n, s.new() and s.kv == 0
                if new_seq:
                    pool.wait_ge(g_kb, s.seq + 1)
                    nc.gpsimd.tensor_tensor(kr[:], kr[:], kb[:], ALU.add).then_inc(g_ka, 1)
                if s.new():
                    pool.wait_ge(g_qb, n + 1)
                    nc.gpsimd.tensor_tensor(qr[:, s.u % 2], qr[:, s.u % 2], rb[:], ALU.add).then_inc(g_qr, 1)
                if s.live(2):
                    pool.wait_ge(g_ri, n - 1)
                    nc.gpsimd.tensor_tensor(p2[:, s.u % 2], p2[:, s.u % 2],
                                            rinv[:, s.u % 2].unsqueeze(2).broadcast_to([P, REP, T]),
                                            ALU.mult).then_inc(g_pn, 1)
                if s.new():
                    pool.wait_ge(g_ss, n + 1)
                    if s.had(2):
                        pool.wait_ge(g_rq, n - 1)
                    nc.gpsimd.tensor_tensor(q_ve[:, s.u % 2], q_ms[:, s.u % 2], eps[:, 0:REP], ALU.add).then_inc(g_qv, 1)
                    pool.wait_ge(g_qv, n + 1)
                    if s.had(4):
                        pool.wait_ge(g_ex, n - 3)
                    nc.gpsimd.tensor_tensor(rq[:, s.u % 4], q_ve[:, s.u % 2], neg_half[:, 0:REP], ALU.pow).then_inc(g_rq, 1)
                if new_seq:
                    pool.wait_ge(g_ks, s.seq + 1)
                    if s.had(4):
                        pool.wait_ge(g_rk, s.seq)
                    nc.gpsimd.tensor_tensor(k_ve[:], k_ms[:], eps[:, 0:HKV], ALU.add).then_inc(g_kv, 1)
                    pool.wait_ge(g_kv, s.seq + 1)
                    nc.gpsimd.tensor_tensor(rk[:], k_ve[:], neg_half[:, 0:HKV], ALU.pow).then_inc(g_rk, 1)
                if s.u == 6 and not s.first:
                    norm(3 * NG + s.g - 1, True)

            attention2(pool, step)
            norm(4 * NG - 1, True)

        @block.scalar
        def _(act):
            def cur(c, g):
                nc.scalar.activation(cur_hi[:], act_t[:, :, bass.ds(g * GT, GT)], ACT.Copy).then_inc(c_hi, 1)

            act.wait_ge(d_small, 7 * 16)
            nc.scalar.activation(bqkv[:, 0], bqkv[:, 0], ACT.Copy, scale=SCALE).then_inc(bq_s, 1)
            for c in range(4):
                hs, cs = slice(4 * c, 4 * c + 4), slice(512 * c, 512 * c + 512)
                act.wait_ge(d_wqk[c], 16)
                nc.scalar.activation(wqk_hi[:, hs], wqk_raw[:, hs], ACT.Copy).then_inc(w_hi1, 1)
                act.wait_ge(d_wv[c], 16)
                nc.scalar.activation(wv_hi[:, :, cs], wv_raw[:, :, cs], ACT.Copy).then_inc(w_hi1, 1)
                act.wait_ge(d_wo[c], 16)
                nc.scalar.activation(wo_hi[:, hs], wo_raw[:, hs], ACT.Copy).then_inc(w_hi1, 1)
                if c == 0:
                    act.wait_ge(ada_s, 9)
                    act.dma_start(gates_dram, gates[:]).then_inc(d_gout, 16)

            def exps(n, h):
                act.wait_ge(a_mx, n + 1)
                if not isinstance(n, int) or n >= 2:
                    act.wait_ge(a_tp, n - 1)
                for b in range(GB):
                    last = nc.scalar.activation(p1[:, h % 2, b], bank[3][:, b * T:(b + 1) * T], ACT.Exp,
                                                bias=nmax[:, h % 2, b:b + 1], accum_out=rsum[:, h % 2, b:b + 1])
                last.then_inc(a_ex, 1)

            def o_hi(n, h):
                act.wait_ge(a_pvp, n + 1)
                if not isinstance(n, int) or n >= 2:
                    act.wait_ge(a_op, n - 1)
                nc.scalar.activation(o1_hi[:, h % 2], bank[5][:], ACT.Identity,
                                     bias=bqkv[:, 2, h:h + 1]).then_inc(a_oh, 1)

            def attention1(g, first):
                if first:
                    act.wait_ge(d_gout, 16)
                for h in range(H):
                    n = g * H + h
                    if h == 0:
                        act.wait_ge(n_ev, 2 * (g + 1))
                        if not first:
                            act.wait_ge(a_vp, n)
                        cur(g, g)
                    if h >= 1 or not first:
                        exps(n - 1, (h - 1) % 2)
                    act.wait_ge(a_qp, n + 1)
                    if h >= 2 or not first:
                        act.wait_ge(a_sp, n - 1)
                    nc.scalar.activation(q1[:, h % 2], bank[0][:], ACT.Identity, scale=SCALE,
                                         bias=bqkv[:, 0, h:h + 1]).then_inc(a_q, 1)
                    if h >= 2 or not first:
                        o_hi(n - 2, (h - 2) % H)
                    act.wait_ge(a_vp, n + 1)
                    if h >= 4 or not first:
                        act.wait_ge(a_pvp, n - h % 2 - 2)
                    nc.scalar.activation(v1[:, h // 2 % 2, h % 2 * 2:h % 2 * 2 + 2],
                                         bank[2][:].rearrange("p (b d) -> p b d", b=2), ACT.Copy).then_inc(a_v, 1)

            attention1(0, True)
            with act.Fori(1, NG) as g:
                attention1(g, False)
            n = NG * H
            exps(n - 1, 1)
            o_hi(n - 2, H - 2)
            o_hi(n - 1, H - 1)

            act.wait_ge(d_w1, 16)
            act.wait_ge(a_kp, NG * H)
            nc.scalar.activation(w1_hi[:], w1_raw[:], ACT.Copy).then_inc(w_hi2, 1)
            act.wait_ge(d_w2, 16)
            nc.scalar.activation(w2_hi[:], w2_raw[:], ACT.Copy).then_inc(w_hi2, 1)

            def split3(c):
                if isinstance(c, int):
                    act.wait_ge(d_wkv, 16)
                nc.scalar.activation(wkv_hi[:, :, bass.ds(c * 256, 256)], wkv_raw[:, :, bass.ds(c * 256, 256)],
                                     ACT.Copy).then_inc(w_hi3, 1)
                nc.scalar.activation(wq_hi[:, :, bass.ds(c * 512, 512)], wq_raw[:, :, bass.ds(c * 512, 512)],
                                     ACT.Copy).then_inc(w_hi3, 1)
                nc.scalar.activation(wo2_hi[:, bass.ds(c * 4, 4)], wo2_raw[:, bass.ds(c * 4, 4)],
                                     ACT.Copy).then_inc(w_hi3, 1)

            def ffn1(g, first):
                for f in range(NF):
                    m = g * NF + f
                    if f == 4 and not first:
                        act.wait_ge(d_wkv, 16)
                        act.wait_ge(d_wq, 16)
                        act.wait_ge(d_oproj, 16)
                        act.wait_ge(a_op, NG * H)
                        split3(g - 1)
                    if f == 0:
                        act.wait_ge(n_ev, 2 * (NG + g + 1))
                        if first:
                            act.wait_ge(a_vp, NG * H)
                        else:
                            act.wait_ge(f_up, m)
                        cur(NG + g, g)
                    act.wait_ge(f_up, m + 1)
                    if f >= 2 or not first:
                        act.wait_ge(f_l, m - 1)
                    nc.scalar.activation(hf[:, f % 2], bank[f % 2][:], ACT.Gelu, bias=b1[:, f:f + 1]).then_inc(f_g, 1)
                    act.wait_ge(f_g, m + 1)
                    if f >= 2 or not first:
                        act.wait_ge(f_dp, m - 1)
                    nc.scalar.activation(h_hi[:, f % 2], hf[:, f % 2], ACT.Copy).then_inc(f_h, 1)

            ffn1(0, True)
            with act.Fori(1, NG) as g:
                ffn1(g, False)
            split3(NG - 1)

            def step(s):
                n, new_seq = s.n, s.new() and s.kv == 0
                if s.u == 0:
                    act.wait_ge(n_ev, 2 * (2 * NG + s.g + 1))
                    if s.first:
                        act.wait_ge(f_up, NG * NF)
                    else:
                        act.wait_ge(g_qp, n)
                    cur(2 * NG + s.g, s.g)
                if s.live(2):
                    act.wait_ge(g_nb, n - 1)
                    if s.had(4):
                        act.wait_ge(g_tp, n - 3)
                    for j in range(REP):
                        last = nc.scalar.activation(p2[:, s.u % 2, j], bank[3][:, j * T:(j + 1) * T], ACT.Exp,
                                                    scale=rq[:, (s.u - 2) % 4, j:j + 1], bias=nb[:, s.u % 2, j:j + 1],
                                                    accum_out=rsum[:, s.u % 2, j:j + 1])
                    last.then_inc(g_ex, 1)
                if new_seq:
                    act.wait_ge(g_kb, s.seq + 1)
                    if s.had(4):
                        act.wait_ge(g_ks, s.seq)
                    nc.scalar.activation(ksq[:], bank[1][:], ACT.Square, scale=SCALE).then_inc(g_ksq, 1)
                if s.new():
                    act.wait_ge(g_qb, n + 1)
                    if s.had(1):
                        act.wait_ge(g_ss, n)
                    nc.scalar.activation(sq[:], bank[0][:], ACT.Square, scale=SCALE).then_inc(g_sq, 1)
                if s.live(3):
                    act.wait_ge(g_tp, n - 2)
                    if s.had(4):
                        act.wait_ge(g_pvp, n - 3)
                    nc.scalar.activation(pt_hi[:], bank[5][:], ACT.Copy).then_inc(g_ph, 1)
                if new_seq:
                    act.wait_ge(g_vp, s.seq + 1)
                    if s.had(8):
                        act.wait_ge(g_pvp, 4 * (s.seq - 1))
                    nc.scalar.activation(v_hi[:, s.b % 2], bank[2][:], ACT.Copy).then_inc(g_vh, 1)
                if s.live(1):
                    act.wait_ge(g_qtp, n)
                    if s.had(2):
                        act.wait_ge(g_sp, n - 1)
                    nc.scalar.activation(q_t[:], bank[4][:], ACT.Copy).then_inc(g_qt, 1)
                if s.live(3):
                    act.wait_ge(g_pvp, n - 2)
                    if s.had(4):
                        act.wait_ge(g_op, n - 3)
                    nc.scalar.activation(o2_hi[:], bank[6][:], ACT.Copy).then_inc(g_oh, 1)
                if s.new() and s.kv == 1:
                    act.wait_ge(g_ktp, s.seq + 1)
                    if s.had(8):
                        act.wait_ge(g_sp, 4 * (s.seq - 1))
                    nc.scalar.activation(k_t[:, s.b % 2], bank[1][:], ACT.Copy).then_inc(g_kt, 1)

            attention2(act, step)

            act.wait_ge(m_sel, 5)
            act.wait_ge(d_rw, 16)
            nc.scalar.activation(sel[:], sel_f[:], ACT.Copy).then_inc(w_hi4, 1)
            nc.scalar.activation(rw_hi[:], rw_raw[:], ACT.Copy).then_inc(w_hi4, 1)
            for d, hi, raw in ((d_wg, wg_hi, wg_raw), (d_wu, wu_hi, wu_raw), (d_wd, wd_hi, wd_raw)):
                act.wait_ge(d, 16)
                nc.scalar.activation(hi[:], raw[:], ACT.Copy).then_inc(w_hi4, 1)

            def experts(g, first):
                for i in range(NR):
                    n, back = g * NR + i, 1 if i == 0 else 2
                    if i == 0:
                        act.wait_ge(n_ev, 2 * (3 * NG + g + 1))
                        if first:
                            act.wait_ge(g_qp, NG * 4 * GB)
                        else:
                            act.wait_ge(m_up, n)
                        cur(3 * NG + g, g)
                        act.wait_ge(t_v, g * RV + 2)
                        nc.scalar.activation(probs[:], probs[:], ACT.Exp).then_inc(t_ex, 1)
                    act.wait_ge(m_gp, n + 1)
                    if i >= 2 or not first:
                        act.wait_ge(m_em, n - back + 1)
                    nc.scalar.activation(sg[:, i % 2], bank[i % 2][:], ACT.Silu).then_inc(m_sg, 1)
                    if i == 0:
                        act.wait_ge(t_ctp, g + 1)
                        if not first:
                            act.wait_ge(m_cp, n)
                        nc.scalar.activation(ct_hi[:], bank[5][0:E, :], ACT.Copy).then_inc(t_h, 1)
                    act.wait_ge(m_em, n + 1)
                    if i >= 2 or not first:
                        act.wait_ge(m_dp, n - back + 1)
                    nc.scalar.activation(e_hi[:, i % 2], em[:, i % 2], ACT.Copy).then_inc(m_h, 1)

            experts(0, True)
            with act.Fori(1, NG) as g:
                experts(g, False)

        @block.vector
        def _(dve):
            def norm_stats(g):
                for b in range(GB):
                    last = nc.vector.bn_stats(bn[:, b], xres[:, bass.ds(g * GB + b, 1), :].rearrange("p a d -> p (a d)"))
                last.then_inc(n_bn, 1)

            def norm_sums():
                for b in range(GB):
                    last = nc.vector.bn_aggr(mv[:, b], bn[:, b])
                last.then_inc(n_st, 1)

            def norm_apply(n, g):
                dve.wait_ge(n_rs, n + 1)
                for b in range(GB):
                    last = nc.vector.tensor_scalar(xn[:, b], xres[:, bass.ds(g * GB + b, 1), :].rearrange("p a d -> p (a d)"),
                                                   mv[:, b, 0:1], rstd[:, b:b + 1], ALU.subtract, ALU.mult)
                last.then_inc(n_xn, 1)

            def norm_apply_rms(n, g):
                dve.wait_ge(n_rs, n + 1)
                for b in range(GB):
                    last = nc.vector.tensor_scalar(xn[:, b], xres[:, bass.ds(g * GB + b, 1), :].rearrange("p a d -> p (a d)"),
                                                   rstd[:, b:b + 1], None, ALU.mult)
                last.then_inc(n_xn, 1)

            def norm_weight(n, g, k, kind, src):
                dve.wait_ge(n_tp, 2 * n + k + 1)
                nc.vector.tensor_scalar(span(act_t, k, g), src[:], norm_w[:, kind, k:k + 1], None,
                                        ALU.mult).then_inc(n_ev, 1)

            def norm_ada(n, g, k, kind, src):
                dve.wait_ge(n_tp, 2 * n + k + 1)
                for b in range(GB):
                    last = nc.vector.tensor_scalar(span(act_t, k, g, b, 1), src[:, b * T:(b + 1) * T],
                                                   ada_t[:, 2 * kind + 1, k, bass.ds(g * GB + b, 1)],
                                                   ada_t[:, 2 * kind, k, bass.ds(g * GB + b, 1)], ALU.mult, ALU.add)
                last.then_inc(n_ev, 1)

            def cur_rest(c, g):
                dve.wait_ge(c_hi, c + 1)
                nc.vector.tensor_tensor(cur_lo[:], act_t[:, :, bass.ds(g * GT, GT)], cur_hi[:].bitcast(F32),
                                        ALU.subtract).then_inc(c_lo, 1)

            def residual(r, g, banks, phase_r):
                dve.wait_ge(d_gate, 16 * (r + 1))
                for j in range(2):
                    ob = bank[banks[j]][:].rearrange("p (b d) -> p b d", b=2)
                    nc.vector.tensor_tensor(ob, ob, obias[:].unsqueeze(1).broadcast_to([P, 2, D]),
                                            ALU.add).then_inc(r_add, 1)
                for j in range(2):
                    ob = bank[banks[j]][:].rearrange("p (b d) -> p b d", b=2)
                    dve.wait_ge(r_add, 2 * r + j + 1)
                    nc.vector.tensor_tensor(gate[:, 2 * j:2 * j + 2], ob, gate[:, 2 * j:2 * j + 2],
                                            ALU.mult).then_inc(r_mul, 1)
                for j in range(2):
                    xs = xres[:, bass.ds(g * GB + 2 * j, 2), :]
                    dve.wait_ge(r_mul, 2 * r + j + 1)
                    nc.vector.tensor_tensor(xs, xs, gate[:, 2 * j:2 * j + 2], ALU.add).then_inc(r_x, 1)

            for g in range(NG):
                dve.wait_ge(d_x[g], 16)
                if g >= 1:
                    dve.wait_ge(n_xn, g)
                norm_stats(g)
                dve.wait_ge(n_bn, g + 1)
                norm_sums()
                if g >= 1:
                    dve.wait_ge(n_tp, 2 * g)
                norm_apply(g, g)
                if g == 0:
                    dve.wait_ge(ada_p, 1)
                    dve.wait_ge(d_small, 7 * 16)
                    for i, c in enumerate((0, 1, 3, 4)):
                        for k in range(KD):
                            nc.vector.tensor_scalar(ada_t[:, i, k], bank[7][:, (i * KD + k) * B:(i * KD + k + 1) * B],
                                                    ada_bt[:, c * KD + k:c * KD + k + 1], float(i % 2),
                                                    ALU.add, ALU.add).then_inc(ada_s, 1)
                    nc.vector.tensor_tensor(gates[:], bank[6][0:B, :].rearrange("b (c d) -> b c d", c=2), ada_bg[:],
                                            ALU.add).then_inc(ada_s, 1)
                    dve.wait_ge(ada_s, 9)
                for k in range(KD):
                    norm_ada(g, g, k, 0, bank[k])
            for c in range(4):
                hs, cs = slice(4 * c, 4 * c + 4), slice(512 * c, 512 * c + 512)
                for i, (lo, raw, hi) in enumerate(((wqk_lo[:, hs], wqk_raw[:, hs], wqk_hi[:, hs]),
                                                   (wv_lo[:, :, cs], wv_raw[:, :, cs], wv_hi[:, :, cs]),
                                                   (wo_lo[:, hs], wo_raw[:, hs], wo_hi[:, hs]))):
                    if i == 0:
                        lo, raw, hi = (x.rearrange("p h c k d -> p (h c k d)") for x in (lo, raw, hi))
                    dve.wait_ge(w_hi1, 3 * c + i + 1)
                    nc.vector.tensor_tensor(lo, raw, hi.bitcast(F32), ALU.subtract).then_inc(w_lo1, 1)

            def row_max(n, h):
                dve.wait_ge(a_sp, n + 1)
                nc.vector.tensor_reduce(nmax[:, h % 2], bank[3][:].rearrange("p (b s) -> p b s", b=GB), X, ALU.max,
                                        negate=True).then_inc(a_mx, 1)

            def p_t(n):
                dve.wait_ge(a_tp, n + 1)
                if not isinstance(n, int) or n >= 1:
                    dve.wait_ge(a_pvp, n)
                nc.vector.tensor_copy(pt1[:], bank[4][:]).then_inc(a_pt, 1)

            def row_inverse(n, h):
                dve.wait_ge(a_ex, n + 1)
                nc.vector.reciprocal(rinv[:, h % 2], rsum[:, h % 2]).then_inc(a_ri, 1)

            def o_lo(n, h):
                dve.wait_ge(a_oh, n + 1)
                nc.vector.scalar_tensor_tensor(out=o1_lo[:, h % 2], in0=bank[5][:], scalar=bqkv[:, 2, h:h + 1],
                                               in1=o1_hi[:, h % 2].bitcast(F32), op0=ALU.add,
                                               op1=ALU.subtract).then_inc(a_ol, 1)

            def attention1(g, first):
                for h in range(H):
                    n = g * H + h
                    if h == 0:
                        cur_rest(g, g)
                    if h == 3 and not first:
                        dve.wait_ge(r_x, 2 * g)
                    if h >= 1 or not first:
                        row_max(n - 1, (h - 1) % 2)
                    if h == 2 and not first:
                        dve.wait_ge(a_op, n - 2)
                        residual(g - 1, g - 1, (6, 7), 0)
                    if h == 3 and not first:
                        norm_stats(g - 1)
                        dve.wait_ge(n_bn, NG + g)
                    if h == 4 and not first:
                        norm_apply(NG + g - 1, g - 1)
                    if h >= 2 or not first:
                        p_t(n - 2)
                    if h == 3 and not first:
                        norm_sums()
                    if h in (5, 6) and not first:
                        norm_ada(NG + g - 1, g - 1, h - 5, 1, bank[4])
                    if h >= 1 or not first:
                        row_inverse(n - 1, (h - 1) % 2)
                    dve.wait_ge(a_kp, n + 1)
                    if h >= 2 or not first:
                        dve.wait_ge(a_sp, n - 1)
                    nc.vector.tensor_scalar(k1[:, h % 2], bank[1][:], bqkv[:, 1, h:h + 1], None, ALU.add).then_inc(a_k, 1)
                    if h >= 2 or not first:
                        o_lo(n - 2, (h - 2) % H)

            attention1(0, True)
            with dve.Fori(1, NG) as g:
                attention1(g, False)
            n = NG * H
            row_max(n - 1, 1)
            p_t(n - 2)
            row_inverse(n - 1, 1)
            o_lo(n - 2, H - 2)
            p_t(n - 1)
            o_lo(n - 1, H - 1)
            dve.wait_ge(w_hi2, 1)
            nc.vector.tensor_tensor(w1_lo[:], w1_raw[:], w1_hi[:].bitcast(F32), ALU.subtract).then_inc(w_lo2, 1)
            dve.wait_ge(w_hi2, 2)
            nc.vector.tensor_tensor(w2_lo[:], w2_raw[:], w2_hi[:].bitcast(F32), ALU.subtract).then_inc(w_lo2, 1)
            dve.wait_ge(a_op, n)
            residual(NG - 1, NG - 1, (6, 7), 0)
            dve.wait_ge(r_x, 2 * NG)
            norm_stats(NG - 1)
            dve.wait_ge(n_bn, 2 * NG)
            norm_sums()
            norm_apply(2 * NG - 1, NG - 1)
            for k in range(KD):
                norm_ada(2 * NG - 1, NG - 1, k, 1, bank[4])

            def split3(c):
                for i, (lo, hi, raw, at, w) in enumerate(((wkv_lo, wkv_hi, wkv_raw, c * 256, 256),
                                                          (wq_lo, wq_hi, wq_raw, c * 512, 512))):
                    dve.wait_ge(w_hi3, 3 * c + i + 1)
                    nc.vector.tensor_tensor(lo[:, :, bass.ds(at, w)], raw[:, :, bass.ds(at, w)],
                                            hi[:, :, bass.ds(at, w)].bitcast(F32), ALU.subtract).then_inc(w_lo3, 1)
                dve.wait_ge(w_hi3, 3 * c + 3)
                nc.vector.tensor_tensor(wo2_lo[:, bass.ds(c * 4, 4)], wo2_raw[:, bass.ds(c * 4, 4)],
                                        wo2_hi[:, bass.ds(c * 4, 4)].bitcast(F32), ALU.subtract).then_inc(w_lo3, 1)

            def ffn1(g, first):
                for f in range(NF):
                    m = g * NF + f
                    if f == 4 and not first:
                        split3(g - 1)
                    if f == 0:
                        cur_rest(NG + g, g)
                        if first:
                            dve.wait_ge(d_b2, 16)
                    if f == 2 and not first:
                        dve.wait_ge(f_dp, m - 2)
                        residual(NG + g - 1, g - 1, (6, 7), 1)
                    if f == 3 and not first:
                        dve.wait_ge(r_x, 2 * (NG + g))
                    if f == 4 and not first:
                        dve.wait_ge(n_bn, 2 * NG + g)
                    if f == 5 and not first:
                        norm_apply_rms(2 * NG + g - 1, g - 1)
                    if f == 7 and not first:
                        for k in range(KD):
                            norm_weight(2 * NG + g - 1, g - 1, k, 0, bank[2 + k])
                    dve.wait_ge(f_h, m + 1)
                    if f >= 2 or not first:
                        dve.wait_ge(f_dp, m - 1)
                    nc.vector.tensor_tensor(h_lo[:, f % 2], hf[:, f % 2], h_hi[:, f % 2].bitcast(F32),
                                            ALU.subtract).then_inc(f_l, 1)
                    if f == 3 and not first:
                        norm_stats(g - 1)
                    if f == 4 and not first:
                        norm_sums()

            dve.wait_ge(d_rope, 32)
            for i in range(4):
                nc.vector.scalar_tensor_tensor(out=rope[:, i], in0=rope[:, i], scalar=SCALE if i < 2 else 1.0,
                                               in1=cos_sin[:, i % 2], op0=ALU.mult, op1=ALU.mult).then_inc(g_tab, 1)
            dve.wait_ge(g_mask, 2)
            nc.vector.tensor_copy(mask[:].rearrange("p (j s) -> p j s", j=REP),
                                  mask_f[:].unsqueeze(1).broadcast_to([P, REP, T])).then_inc(g_tab, 1)
            nc.vector.tensor_copy(ident_b[:], ident[:]).then_inc(g_tab, 1)
            ffn1(0, True)
            with dve.Fori(1, NG) as g:
                ffn1(g, False)
            split3(NG - 1)
            dve.wait_ge(f_dp, NG * NF)
            residual(2 * NG - 1, NG - 1, (6, 7), 1)
            dve.wait_ge(r_x, 4 * NG)
            norm_stats(NG - 1)
            dve.wait_ge(n_bn, 3 * NG)
            norm_sums()
            norm_apply_rms(3 * NG - 1, NG - 1)
            for k in range(KD):
                norm_weight(3 * NG - 1, NG - 1, k, 0, bank[2 + k])
            dve.wait_ge(g_tab, 6)

            def rotate(out_cos, out_sin, src, table, cos_free, sin_free, done):
                heads = src.rearrange("p (h d) -> p h d", d=DH)
                for sem_, value in cos_free:
                    dve.wait_ge(sem_, value)
                nc.vector.tensor_tensor(out_cos.rearrange("p (h d) -> p h d", d=DH), heads,
                                        rope[:, table].unsqueeze(1).broadcast_to([P, 4, DH]), ALU.mult)
                for sem_, value in sin_free:
                    dve.wait_ge(sem_, value)
                nc.vector.tensor_tensor(out_sin.rearrange("p (h c d) -> p h c d", c=2, d=DH // 2),
                                        src.rearrange("p (h c d) -> p h c d", c=2, d=DH // 2)[:, :, ::-1, :],
                                        rope[:, table + 1].rearrange("p (c d) -> p c d", c=2).unsqueeze(1)
                                        .broadcast_to([P, 4, 2, DH // 2]), ALU.mult).then_inc(done, 1)

            def step(s):
                n, new_seq, prev = s.n, s.new() and s.kv == 0, 3 * NG + s.g - 1
                if s.u == 0:
                    cur_rest(2 * NG + s.g, s.g)
                if s.kv == 0 and s.had(8):
                    dve.wait_ge(g_op, 4 * (s.seq - 1))
                    xs = xres[:, bass.ds(s.seq - 2, 1), :].rearrange("p a d -> p (a d)")
                    nc.vector.tensor_tensor(xs, xs, bank[7][:, 0:D], ALU.add).then_inc(g_x, 1)
                if s.u == 5 and not s.first:
                    dve.wait_ge(g_x, GB * s.g)
                if s.live(2):
                    dve.wait_ge(g_sp, n - 1)
                    nc.vector.tensor_reduce(nmax[:, s.u % 2], bank[3][:].rearrange("p (j s) -> p j s", j=REP), X,
                                            ALU.max, negate=True).then_inc(g_mx, 1)
                    dve.wait_ge(g_rq, n - 1)
                    dve.wait_ge(g_mx, n - 1)
                    nc.vector.tensor_tensor(nb[:, s.u % 2], nmax[:, s.u % 2], rq[:, (s.u - 2) % 4],
                                            ALU.mult).then_inc(g_nb, 1)
                if s.u == 5 and not s.first:
                    norm_stats(s.g - 1)
                    dve.wait_ge(n_bn, prev + 1)
                if new_seq:
                    free = [(g_ktp, s.seq)] if s.had(4) else []
                    rotate(kr[:], kb[:], bank[1][:], 2, [(g_kp, s.seq + 1)] + free, free, g_kb)
                if s.new():
                    rotate(qr[:, s.u % 2], rb[:], bank[0][:], 0,
                           [(g_qp, n + 1)] + ([(g_qtp, n - 1)] if s.had(2) else []),
                           [(g_qr, n)] if s.had(1) else [], g_qb)
                if s.u == 5 and not s.first:
                    norm_sums()
                if s.u == 8 and not s.first:
                    norm_apply_rms(prev, s.g - 1)
                if new_seq:
                    dve.wait_ge(g_ksq, s.seq + 1)
                    nc.vector.tensor_reduce(k_ms[:], ksq[:].rearrange("p (h d) -> p h d", d=DH), X,
                                            ALU.add).then_inc(g_ks, 1)
                if s.new() and s.kv == 1:
                    dve.wait_ge(g_rk, s.seq + 1)
                    dve.wait_ge(g_ka, s.seq + 1)
                    kh = kr[:].rearrange("p (h d) -> p h d", d=DH)
                    nc.vector.tensor_tensor(kh, kh, rk[:].unsqueeze(2).broadcast_to([P, HKV, DH]),
                                            ALU.mult).then_inc(g_kr, 1)
                if s.live(3):
                    dve.wait_ge(g_ph, n - 2)
                    nc.vector.tensor_tensor(pt_lo[:], bank[5][:], pt_hi[:].bitcast(F32), ALU.subtract).then_inc(g_pl, 1)
                if s.new():
                    dve.wait_ge(g_sq, n + 1)
                    if s.had(2):
                        dve.wait_ge(g_rq, n - 1)
                    nc.vector.tensor_reduce(q_ms[:, s.u % 2], sq[:].rearrange("p (h d) -> p h d", d=DH), X,
                                            ALU.add).then_inc(g_ss, 1)
                if s.live(2):
                    dve.wait_ge(g_ex, n - 1)
                    nc.vector.reciprocal(rinv[:, s.u % 2], rsum[:, s.u % 2]).then_inc(g_ri, 1)
                if new_seq:
                    dve.wait_ge(g_vh, s.seq + 1)
                    nc.vector.tensor_tensor(v_lo[:, s.b % 2], bank[2][:], v_hi[:, s.b % 2].bitcast(F32),
                                            ALU.subtract).then_inc(g_vl, 1)
                if s.u == 10 and not s.first:
                    for k in range(KD):
                        norm_weight(prev, s.g - 1, k, 1, bank[1 + k])
                if s.live(3):
                    dve.wait_ge(g_oh, n - 2)
                    nc.vector.tensor_tensor(o2_lo[:], bank[6][:], o2_hi[:].bitcast(F32), ALU.subtract).then_inc(g_ol, 1)

            attention2(dve, step)
            dve.wait_ge(g_x, B)
            norm_stats(NG - 1)
            dve.wait_ge(n_bn, 4 * NG)
            norm_sums()
            norm_apply_rms(4 * NG - 1, NG - 1)
            for k in range(KD):
                norm_weight(4 * NG - 1, NG - 1, k, 1, bank[1 + k])

            for i, (lo, raw, hi) in enumerate(((rw_lo, rw_raw, rw_hi), (wg_lo, wg_raw, wg_hi),
                                               (wu_lo, wu_raw, wu_hi), (wd_lo, wd_raw, wd_hi))):
                dve.wait_ge(w_hi4, i + 2)
                nc.vector.tensor_tensor(lo[:], raw[:], hi[:].bitcast(F32), ALU.subtract).then_inc(w_lo4, 1)

            def routing(g, first):
                done = [0]

                def after():
                    dve.wait_ge(t_v, g * RV + done[0])

                def inc(i):
                    done[0] += 1
                    i.then_inc(t_v, 1)

                lg = bank[5][:, 0:GB * E].rearrange("p (b e) -> p b e", b=GB)
                wide = [P, GB, E]
                dve.wait_ge(t_lp, g + 1)
                inc(nc.vector.tensor_reduce(r4[:, 0], lg, X, ALU.max))
                after()
                inc(nc.vector.tensor_tensor(probs[:], lg, r4[:, 0].unsqueeze(2).broadcast_to(wide), ALU.subtract))
                dve.wait_ge(t_ex, g + 1)
                inc(nc.vector.tensor_reduce(r4[:, 1], probs[:], X, ALU.add))
                after()
                inc(nc.vector.reciprocal(r4[:, 2], r4[:, 1]))
                after()
                inc(nc.vector.tensor_tensor(probs[:], probs[:], r4[:, 2].unsqueeze(2).broadcast_to(wide), ALU.mult))
                after()
                pj = probs[:].unsqueeze(2).broadcast_to([P, GB, E, E])
                pe_ = probs[:].unsqueeze(3).broadcast_to([P, GB, E, E])
                nc.vector.tensor_tensor(gt[:], pj, pe_, ALU.is_gt)
                inc(nc.vector.tensor_tensor(eq[:], pj, pe_, ALU.is_equal))
                after()
                inc(nc.vector.tensor_tensor(eq[:].rearrange("p b e j -> p b (e j)"), eq[:].rearrange("p b e j -> p b (e j)"),
                                            before[:].rearrange("p e j -> p (e j)").unsqueeze(1)
                                            .broadcast_to([P, GB, E * E]), ALU.mult))
                after()
                inc(nc.vector.tensor_tensor(gt[:], gt[:], eq[:], ALU.add))
                after()
                inc(nc.vector.tensor_reduce(pick[:], gt[:], X, ALU.add))
                after()
                inc(nc.vector.scalar_tensor_tensor(out=comb[:], in0=pick[:], scalar=2.0, in1=probs[:],
                                                   op0=ALU.is_lt, op1=ALU.mult))
                after()
                inc(nc.vector.tensor_reduce(r4[:, 3], comb[:], X, ALU.add))
                after()
                nc.vector.tensor_scalar(r4[:, 0], r4[:, 3], 1e-9, None, ALU.add).then_inc(t_v, 1)
                done[0] += 1
                after()
                nc.vector.reciprocal(r4[:, 1], r4[:, 0]).then_inc(t_v, 1)
                done[0] += 1
                after()
                assert done[0] == RV
                nc.vector.tensor_tensor(comb[:], comb[:], r4[:, 1].unsqueeze(2).broadcast_to(wide),
                                        ALU.mult).then_inc(t_c, 1)

            def experts(g, first):
                for i in range(NR):
                    n, back = g * NR + i, 1 if i == 0 else 2
                    if i == 0:
                        cur_rest(3 * NG + g, g)
                        routing(g, first)
                    dve.wait_ge(m_sg, n + 1)
                    dve.wait_ge(m_up, n + 1)
                    nc.vector.tensor_tensor(sg[:, i % 2], sg[:, i % 2], bank[2 + i % 2][:], ALU.mult).then_inc(m_su, 1)
                    if i == 0:
                        dve.wait_ge(t_h, g + 1)
                        nc.vector.tensor_tensor(ct_lo[:], bank[5][0:E, :], ct_hi[:].bitcast(F32),
                                                ALU.subtract).then_inc(t_l, 1)
                    if i == 2 and not first:
                        result(g - 1)
                    dve.wait_ge(m_cp, n + 1)
                    dve.wait_ge(m_su, n + 1)
                    if i >= 2 or not first:
                        dve.wait_ge(m_l, n - back + 1)
                    nc.vector.tensor_tensor(em[:, i % 2], sg[:, i % 2], bank[4][:], ALU.mult).then_inc(m_em, 1)
                    dve.wait_ge(m_h, n + 1)
                    nc.vector.tensor_tensor(e_lo[:, i % 2], em[:, i % 2], e_hi[:, i % 2].bitcast(F32),
                                            ALU.subtract).then_inc(m_l, 1)

            def result(g):
                dve.wait_ge(m_dp, NR * (g + 1))
                if not isinstance(g, int) or g >= 1:
                    dve.wait_ge(d_out, 16 * g)
                for j in range(2):
                    nc.vector.tensor_tensor(y[:, 2 * j:2 * j + 2], bank[6 + j][:].rearrange("p (b d) -> p b d", b=2),
                                            xres[:, bass.ds(g * GB + 2 * j, 2), :], ALU.add).then_inc(m_y, 1)
                dve.wait_ge(d_xin, 16 * (g + 1))
                dve.wait_ge(m_y, 4 * g + 2)
                for j in range(2):
                    nc.vector.tensor_tensor(y[:, 2 * j:2 * j + 2], y[:, 2 * j:2 * j + 2], x0[:, 2 * j:2 * j + 2],
                                            ALU.add).then_inc(m_y, 1)

            experts(0, True)
            with dve.Fori(1, NG) as g:
                experts(g, False)
            result(NG - 1)

        @block.tensor
        def _(pe):
            def norm_transposes(n, k, dst):
                for b in range(GB):
                    last = pe.transpose(dst[:, b * T:(b + 1) * T], xn[:, b, k * P:(k + 1) * P], ident[:])
                last.then_inc(n_tp, 1)

            pe.wait_ge(d_small, 7 * 16)
            pe.wait_ge(d_adaw, 16)
            for i, c in enumerate((0, 1, 3, 4)):
                for k in range(KD):
                    for j in range(KD):
                        pe.matmul(bank[7][:, (i * KD + k) * B:(i * KD + k + 1) * B],
                                  ada_w[:, j, c * D + k * P:c * D + (k + 1) * P], cond_t[:, j], start=(j == 0), stop=(j == KD - 1))
            for i, c in enumerate((2, 5)):
                for j in range(KD):
                    last = pe.matmul(bank[6][0:B, i * D:(i + 1) * D], cond_t[:, j], ada_w[:, j, c * D:(c + 1) * D],
                                     start=(j == 0), stop=(j == KD - 1))
            last.then_inc(ada_p, 1)
            pe.wait_ge(consts, 4)
            for g in range(NG):
                pe.wait_ge(n_xn, g + 1)
                for k in range(KD):
                    if g >= 1:
                        pe.wait_ge(n_ev, 2 * (g - 1) + k + 1)
                    norm_transposes(g, k, bank[k])

            def project(dst, h, c):
                for k in range(KD):
                    for i, (l, r) in enumerate(split_products(wqk_hi[:, h, c, k], wqk_lo[:, h, c, k],
                                                              cur_hi[:, k], cur_lo[:, k])):
                        last = pe.matmul(dst, l, r, start=(k == 0 and i == 0), stop=(k == KD - 1 and i == 2))
                return last

            def scores(n, h):
                pe.wait_ge(a_k, n + 1)
                pe.wait_ge(a_q, n + 1)
                if not isinstance(n, int) or n >= 1:
                    pe.wait_ge(a_ex, n)
                for b in range(GB):
                    bs = slice(b * T, (b + 1) * T)
                    last = pe.matmul(bank[3][:, bs], q1[:, h % 2, bs], k1[:, h % 2, bs], start=True, stop=True)
                last.then_inc(a_sp, 1)

            def p_transposes(n, h):
                pe.wait_ge(a_pn, n + 1)
                if not isinstance(n, int) or n >= 1:
                    pe.wait_ge(a_pt, n)
                for b in range(GB):
                    last = pe.transpose(bank[4][:, b * T:(b + 1) * T], p1[:, h % 2, b], ident[:])
                last.then_inc(a_tp, 1)

            def values_product(n, h):
                pe.wait_ge(a_pt, n + 1)
                pe.wait_ge(a_v, n - h % 2 + 2)
                if not isinstance(n, int) or n >= 1:
                    pe.wait_ge(a_ol, n)
                for b in range(GB):
                    bs = slice(b * T, (b + 1) * T)
                    last = pe.matmul(bank[5][:, bs], v1[:, h // 2 % 2, b, h % 2 * DH:h % 2 * DH + DH], pt1[:, bs],
                                     start=True, stop=True)
                last.then_inc(a_pvp, 1)

            def down(banks, lhs_hi, lhs_lo, rhs_hi, rhs_lo, first, last_one):
                for b in range(GB):
                    bs = slice(b * T, (b + 1) * T)
                    for i, (l, r) in enumerate(split_products(lhs_hi[:, bs], lhs_lo[:, bs], rhs_hi, rhs_lo)):
                        last = pe.matmul(bank[banks[b // 2]][:, b % 2 * D:b % 2 * D + D], l, r,
                                         start=(first and b % 2 == 0 and i == 0), stop=(last_one and i == 2),
                                         skip_group_check=True)
                return last

            def out_product(n, h):
                pe.wait_ge(a_ol, n + 1)
                down((6, 7), o1_hi[:, h % 2], o1_lo[:, h % 2], wo_hi[:, h], wo_lo[:, h],
                     h == 0, h == H - 1).then_inc(a_op, 1)

            def attention1(g, first):
                for h in range(H):
                    n = g * H + h
                    if h == 0:
                        pe.wait_ge(c_lo, g + 1)
                    if first and h % 4 == 0:
                        pe.wait_ge(w_lo1, 3 * (h // 4) + 1)
                    if h >= 1 or not first:
                        pe.wait_ge(a_q, n)
                    project(bank[0][:], h, 0).then_inc(a_qp, 1)
                    if h in (6, 7) and not first:
                        pe.wait_ge(n_ev, 2 * (NG + g - 1) + h - 5)
                    if h >= 2 or not first:
                        p_transposes(n - 2, h % 2)
                    if h in (5, 6) and not first:
                        if h == 5:
                            pe.wait_ge(n_xn, NG + g)
                        pe.wait_ge(a_pt, n - 1)
                        norm_transposes(NG + g - 1, h - 5, bank[4])
                    if h >= 1 or not first:
                        pe.wait_ge(a_k, n)
                    project(bank[1][:], h, 1).then_inc(a_kp, 1)
                    if h >= 2 or not first:
                        values_product(n - 2, (h - 2) % H)
                    if first and h % 4 == 0:
                        pe.wait_ge(w_lo1, 3 * (h // 4) + 2)
                    if h >= 1 or not first:
                        pe.wait_ge(a_v, n)
                    ps = slice(h // 2 * 2 * DH, (h // 2 + 1) * 2 * DH)
                    for j in range(2):
                        bs = slice((h % 2 * 2 + j) * T, (h % 2 * 2 + j + 1) * T)
                        for k in range(KD):
                            for i, (l, r) in enumerate(split_products(cur_hi[:, k, bs], cur_lo[:, k, bs],
                                                                      wv_hi[:, k, ps], wv_lo[:, k, ps])):
                                last = pe.matmul(bank[2][:, j * 2 * DH:(j + 1) * 2 * DH], l, r,
                                                 start=(k == 0 and i == 0), stop=(k == KD - 1 and i == 2))
                    last.then_inc(a_vp, 1)
                    if h >= 2 or not first:
                        if first and h % 4 == 2:
                            pe.wait_ge(w_lo1, 3 * (h // 4) + 3)
                        if h == 2 and not first:
                            pe.wait_ge(r_mul, 2 * g)
                        out_product(n - 2, (h - 2) % H)
                    scores(n, h)

            attention1(0, True)
            with pe.Fori(1, NG) as g:
                attention1(g, False)
            n = NG * H
            for h in (H - 2, H - 1):
                p_transposes(n - H + h, h)
                values_product(n - H + h, h)
                out_product(n - H + h, h)
            pe.wait_ge(n_xn, 2 * NG)
            pe.wait_ge(a_pt, n)
            for k in range(KD):
                norm_transposes(2 * NG - 1, k, bank[4])
                pe.wait_ge(n_ev, 2 * (2 * NG - 1) + k + 1)

            def ffn_down(m, f):
                pe.wait_ge(f_l, m + 1)
                down((6, 7), h_hi[:, f % 2], h_lo[:, f % 2], w2_hi[:, f], w2_lo[:, f], f == 0, f == NF - 1).then_inc(f_dp, 1)

            def ffn1(g, first):
                for f in range(NF):
                    m = g * NF + f
                    if f == 0:
                        pe.wait_ge(c_lo, NG + g + 1)
                        if first:
                            pe.wait_ge(w_lo2, 2)
                    if f >= 2 or not first:
                        pe.wait_ge(f_g, m - 1)
                    for k in range(KD):
                        for i, (l, r) in enumerate(split_products(w1_hi[:, f, k], w1_lo[:, f, k], cur_hi[:, k], cur_lo[:, k])):
                            last = pe.matmul(bank[f % 2][:], l, r, start=(k == 0 and i == 0), stop=(k == KD - 1 and i == 2))
                    last.then_inc(f_up, 1)
                    if f == 2:
                        pe.wait_ge(r_mul, 2 * (NG + g))
                    if f >= 2 or not first:
                        ffn_down(m - 2, (f - 2) % NF)
                    if f == 6 and not first:
                        pe.wait_ge(n_xn, 2 * NG + g)
                        pe.wait_ge(n_ev, 2 * (2 * NG + g - 1))
                        for k in range(KD):
                            norm_transposes(2 * NG + g - 1, k, bank[2 + k])

            ffn1(0, True)
            with pe.Fori(1, NG) as g:
                ffn1(g, False)
            ffn_down(NG * NF - 2, NF - 2)
            ffn_down(NG * NF - 1, NF - 1)
            pe.wait_ge(n_xn, 3 * NG)
            pe.wait_ge(n_ev, 2 * (3 * NG - 1))
            for k in range(KD):
                norm_transposes(3 * NG - 1, k, bank[2 + k])

            def token_product(dst, seq, w_hi, w_lo, cols):
                bs = slice(seq * T, (seq + 1) * T)
                for k in range(KD):
                    for i, (l, r) in enumerate(split_products(cur_hi[:, k, bs], cur_lo[:, k, bs],
                                                              w_hi[:, k, cols], w_lo[:, k, cols])):
                        last = pe.matmul(dst, l, r, start=(k == 0 and i == 0), stop=(k == KD - 1 and i == 2))
                return last

            def step(s):
                n, new_seq = s.n, s.new() and s.kv == 0
                if s.u == 0:
                    pe.wait_ge(c_lo, 2 * NG + s.g + 1)
                    if s.first:
                        pe.wait_ge(w_lo3, 12)
                        pe.wait_ge(r_mul, 2 * 2 * NG)
                        pe.wait_ge(n_ev, 2 * 3 * NG)
                if new_seq:
                    if s.had(4):
                        pe.wait_ge(g_kt, s.seq)
                    if s.u == 12 and not s.first:
                        pe.wait_ge(n_ev, 2 * (3 * NG + s.g))
                    token_product(bank[1][:], s.b, wkv_hi, wkv_lo, slice(0, HKV * DH)).then_inc(g_kp, 1)
                if s.new():
                    if s.had(1):
                        pe.wait_ge(g_qb, n)
                        pe.wait_ge(g_sq, n)
                    token_product(bank[0][:], s.b, wq_hi, wq_lo,
                                  slice(s.kv * REP * DH, (s.kv + 1) * REP * DH)).then_inc(g_qp, 1)
                if s.live(3):
                    pe.wait_ge(g_pn, n - 2)
                    if s.had(4):
                        pe.wait_ge(g_pl, n - 3)
                    for j in range(REP):
                        last = pe.transpose(bank[5][:, j * T:(j + 1) * T], p2[:, (s.u - 3) % 2, j], ident[:])
                    last.then_inc(g_tp, 1)
                if new_seq:
                    if s.had(4):
                        pe.wait_ge(g_vl, s.seq)
                    token_product(bank[2][:], s.b, wkv_hi, wkv_lo, slice(HKV * DH, 2 * HKV * DH)).then_inc(g_vp, 1)
                if s.live(1):
                    pe.wait_ge(g_qr, n)
                    if s.had(2):
                        pe.wait_ge(g_qt, n - 1)
                    for j in range(REP):
                        last = pe.transpose(bank[4][:, j * T:(j + 1) * T],
                                            qr[:, (s.u - 1) % 2, j * DH:(j + 1) * DH], ident[:])
                    last.then_inc(g_qtp, 1)
                if s.live(4):
                    kv = (s.u - 4) % HKV
                    pe.wait_ge(g_ol, n - 3)
                    if kv == 0 and s.had(8):
                        pe.wait_ge(g_x, s.seq - 1)
                    for j in range(REP):
                        js = slice(j * T, (j + 1) * T)
                        for i, (l, r) in enumerate(split_products(o2_hi[:, js], o2_lo[:, js],
                                                                  wo2_hi[:, kv * REP + j], wo2_lo[:, kv * REP + j])):
                            last = pe.matmul(bank[7][:, 0:D], l, r, start=(kv == 0 and j == 0 and i == 0),
                                             stop=(kv == HKV - 1 and j == REP - 1 and i == 2))
                    last.then_inc(g_op, 1)
                if s.live(3):
                    kv, slot = (s.u - 3) % HKV, (s.u - 3) // HKV % 2
                    pe.wait_ge(g_pl, n - 2)
                    pe.wait_ge(g_vl, s.g * GB + (s.u - 3) // HKV + 1)
                    if s.had(4):
                        pe.wait_ge(g_ol, n - 3)
                    ks = slice(kv * DH, (kv + 1) * DH)
                    for i, (l, r) in enumerate(split_products(v_hi[:, slot, ks], v_lo[:, slot, ks], pt_hi[:], pt_lo[:])):
                        last = pe.matmul(bank[6][:], l, r, start=(i == 0), stop=(i == 2))
                    last.then_inc(g_pvp, 1)
                if s.new() and s.kv == 1:
                    pe.wait_ge(g_kr, s.seq + 1)
                    for j in range(HKV):
                        last = pe.transpose(bank[1][:, j * T:(j + 1) * T], kr[:, j * DH:(j + 1) * DH], ident[:])
                    last.then_inc(g_ktp, 1)
                if s.u == 10 and not s.first:
                    pe.wait_ge(n_xn, 3 * NG + s.g)
                    pe.wait_ge(g_kt, s.g * GB + 3)
                    pe.wait_ge(g_vl, s.g * GB + 3)
                    for k in range(KD):
                        norm_transposes(3 * NG + s.g - 1, k, bank[1 + k])
                if s.live(1):
                    kv, slot = (s.u - 1) % HKV, (s.u - 1) // HKV % 2
                    pe.wait_ge(g_qt, n)
                    pe.wait_ge(g_kt, s.g * GB + (s.u - 1) // HKV + 1)
                    if s.had(2):
                        pe.wait_ge(g_ex, n - 1)
                    pe.matmul(bank[3][:], ident_b[:], mask[:], start=True, stop=False, skip_group_check=True)
                    for j in range(REP):
                        js = slice(j * T, (j + 1) * T)
                        last = pe.matmul(bank[3][:, js], q_t[:, js], k_t[:, slot, kv * T:(kv + 1) * T], start=False,
                                         stop=(j == REP - 1), skip_group_check=True)
                    last.then_inc(g_sp, 1)

            attention2(pe, step)
            pe.wait_ge(n_xn, 4 * NG)
            for k in range(KD):
                norm_transposes(4 * NG - 1, k, bank[1 + k])

            def expert_down(n, i):
                pe.wait_ge(m_l, n + 1)
                down((6, 7), e_hi[:, i % 2], e_lo[:, i % 2], wd_hi[:, i], wd_lo[:, i], i == 0, i == NR - 1).then_inc(m_dp, 1)

            def experts(g, first):
                for i in range(NR):
                    n, back = g * NR + i, 1 if i == 0 else 2
                    if i == 0:
                        pe.wait_ge(c_lo, 3 * NG + g + 1)
                        if first:
                            pe.wait_ge(w_lo4, 1)
                            pe.wait_ge(n_ev, 2 * 4 * NG)
                            pe.wait_ge(g_x, B)
                        else:
                            pe.wait_ge(t_l, g)
                        for b in range(GB):
                            bs = slice(b * T, (b + 1) * T)
                            for k in range(KD):
                                for j, (l, r) in enumerate(split_products(cur_hi[:, k, bs], cur_lo[:, k, bs],
                                                                          rw_hi[:, k], rw_lo[:, k])):
                                    last = pe.matmul(bank[5][:, b * E:(b + 1) * E], l, r,
                                                     start=(k == 0 and j == 0), stop=(k == KD - 1 and j == 2))
                        last.then_inc(t_lp, 1)
                        if first:
                            pe.wait_ge(w_lo4, 3)
                    for dst, w_hi, w_lo, done, read in ((bank[i % 2], wg_hi, wg_lo, m_gp, m_sg),
                                                        (bank[2 + i % 2], wu_hi, wu_lo, m_up, m_su)):
                        if i >= 2 or not first:
                            pe.wait_ge(read, n - back + 1)
                        for k in range(KD):
                            for j, (l, r) in enumerate(split_products(w_hi[:, i, k], w_lo[:, i, k], cur_hi[:, k], cur_lo[:, k])):
                                last = pe.matmul(dst[:], l, r, start=(k == 0 and j == 0), stop=(k == KD - 1 and j == 2))
                        last.then_inc(done, 1)
                    if i == 2 and first:
                        pe.wait_ge(w_lo4, 4)
                    if i == 2 and not first:
                        pe.wait_ge(m_y, 4 * g - 2)
                    if i >= 2 or not first:
                        expert_down(n - 2 if i >= 2 else n - 2, (i - 2) % NR)
                    if i == 0:
                        pe.wait_ge(t_c, g + 1)
                        for b in range(GB):
                            last = pe.transpose(bank[5][0:E, b * T:(b + 1) * T], comb[:, b, :], ident[:])
                        last.then_inc(t_ctp, 1)
                        pe.wait_ge(t_l, g + 1)
                    if i >= 1 or not first:
                        pe.wait_ge(m_em, n)
                    for j, c in enumerate((ct_hi, ct_lo)):
                        last = pe.matmul(bank[4][:], sel[:, i], c[:], start=(j == 0), stop=(j == 1))
                    last.then_inc(m_cp, 1)

            experts(0, True)
            with pe.Fori(1, NG) as g:
                experts(g, False)
            expert_down(NG * NR - 2, NR - 2)
            expert_down(NG * NR - 1, NR - 1)


def layout(a):
    import numpy as np
    freqs = (1.0 / np.float32(1000000.0) ** (np.arange(0, DH, 2, dtype=np.float32) / np.float32(DH))).astype(np.float32)
    angle = np.outer(np.arange(T, dtype=np.float32), freqs).astype(np.float32)
    cos, sin = np.cos(angle), np.sin(angle)
    cos_sin = np.stack([np.concatenate([cos, cos], 1), np.concatenate([-sin, sin], 1)], 1).astype(np.float32)
    qw, kw = a["L0_ffn_q_norm_w"], a["L0_ffn_k_norm_w"]
    rows = lambda w: w.T.reshape(KD, P, -1).transpose(1, 0, 2)
    tiles = lambda w: w.reshape(E * I, D).T.reshape(KD, P, NR, P).transpose(1, 2, 0, 3)
    qkv = a["L0_cond_qkv_w"].reshape(KD, P, 3, H, DH)
    return {
        "x": a["x"],
        "cond_t": a["cond_2048"].T.reshape(KD, P, B).transpose(1, 0, 2),
        "ada_w": a["L0_cond_ada_w"].reshape(KD, P, 6 * D).transpose(1, 0, 2),
        "ada_bt": a["L0_cond_ada_b"].reshape(12, P).T,
        "ada_bg": np.broadcast_to(a["L0_cond_ada_b"].reshape(6, D)[[2, 5]], (B, 2, D)),
        "wqk": qkv[:, :, 0:2].transpose(1, 3, 2, 0, 4),
        "wv": qkv[:, :, 2].reshape(KD, P, H * DH).transpose(1, 0, 2),
        "wo": a["L0_cond_out_w"].reshape(H, DH, D).transpose(1, 0, 2),
        "bqkv": a["L0_cond_qkv_b"].reshape(3, H, DH).transpose(2, 0, 1),
        "out_b": a["L0_cond_out_b"],
        "w1": a["L0_cond_ffn_w1"].reshape(KD, P, NF, P).transpose(1, 2, 0, 3),
        "b1": a["L0_cond_ffn_b1"].reshape(NF, P).T,
        "w2": a["L0_cond_ffn_w2"].reshape(NF, P, D).transpose(1, 0, 2),
        "b2": a["L0_cond_ffn_b2"],
        "wq": rows(a["L0_ffn_q_w"]),
        "wkv": rows(np.concatenate([a["L0_ffn_k_w"], a["L0_ffn_v_w"]], 0)),
        "wo2": a["L0_ffn_o_w"].T.reshape(H, DH, D).transpose(1, 0, 2),
        "qk_norm": np.stack([qw, np.roll(qw, DH // 2), kw, np.roll(kw, DH // 2)]),
        "cos_sin": cos_sin,
        "rw": rows(a["L0_ffn_gate_w"]),
        "wg": tiles(a["L0_ffn_wg"]),
        "wu": tiles(a["L0_ffn_wu"]),
        "wd": a["L0_ffn_wd"].transpose(0, 2, 1).reshape(NR, P, D).transpose(1, 0, 2),
        "norm_w": np.stack([a["L0_ffn_attn_norm_w"], a["L0_ffn_ffn_norm_w"]]).reshape(2, KD, P).transpose(2, 0, 1),
    }


def kernel(**inputs):
    import numpy as np
    import concourse.bacc as bacc
    from concourse.bass_utils import run_bass_kernel_spmd

    nc = bacc.Bacc("TRN2", target_bir_lowering=False, num_devices=1)
    arrays, args = {}, {}
    for name, a in layout({k: np.asarray(v) for k, v in inputs.items()}).items():
        a = np.ascontiguousarray(a)
        arrays[f"in_{name}"] = a
        args[name] = nc.dram_tensor(f"in_{name}", a.shape, mybir.dt.from_np(a.dtype), kind="ExternalInput").ap()
    out = nc.dram_tensor("out_y", (B, T, D), F32, kind="ExternalOutput").ap()
    program(nc, args, out)
    r = run_bass_kernel_spmd(nc, [arrays], core_ids=[0])
    return r.results[0]["out_y"]
```

```python
import concourse.bass as bass
from concourse import mybir
from contextlib import ExitStack

F32 = mybir.dt.float32
F32R = mybir.dt.float32r
BF16 = mybir.dt.bfloat16
ALU = mybir.AluOpType
ACT = mybir.ActivationFunctionType
X = mybir.AxisListType.X

B, T, D = 16, 128, 256
P = 128
KD = D // P
GB = 4
NG = B // GB
GT = GB * T
H, DH = 16, 128
HKV = 4
REP = H // HKV
F1 = 1024
NF = F1 // P
E, I = 8, 176
NR = E * I // P
SCALE = DH ** -0.5
EPS = 1e-6
KB = 1024


def program(nc, ins, out):
    ctx = ExitStack()
    with ctx:
        place = {}
        cursor = [16512]

        def sb(name, shape, dtype=F32, at=None):
            size = 4 if dtype in (F32, F32R) else 2
            for n in shape[1:]:
                size *= n
            size = -(-size // 32) * 32
            if at is None:
                at = cursor[0]
                cursor[0] += size
            place[name] = (at, at + size)
            return nc.alloc_sbuf_tensor_at(name, shape, dtype, offset=at)

        def sem(name):
            return ctx.enter_context(nc.semaphore(name))

        xres = sb("xres", [P, B, D])
        act_t = sb("act_t", [P, KD, B * T])
        cur_hi = sb("cur_hi", [P, KD, GT], F32R)
        cur_lo = sb("cur_lo", [P, KD, GT], F32R)
        gate = sb("gate", [P, GB, D])
        xn = sb("xn", [P, GB, D], at=place["gate"][0])
        obias = sb("obias", [P, D])
        ident = sb("ident", [P, P])
        ada_t = sb("ada_t", [P, 4, KD, B])
        ada_bt = sb("ada_bt", [P, 12])
        bqkv = sb("bqkv", [P, 3, H])
        b1 = sb("b1", [P, NF])
        norm_w = sb("norm_w", [P, 2, KD])
        bn = sb("bn", [P, GB, 6])
        mv = sb("mv", [P, GB, 2])
        vare = sb("vare", [P, GB])
        rstd = sb("rstd", [P, GB])
        mean2 = sb("mean2", [P, GB])
        neg_half = sb("neg_half", [P, 8])
        eps = sb("eps", [P, 8])
        nmax = sb("nmax", [P, 2, GB])
        rsum = sb("rsum", [P, 2, GB])
        rinv = sb("rinv", [P, 2, GB])
        W = cursor[0]
        WORK = W + 128 * KB

        wqk_hi = sb("wqk_hi", [P, H, 2, KD, DH], F32R, at=W)
        wqk_lo = sb("wqk_lo", [P, H, 2, KD, DH], F32R, at=W + 32 * KB)
        wqk_raw = sb("wqk_raw", [P, H, 2, KD, DH], at=W + 32 * KB)
        wv_hi = sb("wv_hi", [P, KD, H * DH], F32R, at=W + 64 * KB)
        wv_lo = sb("wv_lo", [P, KD, H * DH], F32R, at=W + 80 * KB)
        wv_raw = sb("wv_raw", [P, KD, H * DH], at=W + 80 * KB)
        wo_hi = sb("wo_hi", [P, H, D], F32R, at=W + 96 * KB)
        wo_lo = sb("wo_lo", [P, H, D], F32R, at=W + 112 * KB)
        wo_raw = sb("wo_raw", [P, H, D], at=W + 112 * KB)
        q1 = sb("q1", [P, 2, GT], at=WORK)
        k1 = sb("k1", [P, 2, GT], at=WORK + 4 * KB)
        v1 = sb("v1", [P, 2, GB, 2 * DH], at=WORK + 8 * KB)
        p1 = sb("p1", [P, 2, GB, T], at=WORK + 16 * KB)
        pt1 = sb("pt1", [P, GT], at=WORK + 20 * KB)
        o1_hi = sb("o1_hi", [P, 2, GT], F32R, at=WORK + 22 * KB)
        o1_lo = sb("o1_lo", [P, 2, GT], F32R, at=WORK + 26 * KB)
        ada_w = sb("ada_w", [P, KD, 6 * D], at=W + 16 * KB)
        cond_t = sb("cond_t", [P, KD, B], at=WORK + 30 * KB)
        ada_bg = sb("ada_bg", [B, 2, D], at=W + 28 * KB)
        gates = sb("gates", [B, 2, D], at=W + 30 * KB)
        w1_hi = sb("w1_hi", [P, NF, KD, P], F32R, at=W + 16 * KB)
        w1_lo = sb("w1_lo", [P, NF, KD, P], F32R, at=W)
        w1_raw = sb("w1_raw", [P, NF, KD, P], at=W)
        w2_hi = sb("w2_hi", [P, NF, D], F32R, at=W + 24 * KB)
        w2_lo = sb("w2_lo", [P, NF, D], F32R, at=W + 8 * KB)
        w2_raw = sb("w2_raw", [P, NF, D], at=W + 8 * KB)
        hf = sb("hf", [P, 2, GT], at=WORK)
        h_hi = sb("h_hi", [P, 2, GT], F32R, at=WORK + 4 * KB)
        h_lo = sb("h_lo", [P, 2, GT], F32R, at=WORK + 8 * KB)

        wq_hi = sb("wq_hi", [P, KD, H * DH], F32R, at=W + 32 * KB)
        wq_lo = sb("wq_lo", [P, KD, H * DH], F32R, at=W + 48 * KB)
        wq_raw = sb("wq_raw", [P, KD, H * DH], at=W + 48 * KB)
        wkv_hi = sb("wkv_hi", [P, KD, 2 * HKV * DH], F32R, at=W + 64 * KB)
        wkv_lo = sb("wkv_lo", [P, KD, 2 * HKV * DH], F32R, at=W + 72 * KB)
        wkv_raw = sb("wkv_raw", [P, KD, 2 * HKV * DH], at=W + 72 * KB)
        wo2_hi = sb("wo2_hi", [P, H, D], F32R, at=W + 80 * KB)
        wo2_lo = sb("wo2_lo", [P, H, D], F32R, at=W + 96 * KB)
        wo2_raw = sb("wo2_raw", [P, H, D], at=W + 96 * KB)
        W2 = W + 112 * KB
        qr = sb("qr", [P, 2, REP * DH], at=W2)
        rb = sb("rb", [P, REP * DH], at=W2 + 4 * KB)
        sq = sb("sq", [P, REP * DH], at=W2 + 6 * KB)
        kr = sb("kr", [P, HKV * DH], at=W2 + 8 * KB)
        kb = sb("kb", [P, HKV * DH], at=W2 + 10 * KB)
        ksq = sb("ksq", [P, HKV * DH], at=W2 + 12 * KB)
        q_t = sb("q_t", [P, 2, REP * T], at=W2 + 14 * KB)
        k_t = sb("k_t", [P, 2, HKV * T], at=W2 + 18 * KB)
        v_hi = sb("v_hi", [P, 2, HKV * DH], F32R, at=W2 + 22 * KB)
        v_lo = sb("v_lo", [P, 2, HKV * DH], F32R, at=W2 + 26 * KB)
        p2 = sb("p2", [P, 2, REP, T], at=W2 + 30 * KB)
        pt_hi = sb("pt_hi", [P, REP * T], F32R, at=W2 + 34 * KB)
        pt_lo = sb("pt_lo", [P, REP * T], F32R, at=W2 + 36 * KB)
        o2_hi = sb("o2_hi", [P, REP * T], F32R, at=W2 + 38 * KB)
        o2_lo = sb("o2_lo", [P, REP * T], F32R, at=W2 + 40 * KB)
        rope = sb("rope", [P, 4, DH], at=W2 + 42 * KB)
        cos_sin = sb("cos_sin", [P, 2, DH], at=W2 + 44 * KB)
        mask = sb("mask", [P, REP * T], BF16, at=W2 + 45 * KB)
        ident_b = sb("ident_b", [P, P], BF16, at=W2 + 46 * KB)
        mask_f = sb("mask_f", [P, T], at=W2 + 46 * KB + 256)
        small = W2 + 46 * KB + 768
        q_ms = sb("q_ms", [P, 2, REP], at=small)
        q_ve = sb("q_ve", [P, 2, REP], at=small + 32)
        rq = sb("rq", [P, 4, REP], at=small + 64)
        k_ms = sb("k_ms", [P, HKV], at=small + 128)
        k_ve = sb("k_ve", [P, HKV], at=small + 160)
        rk = sb("rk", [P, HKV], at=small + 192)
        nb = sb("nb", [P, 2, REP], at=small + 224)
        wg_hi = sb("wg_hi", [P, NR, KD, P], F32R, at=W)
        wg_lo = sb("wg_lo", [P, NR, KD, P], F32R, at=W + 11 * KB)
        wg_raw = sb("wg_raw", [P, NR, KD, P], at=W + 11 * KB)
        sel = sb("sel", [E, NR, P], F32R, at=W + 22 * KB)
        sel_f = sb("sel_f", [E, NR, P], at=W + 22 * KB)
        rw_raw = sb("rw_raw", [P, KD, E], at=W + 28 * KB)
        rw_hi = sb("rw_hi", [P, KD, E], F32R, at=W + 28 * KB + 64)
        rw_lo = sb("rw_lo", [P, KD, E], F32R, at=W + 28 * KB + 128)
        before = sb("before", [P, E, E], at=W + 28 * KB + 256)
        wu_hi = sb("wu_hi", [P, NR, KD, P], F32R, at=W + 32 * KB)
        wu_lo = sb("wu_lo", [P, NR, KD, P], F32R, at=W + 43 * KB)
        wu_raw = sb("wu_raw", [P, NR, KD, P], at=W + 43 * KB)
        wd_hi = sb("wd_hi", [P, NR, D], F32R, at=W + 54 * KB)
        wd_lo = sb("wd_lo", [P, NR, D], F32R, at=W + 65 * KB)
        wd_raw = sb("wd_raw", [P, NR, D], at=W + 65 * KB)
        sg = sb("sg", [P, 2, GT], at=W2)
        em = sb("em", [P, 2, GT], at=W2 + 4 * KB)
        e_hi = sb("e_hi", [P, 2, GT], F32R, at=W2 + 8 * KB)
        e_lo = sb("e_lo", [P, 2, GT], F32R, at=W2 + 12 * KB)
        x0 = sb("x0", [P, GB, D], at=W2 + 16 * KB)
        y = sb("y", [P, GB, D], at=W2 + 20 * KB)
        ct_hi = sb("ct_hi", [E, GT], F32R, at=W2 + 24 * KB)
        ct_lo = sb("ct_lo", [E, GT], F32R, at=W2 + 26 * KB)
        gt = sb("gt", [P, GB, E, E], at=W2 + 28 * KB)
        eq = sb("eq", [P, GB, E, E], at=W2 + 29 * KB)
        probs = sb("probs", [P, GB, E], at=W2 + 30 * KB)
        pick = sb("pick", [P, GB, E], at=W2 + 30 * KB + 128)
        comb = sb("comb", [P, GB, E], at=W2 + 30 * KB + 256)
        r4 = sb("r4", [P, 4, GB], at=W2 + 30 * KB + 384)

        bank = [ctx.enter_context(nc.psum_tensor(f"bank{i}", [P, 512], F32)) for i in range(8)]
        gates_dram = nc.dram_tensor("gates_scratch", (B, 2, D), F32).ap()

        d_x = [sem(f"d_x{g}") for g in range(NG)]
        d_first, d_small = sem("d_first"), sem("d_small")
        d_ada1, d_ada2 = sem("d_ada1"), sem("d_ada2")
        d_pair = [sem(f"d_pair{c}") for c in range(H // 2)]
        d_gout = sem("d_gout")
        d_gate = sem("d_gate")
        d_wq, d_wkv, d_oproj, d_rope = sem("d_wq"), sem("d_wkv"), sem("d_oproj"), sem("d_rope")
        d_wg, d_wu, d_wd, d_rw, d_xin = sem("d_wg"), sem("d_wu"), sem("d_wd"), sem("d_rw"), sem("d_xin")
        d_w1, d_w2, d_b2 = sem("d_w1"), sem("d_w2"), sem("d_b2")
        d_out = sem("d_out")
        consts, ada_p, ada_s, bq_s = sem("consts"), sem("ada_p"), sem("ada_s"), sem("bq_s")
        w_hi1, w_lo1 = sem("w_hi1"), sem("w_lo1")
        w_hi2, w_lo2 = sem("w_hi2"), sem("w_lo2")
        n_bn, n_mv, n_st, n_ve, n_rs, n_xn, n_tp, n_ev = (
            sem(f"n_{x}") for x in ("bn", "mv", "st", "ve", "rs", "xn", "tp", "ev"))
        n_m2 = sem("n_m2")
        c_hi, c_lo = sem("c_hi"), sem("c_lo")
        a_qp, a_kp, a_vp, a_sp, a_tp, a_pvp, a_op = (
            sem(f"a_{x}") for x in ("qp", "kp", "vp", "sp", "tp", "pvp", "op"))
        a_q, a_k, a_v, a_mx, a_ex, a_ri, a_pn, a_pt, a_oh, a_ol = (
            sem(f"a_{x}") for x in ("q", "k", "v", "mx", "ex", "ri", "pn", "pt", "oh", "ol"))
        r_add, r_mul, r_x = sem("r_add"), sem("r_mul"), sem("r_x")
        f_up, f_dp, f_g, f_h, f_l = (sem(f"f_{x}") for x in ("up", "dp", "g", "h", "l"))

        w_hi3, w_lo3, g_tab, g_mask = sem("w_hi3"), sem("w_lo3"), sem("g_tab"), sem("g_mask")
        g_kp, g_vp, g_qp, g_tp, g_qtp, g_op, g_pvp, g_ktp, g_sp = (
            sem(f"g_{x}") for x in ("kp", "vp", "qp", "tp", "qtp", "op", "pvp", "ktp", "sp"))
        g_ex, g_ksq, g_sq, g_ph, g_vh, g_qt, g_oh, g_kt = (
            sem(f"g_{x}") for x in ("ex", "ksq", "sq", "ph", "vh", "qt", "oh", "kt"))
        g_x, g_mx, g_nb, g_kb, g_qb, g_ks, g_kr, g_pl, g_ss, g_ri, g_vl, g_ol = (
            sem(f"g_{x}") for x in ("x", "mx", "nb", "kb", "qb", "ks", "kr", "pl", "ss", "ri", "vl", "ol"))
        g_ka, g_rk, g_kv, g_qr, g_rq, g_qv, g_pn = (
            sem(f"g_{x}") for x in ("ka", "rk", "kv", "qr", "rq", "qv", "pn"))
        w_hi4, w_lo4, m_sel = sem("w_hi4"), sem("w_lo4"), sem("m_sel")
        m_gp, m_up, m_cp, m_dp, m_sg, m_su, m_em, m_h, m_l, m_y, m_o = (
            sem(f"m_{x}") for x in ("gp", "up", "cp", "dp", "sg", "su", "em", "h", "l", "y", "o"))
        t_lp, t_ctp, t_ex, t_h, t_l, t_v, t_c = (sem(f"t_{x}") for x in ("lp", "ctp", "ex", "h", "l", "v", "c"))
        RV = 13

        block = ctx.enter_context(nc.Block())

        class NormJob:

            def __init__(self, n, g, kind, part):
                self.n, self.g, self.kind, self.part = n, g, kind, part

        def background_norm(g, h, first):
            if first and 3 <= h < 3 + 4 * (NG - 1):
                return NormJob(1 + (h - 3) // 4, 1 + (h - 3) // 4, 0, (h - 3) % 4)
            if not first and 3 <= h < 7:
                return NormJob(NG + g - 1, g - 1, 1, h - 3)
            return None

        class Step:

            def __init__(self, g, u, first):
                self.g, self.u, self.first = g, u, first
                self.n, self.b, self.kv = g * 4 * GB + u, u // HKV, u % HKV
                self.seq = g * GB + self.b

            def new(self):
                return self.u < 4 * GB

            def live(self, k):
                return self.had(k) and self.u - k < 4 * GB

            def had(self, k):
                return self.u >= k or not self.first

        def attention2(eng, step):
            for u in range(4 * GB):
                step(Step(0, u, True))
            with eng.Fori(1, NG) as g:
                for u in range(4 * GB):
                    step(Step(g, u, False))
            for u in range(4 * GB, 4 * GB + 7):
                step(Step(NG - 1, u, False))

        def span(t, k, g, b0=0, nb=GB):
            return t[:, k, bass.ds((g * GB + b0) * T, nb * T)]

        def split_products(hi_l, lo_l, hi_r, lo_r):
            return ((hi_l, hi_r), (hi_l, lo_r), (lo_l, hi_r))

        @block.sync
        def _(sp):
            def load_x(g):
                sp.dma_start(xres[:, g * GB:(g + 1) * GB, :],
                             ins["x"][g * GB:(g + 1) * GB].rearrange("b t d -> t b d")).then_inc(d_x[g], 16)

            def load_pair(c):
                hs, cs = slice(2 * c, 2 * c + 2), slice(2 * DH * c, 2 * DH * (c + 1))
                sp.dma_start(wqk_raw[:, hs], ins["wqk"][:, hs]).then_inc(d_pair[c], 16)
                sp.dma_start(wv_raw[:, :, cs], ins["wv"][:, :, cs]).then_inc(d_pair[c], 16)
                sp.dma_start(wo_raw[:, hs], ins["wo"][:, hs]).then_inc(d_pair[c], 16)

            load_x(0)
            sp.dma_start(cond_t[:], ins["cond_t"]).then_inc(d_first, 16)
            sp.dma_start(ada_bt[:], ins["ada_bt"]).then_inc(d_first, 16)
            sp.dma_start(bqkv[:], ins["bqkv"]).then_inc(d_first, 16)
            sp.dma_start(ada_w[:, :, 0:2 * D], ins["ada_w"][:, :, 0:2 * D]).then_inc(d_ada1, 16)
            load_pair(0)
            sp.dma_start(ada_w[:, :, 2 * D:], ins["ada_w"][:, :, 2 * D:]).then_inc(d_ada2, 16)
            sp.dma_start(ada_bg[:], ins["ada_bg"]).then_inc(d_small, 16)
            load_pair(1)
            load_x(1)
            for c in range(2, H // 2):
                load_pair(c)
            sp.dma_start(b1[:], ins["b1"]).then_inc(d_small, 16)
            sp.dma_start(norm_w[:], ins["norm_w"]).then_inc(d_small, 16)
            sp.dma_start(obias[:], ins["out_b"].partition_broadcast(P)).then_inc(d_small, 16)
            for g in range(2, NG):
                load_x(g)
            sp.wait_ge(ada_s, 9)
            sp.dma_start(gates_dram, gates[:]).then_inc(d_gout, 16)
            sp.wait_ge(d_gout, 16)
            sp.wait_ge(n_tp, 2 * NG)
            sp.dma_start(gate[:], gates_dram[0:GB, 0, :].partition_broadcast(P)).then_inc(d_gate, 16)
            with sp.Fori(1, NG) as g:
                sp.wait_ge(n_tp, 2 * (NG + g))
                sp.dma_start(gate[:], gates_dram[bass.ds(g * GB, GB), 0, :].partition_broadcast(P)).then_inc(d_gate, 16)
            sp.wait_ge(a_kp, 3 * H + 8)
            sp.dma_start(w1_raw[:], ins["w1"]).then_inc(d_w1, 16)
            sp.dma_start(w2_raw[:], ins["w2"]).then_inc(d_w2, 16)
            sp.wait_ge(a_vp, NG * H)
            sp.dma_start(wkv_raw[:], ins["wkv"]).then_inc(d_wkv, 16)
            sp.dma_start(wq_raw[:], ins["wq"]).then_inc(d_wq, 16)
            sp.wait_ge(a_op, NG * H)
            sp.dma_start(wo2_raw[:], ins["wo2"]).then_inc(d_oproj, 16)
            sp.dma_start(rope[:], ins["qk_norm"].partition_broadcast(P)).then_inc(d_rope, 16)
            sp.dma_start(cos_sin[:], ins["cos_sin"]).then_inc(d_rope, 16)
            sp.wait_ge(r_add, 2 * NG)
            sp.dma_start(obias[:], ins["b2"].partition_broadcast(P)).then_inc(d_b2, 16)
            sp.wait_ge(n_tp, 2 * (2 * NG))
            sp.dma_start(gate[:], gates_dram[0:GB, 1, :].partition_broadcast(P)).then_inc(d_gate, 16)
            with sp.Fori(1, NG) as g:
                sp.wait_ge(n_tp, 2 * (2 * NG + g))
                sp.dma_start(gate[:], gates_dram[bass.ds(g * GB, GB), 1, :].partition_broadcast(P)).then_inc(d_gate, 16)
            sp.wait_ge(f_up, NG * NF)
            sp.wait_ge(f_dp, NG * NF)
            sp.dma_start(wg_raw[:], ins["wg"]).then_inc(d_wg, 16)
            sp.dma_start(rw_raw[:], ins["rw"]).then_inc(d_rw, 16)
            sp.wait_ge(g_qp, NG * 4 * GB)
            sp.wait_ge(g_vp, B)
            sp.dma_start(wu_raw[:], ins["wu"]).then_inc(d_wu, 16)
            sp.dma_start(wd_raw[:], ins["wd"]).then_inc(d_wd, 16)
            sp.wait_ge(g_x, B)
            sp.dma_start(x0[:], ins["x"][0:GB].rearrange("b t d -> t b d")).then_inc(d_xin, 16)
            sp.wait_ge(m_y, 4)
            sp.dma_start(out[0:GB].rearrange("b t d -> t b d"), y[:]).then_inc(d_out, 16)
            with sp.Fori(1, NG) as g:
                sp.dma_start(x0[:], ins["x"][bass.ds(g * GB, GB)].rearrange("b t d -> t b d")).then_inc(d_xin, 16)
                sp.wait_ge(m_y, 4 * g + 4)
                sp.dma_start(out[bass.ds(g * GB, GB)].rearrange("b t d -> t b d"), y[:]).then_inc(d_out, 16)
            sp.wait_ge(d_out, 16 * NG)

        @block.gpsimd
        def _(pool):
            nc.gpsimd.memset(neg_half[:], -0.5).then_inc(consts, 1)
            nc.gpsimd.memset(ident[:], 0.0).then_inc(consts, 1)
            nc.gpsimd.memset(eps[:], EPS).then_inc(consts, 1)
            pool.wait_ge(consts, 3)
            nc.gpsimd.affine_select(out=ident[:], in_=ident[:], compare_op=ALU.not_equal, fill=1.0, base=0,
                                    pattern=[[-1, P]], channel_multiplier=1).then_inc(consts, 1)

            def norm(n, rms=False):
                pool.wait_ge(n_st, n + 1)
                nc.gpsimd.tensor_tensor(vare[:], mv[:, :, 1], eps[:, 0:GB], ALU.add).then_inc(n_ve, 1)
                if rms:
                    nc.gpsimd.tensor_tensor(mean2[:], mv[:, :, 0], mv[:, :, 0], ALU.mult).then_inc(n_m2, 1)
                    pool.wait_ge(n_m2, 2 * (n - 2 * NG) + 1)
                    pool.wait_ge(n_ve, n + 1)
                    nc.gpsimd.tensor_tensor(vare[:], vare[:], mean2[:], ALU.add).then_inc(n_m2, 1)
                    pool.wait_ge(n_m2, 2 * (n - 2 * NG) + 2)
                pool.wait_ge(n_ve, n + 1)
                nc.gpsimd.tensor_tensor(rstd[:], vare[:], neg_half[:, 0:GB], ALU.pow).then_inc(n_rs, 1)

            norm(0)

            def normalise(n, h):
                pool.wait_ge(a_ri, n + 1)
                nc.gpsimd.tensor_tensor(p1[:, h % 2], p1[:, h % 2],
                                        rinv[:, h % 2].unsqueeze(2).broadcast_to([P, GB, T]),
                                        ALU.mult).then_inc(a_pn, 1)

            def attention1(g, first):
                for h in range(H):
                    if h >= 1 or not first:
                        normalise(g * H + h - 1, (h - 1) % 2)
                    job = background_norm(g, h, first)
                    if job and job.part == 0:
                        norm(job.n)

            attention1(0, True)
            with pool.Fori(1, NG) as g:
                attention1(g, False)
            normalise(NG * H - 1, 1)
            norm(2 * NG - 1)

            pool.wait_ge(a_op, NG * H)
            nc.gpsimd.memset(mask_f[:], 0.0).then_inc(g_mask, 1)
            pool.wait_ge(g_mask, 1)
            nc.gpsimd.affine_select(out=mask_f[:], in_=mask_f[:], compare_op=ALU.is_ge, fill=-1e30, base=0,
                                    pattern=[[-1, T]], channel_multiplier=1).then_inc(g_mask, 1)

            for g in range(NG):
                norm(2 * NG + g, True)
            pool.wait_ge(f_dp, NG * NF)
            nc.gpsimd.memset(sel_f[:], 1.0).then_inc(m_sel, 1)
            nc.gpsimd.memset(before[:], 1.0).then_inc(m_sel, 1)
            pool.wait_ge(m_sel, 2)
            nc.gpsimd.affine_select(out=sel_f[:], in_=sel_f[:], compare_op=ALU.is_ge, fill=0.0, base=0,
                                    pattern=[[P, NR], [1, P]], channel_multiplier=-I).then_inc(m_sel, 1)
            nc.gpsimd.affine_select(out=before[:], in_=before[:], compare_op=ALU.is_gt, fill=0.0, base=0,
                                    pattern=[[1, E], [-1, E]], channel_multiplier=0).then_inc(m_sel, 1)
            pool.wait_ge(m_sel, 4)
            nc.gpsimd.affine_select(out=sel_f[:], in_=sel_f[:], compare_op=ALU.is_ge, fill=0.0, base=I - 1,
                                    pattern=[[-P, NR], [-1, P]], channel_multiplier=I).then_inc(m_sel, 1)

            def step(s):
                n, new_seq = s.n, s.new() and s.kv == 0
                if new_seq:
                    pool.wait_ge(g_kb, s.seq + 1)
                    nc.gpsimd.tensor_tensor(kr[:], kr[:], kb[:], ALU.add).then_inc(g_ka, 1)
                if s.new():
                    pool.wait_ge(g_qb, n + 1)
                    nc.gpsimd.tensor_tensor(qr[:, s.u % 2], qr[:, s.u % 2], rb[:], ALU.add).then_inc(g_qr, 1)
                if s.live(3):
                    pool.wait_ge(g_ri, n - 2)
                    nc.gpsimd.tensor_tensor(p2[:, (s.u - 3) % 2], p2[:, (s.u - 3) % 2],
                                            rinv[:, (s.u - 3) % 2].unsqueeze(2).broadcast_to([P, REP, T]),
                                            ALU.mult).then_inc(g_pn, 1)
                if s.new():
                    pool.wait_ge(g_ss, n + 1)
                    if s.had(2):
                        pool.wait_ge(g_rq, n - 1)
                    nc.gpsimd.tensor_tensor(q_ve[:, s.u % 2], q_ms[:, s.u % 2], eps[:, 0:REP], ALU.add).then_inc(g_qv, 1)
                    pool.wait_ge(g_qv, n + 1)
                    if s.had(4):
                        pool.wait_ge(g_ex, n - 3)
                    nc.gpsimd.tensor_tensor(rq[:, s.u % 4], q_ve[:, s.u % 2], neg_half[:, 0:REP], ALU.pow).then_inc(g_rq, 1)
                if new_seq:
                    pool.wait_ge(g_ks, s.seq + 1)
                    if s.had(4):
                        pool.wait_ge(g_rk, s.seq)
                    nc.gpsimd.tensor_tensor(k_ve[:], k_ms[:], eps[:, 0:HKV], ALU.add).then_inc(g_kv, 1)
                    pool.wait_ge(g_kv, s.seq + 1)
                    nc.gpsimd.tensor_tensor(rk[:], k_ve[:], neg_half[:, 0:HKV], ALU.pow).then_inc(g_rk, 1)
                if s.u == 8 and not s.first:
                    norm(3 * NG + s.g - 1, True)

            attention2(pool, step)
            norm(4 * NG - 1, True)

        @block.scalar
        def _(act):
            def cur(c, g):
                nc.scalar.activation(cur_hi[:], act_t[:, :, bass.ds(g * GT, GT)], ACT.Copy).then_inc(c_hi, 1)

            def split_pair(c):
                hs, cs = slice(2 * c, 2 * c + 2), slice(2 * DH * c, 2 * DH * (c + 1))
                act.wait_ge(d_pair[c], 48)
                if c == 4:
                    act.wait_ge(ada_p, 2)
                    act.wait_ge(ada_s, 9)
                    act.wait_ge(d_gout, 16)
                nc.scalar.activation(wqk_hi[:, hs], wqk_raw[:, hs], ACT.Copy).then_inc(w_hi1, 1)
                nc.scalar.activation(wv_hi[:, :, cs], wv_raw[:, :, cs], ACT.Copy).then_inc(w_hi1, 1)
                nc.scalar.activation(wo_hi[:, hs], wo_raw[:, hs], ACT.Copy).then_inc(w_hi1, 1)

            act.wait_ge(d_first, 48)
            nc.scalar.activation(bqkv[:, 0], bqkv[:, 0], ACT.Copy, scale=SCALE).then_inc(bq_s, 1)
            split_pair(0)

            def exps(n, h):
                act.wait_ge(a_mx, n + 1)
                if not isinstance(n, int) or n >= 2:
                    act.wait_ge(a_tp, n - 1)
                for b in range(GB):
                    last = nc.scalar.activation(p1[:, h % 2, b], bank[3][:, b * T:(b + 1) * T], ACT.Exp,
                                                bias=nmax[:, h % 2, b:b + 1], accum_out=rsum[:, h % 2, b:b + 1])
                last.then_inc(a_ex, 1)

            def o_hi(n, h):
                act.wait_ge(a_pvp, n + 1)
                if not isinstance(n, int) or n >= 2:
                    act.wait_ge(a_op, n - 1)
                nc.scalar.activation(o1_hi[:, h % 2], bank[5][:], ACT.Identity,
                                     bias=bqkv[:, 2, h:h + 1]).then_inc(a_oh, 1)

            def attention1(g, first):
                for h in range(H):
                    n = g * H + h
                    if h == 0:
                        act.wait_ge(n_ev, 2 * (g + 1))
                        if not first:
                            act.wait_ge(a_vp, n)
                        cur(g, g)
                    if h >= 1 or not first:
                        exps(n - 1, (h - 1) % 2)
                    act.wait_ge(a_qp, n + 1)
                    if h >= 2 or not first:
                        act.wait_ge(a_sp, n - 1)
                    nc.scalar.activation(q1[:, h % 2], bank[0][:], ACT.Identity, scale=SCALE,
                                         bias=bqkv[:, 0, h:h + 1]).then_inc(a_q, 1)
                    if h >= 2 or not first:
                        o_hi(n - 2, (h - 2) % H)
                    act.wait_ge(a_vp, n + 1)
                    if h >= 4 or not first:
                        act.wait_ge(a_pvp, n - h % 2 - 2)
                    nc.scalar.activation(v1[:, h // 2 % 2, h % 2 * 2:h % 2 * 2 + 2],
                                         bank[2][:].rearrange("p (b d) -> p b d", b=2), ACT.Copy).then_inc(a_v, 1)
                    if first and h % 2 == 0 and h < H - 2:
                        split_pair(h // 2 + 1)

            attention1(0, True)
            with act.Fori(1, NG) as g:
                attention1(g, False)
            n = NG * H
            exps(n - 1, 1)
            o_hi(n - 2, H - 2)
            o_hi(n - 1, H - 1)

            act.wait_ge(d_w1, 16)
            act.wait_ge(a_kp, NG * H)
            nc.scalar.activation(w1_hi[:], w1_raw[:], ACT.Copy).then_inc(w_hi2, 1)
            act.wait_ge(d_w2, 16)
            nc.scalar.activation(w2_hi[:], w2_raw[:], ACT.Copy).then_inc(w_hi2, 1)

            def split3(c):
                if isinstance(c, int):
                    act.wait_ge(d_wkv, 16)
                nc.scalar.activation(wkv_hi[:, :, bass.ds(c * 256, 256)], wkv_raw[:, :, bass.ds(c * 256, 256)],
                                     ACT.Copy).then_inc(w_hi3, 1)
                nc.scalar.activation(wq_hi[:, :, bass.ds(c * 512, 512)], wq_raw[:, :, bass.ds(c * 512, 512)],
                                     ACT.Copy).then_inc(w_hi3, 1)
                nc.scalar.activation(wo2_hi[:, bass.ds(c * 4, 4)], wo2_raw[:, bass.ds(c * 4, 4)],
                                     ACT.Copy).then_inc(w_hi3, 1)

            def ffn1(g, first):
                for f in range(NF):
                    m = g * NF + f
                    if f == 4 and not first:
                        act.wait_ge(d_wkv, 16)
                        act.wait_ge(d_wq, 16)
                        act.wait_ge(d_oproj, 16)
                        act.wait_ge(a_op, NG * H)
                        split3(g - 1)
                    if f == 0:
                        act.wait_ge(n_ev, 2 * (NG + g + 1))
                        if first:
                            act.wait_ge(a_vp, NG * H)
                        else:
                            act.wait_ge(f_up, m)
                        cur(NG + g, g)
                    act.wait_ge(f_up, m + 1)
                    if f >= 2 or not first:
                        act.wait_ge(f_l, m - 1)
                    nc.scalar.activation(hf[:, f % 2], bank[f % 2][:], ACT.Gelu, bias=b1[:, f:f + 1]).then_inc(f_g, 1)
                    act.wait_ge(f_g, m + 1)
                    if f >= 2 or not first:
                        act.wait_ge(f_dp, m - 1)
                    nc.scalar.activation(h_hi[:, f % 2], hf[:, f % 2], ACT.Copy).then_inc(f_h, 1)

            ffn1(0, True)
            with act.Fori(1, NG) as g:
                ffn1(g, False)
            split3(NG - 1)

            def step(s):
                n, new_seq = s.n, s.new() and s.kv == 0
                if s.u == 0:
                    act.wait_ge(n_ev, 2 * (2 * NG + s.g + 1))
                    if s.first:
                        act.wait_ge(f_up, NG * NF)
                    else:
                        act.wait_ge(g_qp, n)
                    cur(2 * NG + s.g, s.g)
                if s.live(3):
                    act.wait_ge(g_nb, n - 2)
                    if s.had(5):
                        act.wait_ge(g_tp, n - 4)
                    for j in range(REP):
                        last = nc.scalar.activation(p2[:, (s.u - 3) % 2, j], bank[3][:, j * T:(j + 1) * T], ACT.Exp,
                                                    scale=rq[:, (s.u - 3) % 4, j:j + 1],
                                                    bias=nb[:, (s.u - 3) % 2, j:j + 1],
                                                    accum_out=rsum[:, (s.u - 3) % 2, j:j + 1])
                    last.then_inc(g_ex, 1)
                if new_seq:
                    act.wait_ge(g_kb, s.seq + 1)
                    if s.had(4):
                        act.wait_ge(g_ks, s.seq)
                    nc.scalar.activation(ksq[:], bank[1][:], ACT.Square, scale=SCALE).then_inc(g_ksq, 1)
                if s.new():
                    act.wait_ge(g_qb, n + 1)
                    if s.had(1):
                        act.wait_ge(g_ss, n)
                    nc.scalar.activation(sq[:], bank[0][:], ACT.Square, scale=SCALE).then_inc(g_sq, 1)
                if s.live(5):
                    act.wait_ge(g_pvp, n - 4)
                    if s.had(6):
                        act.wait_ge(g_op, n - 5)
                    nc.scalar.activation(o2_hi[:], bank[6][:], ACT.Copy).then_inc(g_oh, 1)
                if s.live(1):
                    act.wait_ge(g_qtp, n)
                    if s.had(3):
                        act.wait_ge(g_sp, n - 2)
                    nc.scalar.activation(q_t[:, (s.u - 1) % 2], bank[4][:], ACT.Copy).then_inc(g_qt, 1)
                if s.live(4):
                    act.wait_ge(g_tp, n - 3)
                    if s.had(5):
                        act.wait_ge(g_pvp, n - 4)
                    nc.scalar.activation(pt_hi[:], bank[5][:], ACT.Copy).then_inc(g_ph, 1)
                if new_seq:
                    act.wait_ge(g_vp, s.seq + 1)
                    if s.had(8):
                        act.wait_ge(g_pvp, 4 * (s.seq - 1))
                    nc.scalar.activation(v_hi[:, s.b % 2], bank[2][:], ACT.Copy).then_inc(g_vh, 1)
                if s.new() and s.kv == 1:
                    act.wait_ge(g_ktp, s.seq + 1)
                    if s.had(8):
                        act.wait_ge(g_sp, 4 * (s.seq - 1))
                    nc.scalar.activation(k_t[:, s.b % 2], bank[1][:], ACT.Copy).then_inc(g_kt, 1)

            attention2(act, step)

            act.wait_ge(m_sel, 5)
            act.wait_ge(d_rw, 16)
            nc.scalar.activation(sel[:], sel_f[:], ACT.Copy).then_inc(w_hi4, 1)
            nc.scalar.activation(rw_hi[:], rw_raw[:], ACT.Copy).then_inc(w_hi4, 1)
            for d, hi, raw in ((d_wg, wg_hi, wg_raw), (d_wu, wu_hi, wu_raw), (d_wd, wd_hi, wd_raw)):
                act.wait_ge(d, 16)
                nc.scalar.activation(hi[:], raw[:], ACT.Copy).then_inc(w_hi4, 1)

            def experts(g, first):
                for i in range(NR):
                    n, back = g * NR + i, 1 if i == 0 else 2
                    if i == 0:
                        act.wait_ge(n_ev, 2 * (3 * NG + g + 1))
                        if first:
                            act.wait_ge(g_qp, NG * 4 * GB)
                        else:
                            act.wait_ge(m_up, n)
                        cur(3 * NG + g, g)
                        act.wait_ge(t_v, g * RV + 2)
                        nc.scalar.activation(probs[:], probs[:], ACT.Exp).then_inc(t_ex, 1)
                    act.wait_ge(m_gp, n + 1)
                    if i >= 2 or not first:
                        act.wait_ge(m_em, n - back + 1)
                    nc.scalar.activation(sg[:, i % 2], bank[i % 2][:], ACT.Silu).then_inc(m_sg, 1)
                    if i == 0:
                        act.wait_ge(t_ctp, g + 1)
                        if not first:
                            act.wait_ge(m_cp, n)
                        nc.scalar.activation(ct_hi[:], bank[5][0:E, :], ACT.Copy).then_inc(t_h, 1)
                    act.wait_ge(m_em, n + 1)
                    if i >= 2 or not first:
                        act.wait_ge(m_dp, n - back + 1)
                    nc.scalar.activation(e_hi[:, i % 2], em[:, i % 2], ACT.Copy).then_inc(m_h, 1)

            experts(0, True)
            with act.Fori(1, NG) as g:
                experts(g, False)

        @block.vector
        def _(dve):
            def norm_stats(g):
                for b in range(GB):
                    last = nc.vector.bn_stats(bn[:, b], xres[:, bass.ds(g * GB + b, 1), :].rearrange("p a d -> p (a d)"))
                last.then_inc(n_bn, 1)

            def norm_sums():
                for b in range(GB):
                    last = nc.vector.bn_aggr(mv[:, b], bn[:, b])
                last.then_inc(n_st, 1)

            def norm_apply(n, g):
                dve.wait_ge(n_rs, n + 1)
                for b in range(GB):
                    last = nc.vector.tensor_scalar(xn[:, b], xres[:, bass.ds(g * GB + b, 1), :].rearrange("p a d -> p (a d)"),
                                                   mv[:, b, 0:1], rstd[:, b:b + 1], ALU.subtract, ALU.mult)
                last.then_inc(n_xn, 1)

            def norm_apply_rms(n, g):
                dve.wait_ge(n_rs, n + 1)
                for b in range(GB):
                    last = nc.vector.tensor_scalar(xn[:, b], xres[:, bass.ds(g * GB + b, 1), :].rearrange("p a d -> p (a d)"),
                                                   rstd[:, b:b + 1], None, ALU.mult)
                last.then_inc(n_xn, 1)

            def norm_weight(n, g, k, kind, src):
                dve.wait_ge(n_tp, 2 * n + k + 1)
                nc.vector.tensor_scalar(span(act_t, k, g), src[:], norm_w[:, kind, k:k + 1], None,
                                        ALU.mult).then_inc(n_ev, 1)

            def norm_ada(n, g, k, kind, src):
                dve.wait_ge(n_tp, 2 * n + k + 1)
                for b in range(GB):
                    last = nc.vector.tensor_scalar(span(act_t, k, g, b, 1), src[:, b * T:(b + 1) * T],
                                                   ada_t[:, 2 * kind + 1, k, bass.ds(g * GB + b, 1)],
                                                   ada_t[:, 2 * kind, k, bass.ds(g * GB + b, 1)], ALU.mult, ALU.add)
                last.then_inc(n_ev, 1)

            def cur_rest(c, g):
                dve.wait_ge(c_hi, c + 1)
                nc.vector.tensor_tensor(cur_lo[:], act_t[:, :, bass.ds(g * GT, GT)], cur_hi[:].bitcast(F32),
                                        ALU.subtract).then_inc(c_lo, 1)

            def residual(r, g, banks, phase_r):
                dve.wait_ge(d_gate, 16 * (r + 1))
                for j in range(2):
                    ob = bank[banks[j]][:].rearrange("p (b d) -> p b d", b=2)
                    nc.vector.tensor_tensor(ob, ob, obias[:].unsqueeze(1).broadcast_to([P, 2, D]),
                                            ALU.add).then_inc(r_add, 1)
                for j in range(2):
                    ob = bank[banks[j]][:].rearrange("p (b d) -> p b d", b=2)
                    dve.wait_ge(r_add, 2 * r + j + 1)
                    nc.vector.tensor_tensor(gate[:, 2 * j:2 * j + 2], ob, gate[:, 2 * j:2 * j + 2],
                                            ALU.mult).then_inc(r_mul, 1)
                for j in range(2):
                    xs = xres[:, bass.ds(g * GB + 2 * j, 2), :]
                    dve.wait_ge(r_mul, 2 * r + j + 1)
                    nc.vector.tensor_tensor(xs, xs, gate[:, 2 * j:2 * j + 2], ALU.add).then_inc(r_x, 1)

            def ada_vectors(chunks):
                for i, c in chunks:
                    for k in range(KD):
                        nc.vector.tensor_scalar(ada_t[:, i, k], bank[7][:, (i * KD + k) * B:(i * KD + k + 1) * B],
                                                ada_bt[:, c * KD + k:c * KD + k + 1], float(i % 2),
                                                ALU.add, ALU.add).then_inc(ada_s, 1)

            def split_part(c, i):
                hs, cs = slice(2 * c, 2 * c + 2), slice(2 * DH * c, 2 * DH * (c + 1))
                lo, raw, hi = ((wqk_lo[:, hs], wqk_raw[:, hs], wqk_hi[:, hs]),
                               (wv_lo[:, :, cs], wv_raw[:, :, cs], wv_hi[:, :, cs]),
                               (wo_lo[:, hs], wo_raw[:, hs], wo_hi[:, hs]))[i]
                if i == 0:
                    lo, raw, hi = (x.rearrange("p h c k d -> p (h c k d)") for x in (lo, raw, hi))
                dve.wait_ge(w_hi1, 3 * c + i + 1)
                nc.vector.tensor_tensor(lo, raw, hi.bitcast(F32), ALU.subtract).then_inc(w_lo1, 1)

            dve.wait_ge(d_x[0], 16)
            norm_stats(0)
            dve.wait_ge(n_bn, 1)
            norm_sums()
            norm_apply(0, 0)
            dve.wait_ge(ada_p, 1)
            dve.wait_ge(d_first, 48)
            ada_vectors(((0, 0), (1, 1)))
            dve.wait_ge(ada_s, 4)
            for k in range(KD):
                norm_ada(0, 0, k, 0, bank[k])
            split_part(0, 0)

            def row_max(n, h):
                dve.wait_ge(a_sp, n + 1)
                nc.vector.tensor_reduce(nmax[:, h % 2], bank[3][:].rearrange("p (b s) -> p b s", b=GB), X, ALU.max,
                                        negate=True).then_inc(a_mx, 1)

            def p_t(n):
                dve.wait_ge(a_tp, n + 1)
                if not isinstance(n, int) or n >= 1:
                    dve.wait_ge(a_pvp, n)
                nc.vector.tensor_copy(pt1[:], bank[4][:]).then_inc(a_pt, 1)

            def row_inverse(n, h):
                dve.wait_ge(a_ex, n + 1)
                nc.vector.reciprocal(rinv[:, h % 2], rsum[:, h % 2]).then_inc(a_ri, 1)

            def o_lo(n, h):
                dve.wait_ge(a_oh, n + 1)
                nc.vector.scalar_tensor_tensor(out=o1_lo[:, h % 2], in0=bank[5][:], scalar=bqkv[:, 2, h:h + 1],
                                               in1=o1_hi[:, h % 2].bitcast(F32), op0=ALU.add,
                                               op1=ALU.subtract).then_inc(a_ol, 1)

            def attention1(g, first):
                for h in range(H):
                    n = g * H + h
                    job = background_norm(g, h, first)
                    if h == 0:
                        cur_rest(g, g)
                    if job and job.part == 0:
                        if first:
                            dve.wait_ge(d_x[job.g], 16)
                        else:
                            dve.wait_ge(r_x, 2 * g)
                    if h >= 1 or not first:
                        row_max(n - 1, (h - 1) % 2)
                    if job and job.part == 0:
                        norm_stats(job.g)
                        dve.wait_ge(n_bn, job.n + 1)
                    if h >= 2 or not first:
                        p_t(n - 2)
                    if job and job.part == 0:
                        norm_sums()
                    if job and job.part >= 2:
                        norm_ada(job.n, job.g, job.part - 2, job.kind, bank[4])
                    if h >= 1 or not first:
                        row_inverse(n - 1, (h - 1) % 2)
                    dve.wait_ge(a_kp, n + 1)
                    if h >= 2 or not first:
                        dve.wait_ge(a_sp, n - 1)
                    nc.vector.tensor_scalar(k1[:, h % 2], bank[1][:], bqkv[:, 1, h:h + 1], None, ALU.add).then_inc(a_k, 1)
                    if h >= 2 or not first:
                        o_lo(n - 2, (h - 2) % H)
                    if h == 1 and not first:
                        dve.wait_ge(a_op, n - 1)
                        residual(g - 1, g - 1, (6, 7), 0)
                    if job and job.part == 1:
                        norm_apply(job.n, job.g)
                    if first and h == 0:
                        split_part(0, 1)
                        split_part(0, 2)
                    if first and h == 1:
                        dve.wait_ge(ada_p, 2)
                        dve.wait_ge(d_small, 16 * 4)
                        ada_vectors(((2, 3), (3, 4)))
                        nc.vector.tensor_tensor(gates[:], bank[6][0:B, :].rearrange("b (c d) -> b c d", c=2), ada_bg[:],
                                                ALU.add).then_inc(ada_s, 1)
                    if first and h % 2 == 0 and h < H - 2:
                        for i in range(3):
                            split_part(h // 2 + 1, i)

            attention1(0, True)
            with dve.Fori(1, NG) as g:
                attention1(g, False)
            n = NG * H
            row_max(n - 1, 1)
            p_t(n - 2)
            row_inverse(n - 1, 1)
            o_lo(n - 2, H - 2)
            p_t(n - 1)
            o_lo(n - 1, H - 1)
            dve.wait_ge(w_hi2, 1)
            nc.vector.tensor_tensor(w1_lo[:], w1_raw[:], w1_hi[:].bitcast(F32), ALU.subtract).then_inc(w_lo2, 1)
            dve.wait_ge(w_hi2, 2)
            nc.vector.tensor_tensor(w2_lo[:], w2_raw[:], w2_hi[:].bitcast(F32), ALU.subtract).then_inc(w_lo2, 1)
            dve.wait_ge(a_op, n)
            residual(NG - 1, NG - 1, (6, 7), 0)
            dve.wait_ge(r_x, 2 * NG)
            norm_stats(NG - 1)
            dve.wait_ge(n_bn, 2 * NG)
            norm_sums()
            norm_apply(2 * NG - 1, NG - 1)
            for k in range(KD):
                norm_ada(2 * NG - 1, NG - 1, k, 1, bank[4])

            def split3(c):
                for i, (lo, hi, raw, at, w) in enumerate(((wkv_lo, wkv_hi, wkv_raw, c * 256, 256),
                                                          (wq_lo, wq_hi, wq_raw, c * 512, 512))):
                    dve.wait_ge(w_hi3, 3 * c + i + 1)
                    nc.vector.tensor_tensor(lo[:, :, bass.ds(at, w)], raw[:, :, bass.ds(at, w)],
                                            hi[:, :, bass.ds(at, w)].bitcast(F32), ALU.subtract).then_inc(w_lo3, 1)
                dve.wait_ge(w_hi3, 3 * c + 3)
                nc.vector.tensor_tensor(wo2_lo[:, bass.ds(c * 4, 4)], wo2_raw[:, bass.ds(c * 4, 4)],
                                        wo2_hi[:, bass.ds(c * 4, 4)].bitcast(F32), ALU.subtract).then_inc(w_lo3, 1)

            def ffn1(g, first):
                for f in range(NF):
                    m = g * NF + f
                    if f == 4 and not first:
                        split3(g - 1)
                    if f == 0:
                        cur_rest(NG + g, g)
                        if first:
                            dve.wait_ge(d_b2, 16)
                    if f == 2 and not first:
                        dve.wait_ge(f_dp, m - 2)
                        residual(NG + g - 1, g - 1, (6, 7), 1)
                    if f == 3 and not first:
                        dve.wait_ge(r_x, 2 * (NG + g))
                    if f == 4 and not first:
                        dve.wait_ge(n_bn, 2 * NG + g)
                    if f == 5 and not first:
                        norm_apply_rms(2 * NG + g - 1, g - 1)
                    if f == 7 and not first:
                        for k in range(KD):
                            norm_weight(2 * NG + g - 1, g - 1, k, 0, bank[2 + k])
                    dve.wait_ge(f_h, m + 1)
                    if f >= 2 or not first:
                        dve.wait_ge(f_dp, m - 1)
                    nc.vector.tensor_tensor(h_lo[:, f % 2], hf[:, f % 2], h_hi[:, f % 2].bitcast(F32),
                                            ALU.subtract).then_inc(f_l, 1)
                    if f == 3 and not first:
                        norm_stats(g - 1)
                    if f == 4 and not first:
                        norm_sums()

            dve.wait_ge(d_rope, 32)
            for i in range(4):
                nc.vector.scalar_tensor_tensor(out=rope[:, i], in0=rope[:, i], scalar=SCALE if i < 2 else 1.0,
                                               in1=cos_sin[:, i % 2], op0=ALU.mult, op1=ALU.mult).then_inc(g_tab, 1)
            dve.wait_ge(g_mask, 2)
            nc.vector.tensor_copy(mask[:].rearrange("p (j s) -> p j s", j=REP),
                                  mask_f[:].unsqueeze(1).broadcast_to([P, REP, T])).then_inc(g_tab, 1)
            nc.vector.tensor_copy(ident_b[:], ident[:]).then_inc(g_tab, 1)
            ffn1(0, True)
            with dve.Fori(1, NG) as g:
                ffn1(g, False)
            split3(NG - 1)
            dve.wait_ge(f_dp, NG * NF)
            residual(2 * NG - 1, NG - 1, (6, 7), 1)
            dve.wait_ge(r_x, 4 * NG)
            norm_stats(NG - 1)
            dve.wait_ge(n_bn, 3 * NG)
            norm_sums()
            norm_apply_rms(3 * NG - 1, NG - 1)
            for k in range(KD):
                norm_weight(3 * NG - 1, NG - 1, k, 0, bank[2 + k])
            dve.wait_ge(g_tab, 6)

            def rotate(out_cos, out_sin, src, table, cos_free, sin_free, done):
                heads = src.rearrange("p (h d) -> p h d", d=DH)
                for sem_, value in cos_free:
                    dve.wait_ge(sem_, value)
                nc.vector.tensor_tensor(out_cos.rearrange("p (h d) -> p h d", d=DH), heads,
                                        rope[:, table].unsqueeze(1).broadcast_to([P, 4, DH]), ALU.mult)
                for sem_, value in sin_free:
                    dve.wait_ge(sem_, value)
                nc.vector.tensor_tensor(out_sin.rearrange("p (h c d) -> p h c d", c=2, d=DH // 2),
                                        src.rearrange("p (h c d) -> p h c d", c=2, d=DH // 2)[:, :, ::-1, :],
                                        rope[:, table + 1].rearrange("p (c d) -> p c d", c=2).unsqueeze(1)
                                        .broadcast_to([P, 4, 2, DH // 2]), ALU.mult).then_inc(done, 1)

            def step(s):
                n, new_seq, prev = s.n, s.new() and s.kv == 0, 3 * NG + s.g - 1
                if s.u == 0:
                    cur_rest(2 * NG + s.g, s.g)
                if s.kv == 2 and s.had(10):
                    dve.wait_ge(g_op, 4 * (s.seq - 1))
                    xs = xres[:, bass.ds(s.seq - 2, 1), :].rearrange("p a d -> p (a d)")
                    nc.vector.tensor_tensor(xs, xs, bank[7][:, 0:D], ALU.add).then_inc(g_x, 1)
                if s.u == 7 and not s.first:
                    dve.wait_ge(g_x, GB * s.g)
                if s.live(3):
                    dve.wait_ge(g_sp, n - 2)
                    nc.vector.tensor_reduce(nmax[:, (s.u - 3) % 2], bank[3][:].rearrange("p (j s) -> p j s", j=REP), X,
                                            ALU.max, negate=True).then_inc(g_mx, 1)
                    dve.wait_ge(g_rq, n - 2)
                    dve.wait_ge(g_mx, n - 2)
                    nc.vector.tensor_tensor(nb[:, (s.u - 3) % 2], nmax[:, (s.u - 3) % 2], rq[:, (s.u - 3) % 4],
                                            ALU.mult).then_inc(g_nb, 1)
                if s.u == 7 and not s.first:
                    norm_stats(s.g - 1)
                if new_seq:
                    free = [(g_ktp, s.seq)] if s.had(4) else []
                    rotate(kr[:], kb[:], bank[1][:], 2, [(g_kp, s.seq + 1)] + free, free, g_kb)
                if s.u == 7 and not s.first:
                    dve.wait_ge(n_bn, prev + 1)
                if s.new() and s.kv == 1:
                    dve.wait_ge(g_rk, s.seq + 1)
                    dve.wait_ge(g_ka, s.seq + 1)
                    kh = kr[:].rearrange("p (h d) -> p h d", d=DH)
                    nc.vector.tensor_tensor(kh, kh, rk[:].unsqueeze(2).broadcast_to([P, HKV, DH]),
                                            ALU.mult).then_inc(g_kr, 1)
                if s.new():
                    rotate(qr[:, s.u % 2], rb[:], bank[0][:], 0,
                           [(g_qp, n + 1)] + ([(g_qtp, n - 1)] if s.had(2) else []),
                           [(g_qr, n)] if s.had(1) else [], g_qb)
                if s.live(3):
                    dve.wait_ge(g_ex, n - 2)
                    nc.vector.reciprocal(rinv[:, (s.u - 3) % 2], rsum[:, (s.u - 3) % 2]).then_inc(g_ri, 1)
                if s.u == 7 and not s.first:
                    norm_sums()
                if new_seq:
                    dve.wait_ge(g_ksq, s.seq + 1)
                    nc.vector.tensor_reduce(k_ms[:], ksq[:].rearrange("p (h d) -> p h d", d=DH), X,
                                            ALU.add).then_inc(g_ks, 1)
                if s.new():
                    dve.wait_ge(g_sq, n + 1)
                    if s.had(2):
                        dve.wait_ge(g_rq, n - 1)
                    nc.vector.tensor_reduce(q_ms[:, s.u % 2], sq[:].rearrange("p (h d) -> p h d", d=DH), X,
                                            ALU.add).then_inc(g_ss, 1)
                if s.live(5):
                    dve.wait_ge(g_oh, n - 4)
                    nc.vector.tensor_tensor(o2_lo[:], bank[6][:], o2_hi[:].bitcast(F32), ALU.subtract).then_inc(g_ol, 1)
                if s.live(4):
                    dve.wait_ge(g_ph, n - 3)
                    nc.vector.tensor_tensor(pt_lo[:], bank[5][:], pt_hi[:].bitcast(F32), ALU.subtract).then_inc(g_pl, 1)
                if new_seq:
                    dve.wait_ge(g_vh, s.seq + 1)
                    nc.vector.tensor_tensor(v_lo[:, s.b % 2], bank[2][:], v_hi[:, s.b % 2].bitcast(F32),
                                            ALU.subtract).then_inc(g_vl, 1)
                if s.u == 9 and not s.first:
                    norm_apply_rms(prev, s.g - 1)
                if s.u == 10 and not s.first:
                    for k in range(KD):
                        norm_weight(prev, s.g - 1, k, 1, bank[1 + k])

            attention2(dve, step)
            dve.wait_ge(g_x, B)
            norm_stats(NG - 1)
            dve.wait_ge(n_bn, 4 * NG)
            norm_sums()
            norm_apply_rms(4 * NG - 1, NG - 1)
            for k in range(KD):
                norm_weight(4 * NG - 1, NG - 1, k, 1, bank[1 + k])

            for i, (lo, raw, hi) in enumerate(((rw_lo, rw_raw, rw_hi), (wg_lo, wg_raw, wg_hi),
                                               (wu_lo, wu_raw, wu_hi), (wd_lo, wd_raw, wd_hi))):
                dve.wait_ge(w_hi4, i + 2)
                nc.vector.tensor_tensor(lo[:], raw[:], hi[:].bitcast(F32), ALU.subtract).then_inc(w_lo4, 1)

            def routing(g, first):
                done = [0]

                def after():
                    dve.wait_ge(t_v, g * RV + done[0])

                def inc(i):
                    done[0] += 1
                    i.then_inc(t_v, 1)

                lg = bank[5][:, 0:GB * E].rearrange("p (b e) -> p b e", b=GB)
                wide = [P, GB, E]
                dve.wait_ge(t_lp, g + 1)
                inc(nc.vector.tensor_reduce(r4[:, 0], lg, X, ALU.max))
                after()
                inc(nc.vector.tensor_tensor(probs[:], lg, r4[:, 0].unsqueeze(2).broadcast_to(wide), ALU.subtract))
                dve.wait_ge(t_ex, g + 1)
                inc(nc.vector.tensor_reduce(r4[:, 1], probs[:], X, ALU.add))
                after()
                inc(nc.vector.reciprocal(r4[:, 2], r4[:, 1]))
                after()
                inc(nc.vector.tensor_tensor(probs[:], probs[:], r4[:, 2].unsqueeze(2).broadcast_to(wide), ALU.mult))
                after()
                pj = probs[:].unsqueeze(2).broadcast_to([P, GB, E, E])
                pe_ = probs[:].unsqueeze(3).broadcast_to([P, GB, E, E])
                nc.vector.tensor_tensor(gt[:], pj, pe_, ALU.is_gt)
                inc(nc.vector.tensor_tensor(eq[:], pj, pe_, ALU.is_equal))
                after()
                inc(nc.vector.tensor_tensor(eq[:].rearrange("p b e j -> p b (e j)"), eq[:].rearrange("p b e j -> p b (e j)"),
                                            before[:].rearrange("p e j -> p (e j)").unsqueeze(1)
                                            .broadcast_to([P, GB, E * E]), ALU.mult))
                after()
                inc(nc.vector.tensor_tensor(gt[:], gt[:], eq[:], ALU.add))
                after()
                inc(nc.vector.tensor_reduce(pick[:], gt[:], X, ALU.add))
                after()
                inc(nc.vector.scalar_tensor_tensor(out=comb[:], in0=pick[:], scalar=2.0, in1=probs[:],
                                                   op0=ALU.is_lt, op1=ALU.mult))
                after()
                inc(nc.vector.tensor_reduce(r4[:, 3], comb[:], X, ALU.add))
                after()
                nc.vector.tensor_scalar(r4[:, 0], r4[:, 3], 1e-9, None, ALU.add).then_inc(t_v, 1)
                done[0] += 1
                after()
                nc.vector.reciprocal(r4[:, 1], r4[:, 0]).then_inc(t_v, 1)
                done[0] += 1
                after()
                assert done[0] == RV
                nc.vector.tensor_tensor(comb[:], comb[:], r4[:, 1].unsqueeze(2).broadcast_to(wide),
                                        ALU.mult).then_inc(t_c, 1)

            def experts(g, first):
                for i in range(NR):
                    n, back = g * NR + i, 1 if i == 0 else 2
                    if i == 0:
                        cur_rest(3 * NG + g, g)
                        routing(g, first)
                    dve.wait_ge(m_sg, n + 1)
                    dve.wait_ge(m_up, n + 1)
                    nc.vector.tensor_tensor(sg[:, i % 2], sg[:, i % 2], bank[2 + i % 2][:], ALU.mult).then_inc(m_su, 1)
                    if i == 0:
                        dve.wait_ge(t_h, g + 1)
                        nc.vector.tensor_tensor(ct_lo[:], bank[5][0:E, :], ct_hi[:].bitcast(F32),
                                                ALU.subtract).then_inc(t_l, 1)
                    if i == 2 and not first:
                        result(g - 1)
                    dve.wait_ge(m_cp, n + 1)
                    dve.wait_ge(m_su, n + 1)
                    if i >= 2 or not first:
                        dve.wait_ge(m_l, n - back + 1)
                    nc.vector.tensor_tensor(em[:, i % 2], sg[:, i % 2], bank[4][:], ALU.mult).then_inc(m_em, 1)
                    dve.wait_ge(m_h, n + 1)
                    nc.vector.tensor_tensor(e_lo[:, i % 2], em[:, i % 2], e_hi[:, i % 2].bitcast(F32),
                                            ALU.subtract).then_inc(m_l, 1)

            def result(g):
                dve.wait_ge(m_dp, NR * (g + 1))
                if not isinstance(g, int) or g >= 1:
                    dve.wait_ge(d_out, 16 * g)
                for j in range(2):
                    nc.vector.tensor_tensor(y[:, 2 * j:2 * j + 2], bank[6 + j][:].rearrange("p (b d) -> p b d", b=2),
                                            xres[:, bass.ds(g * GB + 2 * j, 2), :], ALU.add).then_inc(m_y, 1)
                dve.wait_ge(d_xin, 16 * (g + 1))
                dve.wait_ge(m_y, 4 * g + 2)
                for j in range(2):
                    nc.vector.tensor_tensor(y[:, 2 * j:2 * j + 2], y[:, 2 * j:2 * j + 2], x0[:, 2 * j:2 * j + 2],
                                            ALU.add).then_inc(m_y, 1)

            experts(0, True)
            with dve.Fori(1, NG) as g:
                experts(g, False)
            result(NG - 1)

        @block.tensor
        def _(pe):
            def norm_transposes(n, k, dst):
                for b in range(GB):
                    last = pe.transpose(dst[:, b * T:(b + 1) * T], xn[:, b, k * P:(k + 1) * P], ident[:])
                last.then_inc(n_tp, 1)

            def ada_columns(chunks):
                for i, c in chunks:
                    for k in range(KD):
                        for j in range(KD):
                            last = pe.matmul(bank[7][:, (i * KD + k) * B:(i * KD + k + 1) * B],
                                             ada_w[:, j, c * D + k * P:c * D + (k + 1) * P], cond_t[:, j],
                                             start=(j == 0), stop=(j == KD - 1))
                return last

            pe.wait_ge(d_first, 48)
            pe.wait_ge(d_ada1, 16)
            ada_columns(((0, 0), (1, 1))).then_inc(ada_p, 1)
            pe.wait_ge(consts, 4)
            pe.wait_ge(n_xn, 1)
            for k in range(KD):
                norm_transposes(0, k, bank[k])

            def project(dst, h, c):
                for k in range(KD):
                    for i, (l, r) in enumerate(split_products(wqk_hi[:, h, c, k], wqk_lo[:, h, c, k],
                                                              cur_hi[:, k], cur_lo[:, k])):
                        last = pe.matmul(dst, l, r, start=(k == 0 and i == 0), stop=(k == KD - 1 and i == 2))
                return last

            def scores(n, h):
                pe.wait_ge(a_k, n + 1)
                pe.wait_ge(a_q, n + 1)
                if not isinstance(n, int) or n >= 1:
                    pe.wait_ge(a_ex, n)
                for b in range(GB):
                    bs = slice(b * T, (b + 1) * T)
                    last = pe.matmul(bank[3][:, bs], q1[:, h % 2, bs], k1[:, h % 2, bs], start=True, stop=True)
                last.then_inc(a_sp, 1)

            def p_transposes(n, h):
                pe.wait_ge(a_pn, n + 1)
                if not isinstance(n, int) or n >= 1:
                    pe.wait_ge(a_pt, n)
                for b in range(GB):
                    last = pe.transpose(bank[4][:, b * T:(b + 1) * T], p1[:, h % 2, b], ident[:])
                last.then_inc(a_tp, 1)

            def values_product(n, h):
                pe.wait_ge(a_pt, n + 1)
                pe.wait_ge(a_v, n - h % 2 + 2)
                if not isinstance(n, int) or n >= 1:
                    pe.wait_ge(a_ol, n)
                for b in range(GB):
                    bs = slice(b * T, (b + 1) * T)
                    last = pe.matmul(bank[5][:, bs], v1[:, h // 2 % 2, b, h % 2 * DH:h % 2 * DH + DH], pt1[:, bs],
                                     start=True, stop=True)
                last.then_inc(a_pvp, 1)

            def down(banks, lhs_hi, lhs_lo, rhs_hi, rhs_lo, first, last_one):
                for b in range(GB):
                    bs = slice(b * T, (b + 1) * T)
                    for i, (l, r) in enumerate(split_products(lhs_hi[:, bs], lhs_lo[:, bs], rhs_hi, rhs_lo)):
                        last = pe.matmul(bank[banks[b // 2]][:, b % 2 * D:b % 2 * D + D], l, r,
                                         start=(first and b % 2 == 0 and i == 0), stop=(last_one and i == 2),
                                         skip_group_check=True)
                return last

            def out_product(n, h):
                pe.wait_ge(a_ol, n + 1)
                down((6, 7), o1_hi[:, h % 2], o1_lo[:, h % 2], wo_hi[:, h], wo_lo[:, h],
                     h == 0, h == H - 1).then_inc(a_op, 1)

            def attention1(g, first):
                for h in range(H):
                    n = g * H + h
                    job = background_norm(g, h, first)
                    past = background_norm(g, h - 1, first)
                    if h == 0:
                        if not first:
                            p_transposes(n - 2, 0)
                        pe.wait_ge(c_lo, g + 1)
                    if first and h % 2 == 0:
                        pe.wait_ge(w_lo1, 3 * (h // 2) + 1)
                    if h >= 1 or not first:
                        pe.wait_ge(a_q, n)
                    project(bank[0][:], h, 0).then_inc(a_qp, 1)
                    if past and past.part >= 2:
                        pe.wait_ge(n_ev, 2 * past.n + past.part - 1)
                    if h >= 1 and (h >= 2 or not first):
                        p_transposes(n - 2, h % 2)
                    if job and job.part >= 2:
                        if job.part == 2:
                            pe.wait_ge(n_xn, job.n + 1)
                        pe.wait_ge(a_pt, n - 1)
                        norm_transposes(job.n, job.part - 2, bank[4])
                    if h >= 1 or not first:
                        pe.wait_ge(a_k, n)
                    project(bank[1][:], h, 1).then_inc(a_kp, 1)
                    if h >= 2 or not first:
                        values_product(n - 2, (h - 2) % H)
                    if first and h % 2 == 0:
                        pe.wait_ge(w_lo1, 3 * (h // 2) + 2)
                    if h >= 1 or not first:
                        pe.wait_ge(a_v, n)
                    ps = slice(h // 2 * 2 * DH, (h // 2 + 1) * 2 * DH)
                    for j in range(2):
                        bs = slice((h % 2 * 2 + j) * T, (h % 2 * 2 + j + 1) * T)
                        for k in range(KD):
                            for i, (l, r) in enumerate(split_products(cur_hi[:, k, bs], cur_lo[:, k, bs],
                                                                      wv_hi[:, k, ps], wv_lo[:, k, ps])):
                                last = pe.matmul(bank[2][:, j * 2 * DH:(j + 1) * 2 * DH], l, r,
                                                 start=(k == 0 and i == 0), stop=(k == KD - 1 and i == 2))
                    last.then_inc(a_vp, 1)
                    scores(n, h)
                    if first and h == 1:
                        pe.wait_ge(d_ada2, 16)
                        ada_columns(((2, 3), (3, 4)))
                        for i, c in enumerate((2, 5)):
                            for j in range(KD):
                                last = pe.matmul(bank[6][0:B, i * D:(i + 1) * D], cond_t[:, j],
                                                 ada_w[:, j, c * D:(c + 1) * D], start=(j == 0), stop=(j == KD - 1))
                        last.then_inc(ada_p, 1)
                    if h >= 2 or not first:
                        if first and h % 2 == 0:
                            pe.wait_ge(w_lo1, 3 * (h // 2))
                        if first and h == 2:
                            pe.wait_ge(ada_s, 9)
                        if h == 2 and not first:
                            pe.wait_ge(r_mul, 2 * g)
                        out_product(n - 2, (h - 2) % H)

            attention1(0, True)
            with pe.Fori(1, NG) as g:
                attention1(g, False)
            n = NG * H
            for h in (H - 2, H - 1):
                p_transposes(n - H + h, h)
                values_product(n - H + h, h)
                out_product(n - H + h, h)
            pe.wait_ge(n_xn, 2 * NG)
            pe.wait_ge(a_pt, n)
            for k in range(KD):
                norm_transposes(2 * NG - 1, k, bank[4])
                pe.wait_ge(n_ev, 2 * (2 * NG - 1) + k + 1)

            def ffn_down(m, f):
                pe.wait_ge(f_l, m + 1)
                down((6, 7), h_hi[:, f % 2], h_lo[:, f % 2], w2_hi[:, f], w2_lo[:, f], f == 0, f == NF - 1).then_inc(f_dp, 1)

            def ffn1(g, first):
                for f in range(NF):
                    m = g * NF + f
                    if f == 0:
                        pe.wait_ge(c_lo, NG + g + 1)
                        if first:
                            pe.wait_ge(w_lo2, 2)
                    if f >= 2 or not first:
                        pe.wait_ge(f_g, m - 1)
                    for k in range(KD):
                        for i, (l, r) in enumerate(split_products(w1_hi[:, f, k], w1_lo[:, f, k], cur_hi[:, k], cur_lo[:, k])):
                            last = pe.matmul(bank[f % 2][:], l, r, start=(k == 0 and i == 0), stop=(k == KD - 1 and i == 2))
                    last.then_inc(f_up, 1)
                    if f == 2:
                        pe.wait_ge(r_mul, 2 * (NG + g))
                    if f >= 2 or not first:
                        ffn_down(m - 2, (f - 2) % NF)
                    if f == 6 and not first:
                        pe.wait_ge(n_xn, 2 * NG + g)
                        pe.wait_ge(n_ev, 2 * (2 * NG + g - 1))
                        for k in range(KD):
                            norm_transposes(2 * NG + g - 1, k, bank[2 + k])

            ffn1(0, True)
            with pe.Fori(1, NG) as g:
                ffn1(g, False)
            ffn_down(NG * NF - 2, NF - 2)
            ffn_down(NG * NF - 1, NF - 1)
            pe.wait_ge(n_xn, 3 * NG)
            pe.wait_ge(n_ev, 2 * (3 * NG - 1))
            for k in range(KD):
                norm_transposes(3 * NG - 1, k, bank[2 + k])

            def token_product(dst, seq, w_hi, w_lo, cols):
                bs = slice(seq * T, (seq + 1) * T)
                for k in range(KD):
                    for i, (l, r) in enumerate(split_products(cur_hi[:, k, bs], cur_lo[:, k, bs],
                                                              w_hi[:, k, cols], w_lo[:, k, cols])):
                        last = pe.matmul(dst, l, r, start=(k == 0 and i == 0), stop=(k == KD - 1 and i == 2))
                return last

            def step(s):
                n, new_seq = s.n, s.new() and s.kv == 0
                if s.u == 0:
                    pe.wait_ge(c_lo, 2 * NG + s.g + 1)
                    if s.first:
                        pe.wait_ge(w_lo3, 12)
                        pe.wait_ge(r_mul, 2 * 2 * NG)
                        pe.wait_ge(n_ev, 2 * 3 * NG)
                if new_seq:
                    if s.had(4):
                        pe.wait_ge(g_kt, s.seq)
                    if s.u == 12 and not s.first:
                        pe.wait_ge(n_ev, 2 * (3 * NG + s.g))
                    token_product(bank[1][:], s.b, wkv_hi, wkv_lo, slice(0, HKV * DH)).then_inc(g_kp, 1)
                if s.new():
                    if s.had(1):
                        pe.wait_ge(g_qb, n)
                        pe.wait_ge(g_sq, n)
                    token_product(bank[0][:], s.b, wq_hi, wq_lo,
                                  slice(s.kv * REP * DH, (s.kv + 1) * REP * DH)).then_inc(g_qp, 1)
                if s.live(6):
                    kv = (s.u - 6) % HKV
                    pe.wait_ge(g_ol, n - 5)
                    if kv == 0 and s.had(10):
                        pe.wait_ge(g_x, s.seq - 1)
                    for j in range(REP):
                        js = slice(j * T, (j + 1) * T)
                        for i, (l, r) in enumerate(split_products(o2_hi[:, js], o2_lo[:, js],
                                                                  wo2_hi[:, kv * REP + j], wo2_lo[:, kv * REP + j])):
                            last = pe.matmul(bank[7][:, 0:D], l, r, start=(kv == 0 and j == 0 and i == 0),
                                             stop=(kv == HKV - 1 and j == REP - 1 and i == 2))
                    last.then_inc(g_op, 1)
                if new_seq:
                    if s.had(4):
                        pe.wait_ge(g_vl, s.seq)
                    token_product(bank[2][:], s.b, wkv_hi, wkv_lo, slice(HKV * DH, 2 * HKV * DH)).then_inc(g_vp, 1)
                if s.live(5):
                    kv, slot = (s.u - 5) % HKV, (s.u - 5) // HKV % 2
                    pe.wait_ge(g_pl, n - 4)
                    pe.wait_ge(g_vl, s.g * GB + (s.u - 5) // HKV + 1)
                    if s.had(6):
                        pe.wait_ge(g_ol, n - 5)
                    ks = slice(kv * DH, (kv + 1) * DH)
                    for i, (l, r) in enumerate(split_products(v_hi[:, slot, ks], v_lo[:, slot, ks], pt_hi[:], pt_lo[:])):
                        last = pe.matmul(bank[6][:], l, r, start=(i == 0), stop=(i == 2))
                    last.then_inc(g_pvp, 1)
                if s.live(1):
                    pe.wait_ge(g_qr, n)
                    if s.had(2):
                        pe.wait_ge(g_qt, n - 1)
                    for j in range(REP):
                        last = pe.transpose(bank[4][:, j * T:(j + 1) * T],
                                            qr[:, (s.u - 1) % 2, j * DH:(j + 1) * DH], ident[:])
                    last.then_inc(g_qtp, 1)
                if s.live(4):
                    pe.wait_ge(g_pn, n - 3)
                    if s.had(5):
                        pe.wait_ge(g_pl, n - 4)
                    for j in range(REP):
                        last = pe.transpose(bank[5][:, j * T:(j + 1) * T], p2[:, (s.u - 4) % 2, j], ident[:])
                    last.then_inc(g_tp, 1)
                if s.new() and s.kv == 1:
                    pe.wait_ge(g_kr, s.seq + 1)
                    for j in range(HKV):
                        last = pe.transpose(bank[1][:, j * T:(j + 1) * T], kr[:, j * DH:(j + 1) * DH], ident[:])
                    last.then_inc(g_ktp, 1)
                if s.u == 10 and not s.first:
                    pe.wait_ge(n_xn, 3 * NG + s.g)
                    pe.wait_ge(g_kt, s.g * GB + 3)
                    pe.wait_ge(g_vl, s.g * GB + 3)
                    for k in range(KD):
                        norm_transposes(3 * NG + s.g - 1, k, bank[1 + k])
                if s.live(2):
                    kv, slot = (s.u - 2) % HKV, (s.u - 2) // HKV % 2
                    pe.wait_ge(g_qt, n - 1)
                    pe.wait_ge(g_kt, s.g * GB + (s.u - 2) // HKV + 1)
                    if s.had(3):
                        pe.wait_ge(g_ex, n - 2)
                    pe.matmul(bank[3][:], ident_b[:], mask[:], start=True, stop=False, skip_group_check=True)
                    for j in range(REP):
                        js = slice(j * T, (j + 1) * T)
                        last = pe.matmul(bank[3][:, js], q_t[:, s.u % 2, js], k_t[:, slot, kv * T:(kv + 1) * T],
                                         start=False, stop=(j == REP - 1), skip_group_check=True)
                    last.then_inc(g_sp, 1)

            attention2(pe, step)
            pe.wait_ge(n_xn, 4 * NG)
            for k in range(KD):
                norm_transposes(4 * NG - 1, k, bank[1 + k])

            def expert_down(n, i):
                pe.wait_ge(m_l, n + 1)
                down((6, 7), e_hi[:, i % 2], e_lo[:, i % 2], wd_hi[:, i], wd_lo[:, i], i == 0, i == NR - 1).then_inc(m_dp, 1)

            def experts(g, first):
                for i in range(NR):
                    n, back = g * NR + i, 1 if i == 0 else 2
                    if i == 0:
                        pe.wait_ge(c_lo, 3 * NG + g + 1)
                        if first:
                            pe.wait_ge(w_lo4, 1)
                            pe.wait_ge(n_ev, 2 * 4 * NG)
                            pe.wait_ge(g_x, B)
                        else:
                            pe.wait_ge(t_l, g)
                        for b in range(GB):
                            bs = slice(b * T, (b + 1) * T)
                            for k in range(KD):
                                for j, (l, r) in enumerate(split_products(cur_hi[:, k, bs], cur_lo[:, k, bs],
                                                                          rw_hi[:, k], rw_lo[:, k])):
                                    last = pe.matmul(bank[5][:, b * E:(b + 1) * E], l, r,
                                                     start=(k == 0 and j == 0), stop=(k == KD - 1 and j == 2))
                        last.then_inc(t_lp, 1)
                        if first:
                            pe.wait_ge(w_lo4, 3)
                    for dst, w_hi, w_lo, done, read in ((bank[i % 2], wg_hi, wg_lo, m_gp, m_sg),
                                                        (bank[2 + i % 2], wu_hi, wu_lo, m_up, m_su)):
                        if i >= 2 or not first:
                            pe.wait_ge(read, n - back + 1)
                        for k in range(KD):
                            for j, (l, r) in enumerate(split_products(w_hi[:, i, k], w_lo[:, i, k], cur_hi[:, k], cur_lo[:, k])):
                                last = pe.matmul(dst[:], l, r, start=(k == 0 and j == 0), stop=(k == KD - 1 and j == 2))
                        last.then_inc(done, 1)
                    if i == 2 and first:
                        pe.wait_ge(w_lo4, 4)
                    if i == 2 and not first:
                        pe.wait_ge(m_y, 4 * g - 2)
                    if i >= 2 or not first:
                        expert_down(n - 2 if i >= 2 else n - 2, (i - 2) % NR)
                    if i == 0:
                        pe.wait_ge(t_c, g + 1)
                        for b in range(GB):
                            last = pe.transpose(bank[5][0:E, b * T:(b + 1) * T], comb[:, b, :], ident[:])
                        last.then_inc(t_ctp, 1)
                        pe.wait_ge(t_l, g + 1)
                    if i >= 1 or not first:
                        pe.wait_ge(m_em, n)
                    for j, c in enumerate((ct_hi, ct_lo)):
                        last = pe.matmul(bank[4][:], sel[:, i], c[:], start=(j == 0), stop=(j == 1))
                    last.then_inc(m_cp, 1)

            experts(0, True)
            with pe.Fori(1, NG) as g:
                experts(g, False)
            expert_down(NG * NR - 2, NR - 2)
            expert_down(NG * NR - 1, NR - 1)


def layout(a):
    import numpy as np
    freqs = (1.0 / np.float32(1000000.0) ** (np.arange(0, DH, 2, dtype=np.float32) / np.float32(DH))).astype(np.float32)
    angle = np.outer(np.arange(T, dtype=np.float32), freqs).astype(np.float32)
    cos, sin = np.cos(angle), np.sin(angle)
    cos_sin = np.stack([np.concatenate([cos, cos], 1), np.concatenate([-sin, sin], 1)], 1).astype(np.float32)
    qw, kw = a["L0_ffn_q_norm_w"], a["L0_ffn_k_norm_w"]
    rows = lambda w: w.T.reshape(KD, P, -1).transpose(1, 0, 2)
    tiles = lambda w: w.reshape(E * I, D).T.reshape(KD, P, NR, P).transpose(1, 2, 0, 3)
    qkv = a["L0_cond_qkv_w"].reshape(KD, P, 3, H, DH)
    return {
        "x": a["x"],
        "cond_t": a["cond_2048"].T.reshape(KD, P, B).transpose(1, 0, 2),
        "ada_w": a["L0_cond_ada_w"].reshape(KD, P, 6 * D).transpose(1, 0, 2),
        "ada_bt": a["L0_cond_ada_b"].reshape(12, P).T,
        "ada_bg": np.broadcast_to(a["L0_cond_ada_b"].reshape(6, D)[[2, 5]], (B, 2, D)),
        "wqk": qkv[:, :, 0:2].transpose(1, 3, 2, 0, 4),
        "wv": qkv[:, :, 2].reshape(KD, P, H * DH).transpose(1, 0, 2),
        "wo": a["L0_cond_out_w"].reshape(H, DH, D).transpose(1, 0, 2),
        "bqkv": a["L0_cond_qkv_b"].reshape(3, H, DH).transpose(2, 0, 1),
        "out_b": a["L0_cond_out_b"],
        "w1": a["L0_cond_ffn_w1"].reshape(KD, P, NF, P).transpose(1, 2, 0, 3),
        "b1": a["L0_cond_ffn_b1"].reshape(NF, P).T,
        "w2": a["L0_cond_ffn_w2"].reshape(NF, P, D).transpose(1, 0, 2),
        "b2": a["L0_cond_ffn_b2"],
        "wq": rows(a["L0_ffn_q_w"]),
        "wkv": rows(np.concatenate([a["L0_ffn_k_w"], a["L0_ffn_v_w"]], 0)),
        "wo2": a["L0_ffn_o_w"].T.reshape(H, DH, D).transpose(1, 0, 2),
        "qk_norm": np.stack([qw, np.roll(qw, DH // 2), kw, np.roll(kw, DH // 2)]),
        "cos_sin": cos_sin,
        "rw": rows(a["L0_ffn_gate_w"]),
        "wg": tiles(a["L0_ffn_wg"]),
        "wu": tiles(a["L0_ffn_wu"]),
        "wd": a["L0_ffn_wd"].transpose(0, 2, 1).reshape(NR, P, D).transpose(1, 0, 2),
        "norm_w": np.stack([a["L0_ffn_attn_norm_w"], a["L0_ffn_ffn_norm_w"]]).reshape(2, KD, P).transpose(2, 0, 1),
    }


def kernel(**inputs):
    import numpy as np
    import concourse.bacc as bacc
    from concourse.bass_utils import run_bass_kernel_spmd

    nc = bacc.Bacc("TRN2", target_bir_lowering=False, num_devices=1)
    arrays, args = {}, {}
    for name, a in layout({k: np.asarray(v) for k, v in inputs.items()}).items():
        a = np.ascontiguousarray(a)
        arrays[f"in_{name}"] = a
        args[name] = nc.dram_tensor(f"in_{name}", a.shape, mybir.dt.from_np(a.dtype), kind="ExternalInput").ap()
    out = nc.dram_tensor("out_y", (B, T, D), F32, kind="ExternalOutput").ap()
    program(nc, args, out)
    r = run_bass_kernel_spmd(nc, [arrays], core_ids=[0])
    return r.results[0]["out_y"]
```

```python
import concourse.bass as bass
from concourse import mybir
from contextlib import ExitStack

F32 = mybir.dt.float32
F32R = mybir.dt.float32r
BF16 = mybir.dt.bfloat16
ALU = mybir.AluOpType
ACT = mybir.ActivationFunctionType
X = mybir.AxisListType.X

B, T, D = 16, 128, 256
P = 128
KD = D // P
GB = 4
NG = B // GB
GT = GB * T
H, DH = 16, 128
HKV = 4
REP = H // HKV
F1 = 1024
NF = F1 // P
E, I = 8, 176
NR = E * I // P
SCALE = DH ** -0.5
EPS = 1e-6
KB = 1024


def program(nc, ins, out):
    ctx = ExitStack()
    with ctx:
        place = {}
        cursor = [16512]

        def sb(name, shape, dtype=F32, at=None):
            size = 4 if dtype in (F32, F32R) else 2
            for n in shape[1:]:
                size *= n
            size = -(-size // 32) * 32
            if at is None:
                at = cursor[0]
                cursor[0] += size
            place[name] = (at, at + size)
            return nc.alloc_sbuf_tensor_at(name, shape, dtype, offset=at)

        def sem(name):
            return ctx.enter_context(nc.semaphore(name))

        xres = sb("xres", [P, B, D])
        act_t = sb("act_t", [P, KD, B * T])
        cur_hi = sb("cur_hi", [P, KD, GT], F32R)
        cur_lo = sb("cur_lo", [P, KD, GT], F32R)
        gate = sb("gate", [P, GB, D])
        xn = sb("xn", [P, GB, D], at=place["gate"][0])
        obias = sb("obias", [P, D])
        ident = sb("ident", [P, P])
        ada_t = sb("ada_t", [P, 4, KD, B])
        ada_bt = sb("ada_bt", [P, 12])
        bqkv = sb("bqkv", [P, 3, H])
        b1 = sb("b1", [P, NF])
        norm_w = sb("norm_w", [P, 2, KD])
        bn = sb("bn", [P, GB, 6])
        mv = sb("mv", [P, GB, 2])
        vare = sb("vare", [P, GB])
        rstd = sb("rstd", [P, GB])
        mean2 = sb("mean2", [P, GB])
        neg_half = sb("neg_half", [P, 8])
        eps = sb("eps", [P, 8])
        nmax = sb("nmax", [P, 2, GB])
        rsum = sb("rsum", [P, 2, GB])
        rinv = sb("rinv", [P, 2, GB])
        W = cursor[0]
        WORK = W + 128 * KB

        wqk_hi = sb("wqk_hi", [P, H, 2, KD, DH], F32R, at=W)
        wqk_lo = sb("wqk_lo", [P, H, 2, KD, DH], F32R, at=W + 32 * KB)
        wqk_raw = sb("wqk_raw", [P, H, 2, KD, DH], at=W + 32 * KB)
        wv_hi = sb("wv_hi", [P, KD, H * DH], F32R, at=W + 64 * KB)
        wv_lo = sb("wv_lo", [P, KD, H * DH], F32R, at=W + 80 * KB)
        wv_raw = sb("wv_raw", [P, KD, H * DH], at=W + 80 * KB)
        wo_hi = sb("wo_hi", [P, H, D], F32R, at=W + 96 * KB)
        wo_lo = sb("wo_lo", [P, H, D], F32R, at=W + 112 * KB)
        wo_raw = sb("wo_raw", [P, H, D], at=W + 112 * KB)
        q1 = sb("q1", [P, 2, GT], at=WORK)
        k1 = sb("k1", [P, 2, GT], at=WORK + 4 * KB)
        v1 = sb("v1", [P, 2, GB, 2 * DH], at=WORK + 8 * KB)
        p1 = sb("p1", [P, 2, GB, T], at=WORK + 16 * KB)
        pt1 = sb("pt1", [P, GT], at=WORK + 20 * KB)
        o1_hi = sb("o1_hi", [P, 2, GT], F32R, at=WORK + 22 * KB)
        o1_lo = sb("o1_lo", [P, 2, GT], F32R, at=WORK + 26 * KB)
        ada_w = sb("ada_w", [P, KD, 6 * D], at=W + 16 * KB)
        cond_t = sb("cond_t", [P, KD, B], at=WORK + 30 * KB)
        gb1 = sb("gb1", [P, D], at=WORK + 30 * KB + 512)
        ada_bg = sb("ada_bg", [B, 2, D], at=W + 28 * KB)
        gates = sb("gates", [B, 2, D], at=W + 30 * KB)
        w1_hi = sb("w1_hi", [P, NF, KD, P], F32R, at=W + 16 * KB)
        w1_lo = sb("w1_lo", [P, NF, KD, P], F32R, at=W)
        w1_raw = sb("w1_raw", [P, NF, KD, P], at=W)
        w2_hi = sb("w2_hi", [P, NF, D], F32R, at=W + 24 * KB)
        w2_lo = sb("w2_lo", [P, NF, D], F32R, at=W + 8 * KB)
        w2_raw = sb("w2_raw", [P, NF, D], at=W + 8 * KB)
        gb2 = sb("gb2", [P, D], at=W + 114 * KB)
        hf = sb("hf", [P, 2, GT], at=WORK)
        h_hi = sb("h_hi", [P, 2, GT], F32R, at=WORK + 4 * KB)
        h_lo = sb("h_lo", [P, 2, GT], F32R, at=WORK + 8 * KB)

        wq_hi = sb("wq_hi", [P, KD, H * DH], F32R, at=W + 32 * KB)
        wq_lo = sb("wq_lo", [P, KD, H * DH], F32R, at=W + 48 * KB)
        wq_raw = sb("wq_raw", [P, KD, H * DH], at=W + 48 * KB)
        wkv_hi = sb("wkv_hi", [P, KD, 2 * HKV * DH], F32R, at=W + 64 * KB)
        wkv_lo = sb("wkv_lo", [P, KD, 2 * HKV * DH], F32R, at=W + 72 * KB)
        wkv_raw = sb("wkv_raw", [P, KD, 2 * HKV * DH], at=W + 72 * KB)
        wo2_hi = sb("wo2_hi", [P, H, D], F32R, at=W + 80 * KB)
        wo2_lo = sb("wo2_lo", [P, H, D], F32R, at=W + 96 * KB)
        wo2_raw = sb("wo2_raw", [P, H, D], at=W + 96 * KB)
        W2 = W + 112 * KB
        qr = sb("qr", [P, 2, REP * DH], at=W2)
        rb = sb("rb", [P, REP * DH], at=W2 + 4 * KB)
        sq = sb("sq", [P, REP * DH], at=W2 + 6 * KB)
        kr = sb("kr", [P, HKV * DH], at=W2 + 8 * KB)
        kb = sb("kb", [P, HKV * DH], at=W2 + 10 * KB)
        ksq = sb("ksq", [P, HKV * DH], at=W2 + 12 * KB)
        q_t = sb("q_t", [P, 2, REP * T], at=W2 + 14 * KB)
        k_t = sb("k_t", [P, 2, HKV * T], at=W2 + 18 * KB)
        v_hi = sb("v_hi", [P, 2, HKV * DH], F32R, at=W2 + 22 * KB)
        v_lo = sb("v_lo", [P, 2, HKV * DH], F32R, at=W2 + 26 * KB)
        p2 = sb("p2", [P, 2, REP, T], at=W2 + 30 * KB)
        pt_hi = sb("pt_hi", [P, REP * T], F32R, at=W2 + 34 * KB)
        pt_lo = sb("pt_lo", [P, REP * T], F32R, at=W2 + 36 * KB)
        o2_hi = sb("o2_hi", [P, REP * T], F32R, at=W2 + 38 * KB)
        o2_lo = sb("o2_lo", [P, REP * T], F32R, at=W2 + 40 * KB)
        rope = sb("rope", [P, 4, DH], at=W2 + 42 * KB)
        cos_sin = sb("cos_sin", [P, 2, DH], at=W2 + 44 * KB)
        mask = sb("mask", [P, REP * T], BF16, at=W2 + 45 * KB)
        ident_b = sb("ident_b", [P, P], BF16, at=W2 + 46 * KB)
        mask_f = sb("mask_f", [P, T], at=W2 + 46 * KB + 256)
        small = W2 + 46 * KB + 768
        q_ms = sb("q_ms", [P, 2, REP], at=small)
        q_ve = sb("q_ve", [P, 2, REP], at=small + 32)
        rq = sb("rq", [P, 4, REP], at=small + 64)
        k_ms = sb("k_ms", [P, HKV], at=small + 128)
        k_ve = sb("k_ve", [P, HKV], at=small + 160)
        rk = sb("rk", [P, HKV], at=small + 192)
        nb = sb("nb", [P, 2, REP], at=small + 224)
        wg_hi = sb("wg_hi", [P, NR, KD, P], F32R, at=W)
        wg_lo = sb("wg_lo", [P, NR, KD, P], F32R, at=W + 11 * KB)
        wg_raw = sb("wg_raw", [P, NR, KD, P], at=W + 11 * KB)
        rw = sb("rw", [P, KD, E], at=W + 28 * KB)
        before = sb("before", [P, E, E], at=W + 28 * KB + 256)
        gt = sb("gt", [P, GB, E, E], at=W + 28 * KB + 512)
        eq = sb("eq", [P, GB, E, E], at=W + 29 * KB + 512)
        probs = sb("probs", [P, B, E], at=W2 + 47 * KB)
        pick = sb("pick", [P, GB, E], at=W + 30 * KB + 640)
        r4 = sb("r4", [P, 4, GB], at=W + 30 * KB + 768)
        comb = sb("comb", [P, B, E], at=W + 31 * KB)
        lt = sb("lt", [E, GT], at=place["gate"][0])
        wu_hi = sb("wu_hi", [P, NR, KD, P], F32R, at=W + 32 * KB)
        wu_lo = sb("wu_lo", [P, NR, KD, P], F32R, at=W + 65 * KB)
        wu_raw = sb("wu_raw", [P, NR, KD, P], at=W + 65 * KB)
        wd_hi = sb("wd_hi", [P, NR, D], F32R, at=W + 54 * KB)
        wd_lo = sb("wd_lo", [P, NR, D], F32R, at=W + 43 * KB)
        wd_raw = sb("wd_raw", [P, NR, D], at=W + 43 * KB)
        sg = sb("sg", [P, 2, GT], at=W2)
        em = sb("em", [P, 2, GT], at=W2 + 4 * KB)
        e_hi = sb("e_hi", [P, 2, GT], F32R, at=W2 + 8 * KB)
        e_lo = sb("e_lo", [P, 2, GT], F32R, at=W2 + 12 * KB)
        x0 = sb("x0", [P, GB, D], at=W2 + 16 * KB)
        y = sb("y", [P, GB, D], at=W2 + 20 * KB)
        ct = [sb(f"ct{r}", [E, GT], at=W2 + (42 if r == 0 else 22 + 2 * r) * KB) for r in range(NG)]
        cw = [sb(f"cw{i}", [P, GT], at=W + (76 + 2 * i if i < 2 else 18 + 2 * i if i < 5 else 70 + 2 * i) * KB)
              for i in range(NR)]

        bank = [ctx.enter_context(nc.psum_tensor(f"bank{i}", [P, 512], F32)) for i in range(8)]
        ct_dram = nc.dram_tensor("combination_scratch", (NG, E, GT), F32).ap()
        gates_dram = nc.dram_tensor("gates_scratch", (B, 2, D), F32).ap()

        d_x = [sem(f"d_x{g}") for g in range(NG)]
        d_first, d_small = sem("d_first"), sem("d_small")
        d_ada1, d_ada2 = sem("d_ada1"), sem("d_ada2")
        d_pair = [sem(f"d_pair{c}") for c in range(H // 2)]
        d_gout = sem("d_gout")
        d_gate = sem("d_gate")
        d_wq, d_wkv, d_oproj, d_rope = sem("d_wq"), sem("d_wkv"), sem("d_oproj"), sem("d_rope")
        d_wg, d_wu, d_wd, d_rw, d_xin = sem("d_wg"), sem("d_wu"), sem("d_wd"), sem("d_rw"), sem("d_xin")
        d_w1, d_w2, d_b2 = sem("d_w1"), sem("d_w2"), sem("d_b2")
        d_out = sem("d_out")
        consts, ada_p, ada_s, bq_s = sem("consts"), sem("ada_p"), sem("ada_s"), sem("bq_s")
        w_hi1, w_lo1 = sem("w_hi1"), sem("w_lo1")
        w_lo1p = sem("w_lo1p")

        def lo1(c, i):
            return (w_lo1p, 3 * c + i + 1) if c < 2 else (w_lo1, 3 * (c - 2) + i + 1)

        w_hi2, w_lo2 = sem("w_hi2"), sem("w_lo2")
        n_bn, n_st, n_ve, n_rs, n_xn, n_tp, n_ev = (
            sem(f"n_{x}") for x in ("bn", "st", "ve", "rs", "xn", "tp", "ev"))
        n_m2 = sem("n_m2")
        c_hi, c_lo = sem("c_hi"), sem("c_lo")
        a_qp, a_kp, a_vp, a_sp, a_tp, a_pvp, a_op = (
            sem(f"a_{x}") for x in ("qp", "kp", "vp", "sp", "tp", "pvp", "op"))
        a_q, a_k, a_v, a_mx, a_ex, a_ri, a_pn, a_pt, a_oh, a_ol = (
            sem(f"a_{x}") for x in ("q", "k", "v", "mx", "ex", "ri", "pn", "pt", "oh", "ol"))
        r_gb, r_b, r_mul, r_x = sem("r_gb"), sem("r_b"), sem("r_mul"), sem("r_x")
        f_up, f_dp, f_g, f_h, f_l = (sem(f"f_{x}") for x in ("up", "dp", "g", "h", "l"))

        w_ohi3, w_olo3 = sem("w_ohi3"), sem("w_olo3")
        w_hi3, w_lo3, g_tab, g_mask = sem("w_hi3"), sem("w_lo3"), sem("g_tab"), sem("g_mask")
        g_kp, g_vp, g_qp, g_tp, g_qtp, g_op, g_pvp, g_ktp, g_sp = (
            sem(f"g_{x}") for x in ("kp", "vp", "qp", "tp", "qtp", "op", "pvp", "ktp", "sp"))
        g_ex, g_ksq, g_sq, g_ph, g_vh, g_qt, g_oh, g_kt = (
            sem(f"g_{x}") for x in ("ex", "ksq", "sq", "ph", "vh", "qt", "oh", "kt"))
        g_x, g_mx, g_nb, g_kb, g_qb, g_ks, g_kr, g_pl, g_ss, g_ri, g_vl, g_ol = (
            sem(f"g_{x}") for x in ("x", "mx", "nb", "kb", "qb", "ks", "kr", "pl", "ss", "ri", "vl", "ol"))
        g_ka, g_rk, g_kv, g_qr, g_rq, g_qv, g_pn = (
            sem(f"g_{x}") for x in ("ka", "rk", "kv", "qr", "rq", "qv", "pn"))
        w_hi4, w_lo4, m_sel = sem("w_hi4"), sem("w_lo4"), sem("m_sel")
        m_gp, m_up, m_dp, m_sg, m_su, m_em, m_h, m_l, m_y = (
            sem(f"m_{x}") for x in ("gp", "up", "dp", "sg", "su", "em", "h", "l", "y"))
        t_lp, t_lt, t_ltp, t_ctp, t_ex, t_v0, t_v, t_cb = (
            sem(f"t_{x}") for x in ("lp", "lt", "ltp", "ctp", "ex", "v0", "v", "cb"))
        d_ct = [sem(f"d_ct{r}") for r in range(NG)]
        d_cw = [sem(f"d_cw{i}") for i in range(NR)]
        t_ct = sem("t_ct")
        RV = 11

        block = ctx.enter_context(nc.Block())

        class NormJob:

            def __init__(self, n, g, kind, part):
                self.n, self.g, self.kind, self.part = n, g, kind, part

        def background_norm(g, h, first):
            if first and 3 <= h < 3 + 4 * (NG - 1):
                return NormJob(1 + (h - 3) // 4, 1 + (h - 3) // 4, 0, (h - 3) % 4)
            if not first and 3 <= h < 7:
                return NormJob(NG + g - 1, g - 1, 1, h - 3)
            return None

        class Step:

            def __init__(self, g, u, first):
                self.g, self.u, self.first = g, u, first
                self.n, self.b, self.kv = g * 4 * GB + u, u // HKV, u % HKV
                self.seq = g * GB + self.b

            def new(self):
                return self.u < 4 * GB

            def live(self, k):
                return self.had(k) and self.u - k < 4 * GB

            def had(self, k):
                return self.u >= k or not self.first

        def attention2(eng, step):
            for u in range(4 * GB):
                step(Step(0, u, True))
            with eng.Fori(1, NG) as g:
                for u in range(4 * GB):
                    step(Step(g, u, False))
            for u in range(4 * GB, 4 * GB + 7):
                step(Step(NG - 1, u, False))

        def back(i):
            return 1 if i == 0 else 2

        def segments(i):
            return [(e, max(e * I - i * P, 0), min((e + 1) * I - i * P, P))
                    for e in range(i * P // I, ((i + 1) * P - 1) // I + 1)]

        WG_STEP = 5

        def late_chunk(u):
            c = u - (4 * GB + 1)
            return None if not 0 <= c < 6 else (c // 3, c % 3, slice(4 * (c % 3), min(4 * (c % 3) + 4, NR)))

        def pair_part(c, i):
            hs, cs = slice(2 * c, 2 * c + 2), slice(2 * DH * c, 2 * DH * (c + 1))
            if i == 0:
                return [w[:, hs].rearrange("p h c k d -> p (h c k d)") for w in (wqk_lo, wqk_raw, wqk_hi)]
            if i == 1:
                return [w[:, :, cs] for w in (wv_lo, wv_raw, wv_hi)]
            return [w[:, hs] for w in (wo_lo, wo_raw, wo_hi)]

        def span(t, k, g, b0=0, nb=GB):
            return t[:, k, bass.ds((g * GB + b0) * T, nb * T)]

        def split_products(hi_l, lo_l, hi_r, lo_r):
            return ((hi_l, hi_r), (hi_l, lo_r), (lo_l, hi_r))

        @block.sync
        def _(sp):
            def load_x(g):
                sp.dma_start(xres[:, g * GB:(g + 1) * GB, :],
                             ins["x"][g * GB:(g + 1) * GB].rearrange("b t d -> t b d")).then_inc(d_x[g], 16)

            def load_pair(c):
                hs, cs = slice(2 * c, 2 * c + 2), slice(2 * DH * c, 2 * DH * (c + 1))
                sp.dma_start(wqk_raw[:, hs], ins["wqk"][:, hs]).then_inc(d_pair[c], 16)
                sp.dma_start(wv_raw[:, :, cs], ins["wv"][:, :, cs]).then_inc(d_pair[c], 16)
                sp.dma_start(wo_raw[:, hs], ins["wo"][:, hs]).then_inc(d_pair[c], 16)

            load_x(0)
            sp.dma_start(cond_t[:], ins["cond_t"]).then_inc(d_first, 16)
            sp.dma_start(ada_bt[:], ins["ada_bt"]).then_inc(d_first, 16)
            sp.dma_start(bqkv[:], ins["bqkv"]).then_inc(d_first, 16)
            sp.dma_start(ada_w[:, :, 0:2 * D], ins["ada_w"][:, :, 0:2 * D]).then_inc(d_ada1, 16)
            load_pair(0)
            load_pair(1)
            sp.dma_start(ada_w[:, :, 2 * D:], ins["ada_w"][:, :, 2 * D:]).then_inc(d_ada2, 16)
            sp.dma_start(ada_bg[:], ins["ada_bg"]).then_inc(d_small, 16)
            load_x(1)
            for c in range(2, H // 2):
                load_pair(c)
            sp.dma_start(b1[:], ins["b1"]).then_inc(d_small, 16)
            sp.dma_start(norm_w[:], ins["norm_w"]).then_inc(d_small, 16)
            sp.dma_start(obias[:], ins["out_b"].partition_broadcast(P)).then_inc(d_small, 16)
            for g in range(2, NG):
                load_x(g)
            sp.wait_ge(ada_s, 9)
            sp.dma_start(gates_dram, gates[:]).then_inc(d_gout, 16)
            sp.wait_ge(d_gout, 16)
            sp.wait_ge(n_tp, 2 * NG)
            sp.dma_start(gate[:], gates_dram[0:GB, 0, :].partition_broadcast(P)).then_inc(d_gate, 16)
            with sp.Fori(1, NG) as g:
                sp.wait_ge(n_tp, 2 * (NG + g))
                sp.dma_start(gate[:], gates_dram[bass.ds(g * GB, GB), 0, :].partition_broadcast(P)).then_inc(d_gate, 16)
            sp.wait_ge(a_kp, 3 * H + 8)
            sp.dma_start(w1_raw[:], ins["w1"]).then_inc(d_w1, 16)
            sp.dma_start(w2_raw[:], ins["w2"]).then_inc(d_w2, 16)
            sp.wait_ge(a_vp, NG * H)
            sp.dma_start(wkv_raw[:], ins["wkv"]).then_inc(d_wkv, 16)
            sp.dma_start(wq_raw[:], ins["wq"]).then_inc(d_wq, 16)
            sp.wait_ge(a_op, NG * H)
            sp.dma_start(wo2_raw[:], ins["wo2"]).then_inc(d_oproj, 16)
            sp.dma_start(rope[:], ins["qk_norm"].partition_broadcast(P)).then_inc(d_rope, 16)
            sp.dma_start(cos_sin[:], ins["cos_sin"]).then_inc(d_rope, 16)
            sp.wait_ge(r_b, GB * NG)
            sp.dma_start(obias[:], ins["b2"].partition_broadcast(P)).then_inc(d_b2, 16)
            sp.wait_ge(n_tp, 2 * (2 * NG))
            sp.dma_start(gate[:], gates_dram[0:GB, 1, :].partition_broadcast(P)).then_inc(d_gate, 16)
            with sp.Fori(1, NG) as g:
                sp.wait_ge(n_tp, 2 * (2 * NG + g))
                sp.dma_start(gate[:], gates_dram[bass.ds(g * GB, GB), 1, :].partition_broadcast(P)).then_inc(d_gate, 16)
            sp.wait_ge(f_up, NG * NF)
            sp.wait_ge(f_dp, NG * NF)
            sp.dma_start(wg_raw[:], ins["wg"]).then_inc(d_wg, 16)
            sp.dma_start(rw[:], ins["rw"]).then_inc(d_rw, 16)
            sp.wait_ge(g_kp, B)
            sp.wait_ge(g_vp, B)
            sp.dma_start(wu_raw[:], ins["wu"]).then_inc(d_wu, 16)
            sp.wait_ge(g_qp, NG * 4 * GB)
            sp.dma_start(wd_raw[:], ins["wd"]).then_inc(d_wd, 16)

            def load_weights(g, i):
                for e, first, end in segments(i):
                    sp.dma_start(cw[i][first:end].unsqueeze(1),
                                 ct_dram[bass.ds(g, 1), e, :].partition_broadcast(end - first)).then_inc(d_cw[i], 16)

            def load_input(g):
                sp.dma_start(x0[:], ins["x"][bass.ds(g * GB, GB)].rearrange("b t d -> t b d")).then_inc(d_xin, 16)

            def store(g):
                sp.wait_ge(m_y, 4 * g + 4)
                sp.dma_start(out[bass.ds(g * GB, GB)].rearrange("b t d -> t b d"), y[:]).then_inc(d_out, 16)

            sp.wait_ge(d_ct[0], 16)
            for i in range(5):
                load_weights(0, i)
            sp.wait_ge(g_op, NG * 4 * GB)
            for i in range(5, NR):
                load_weights(0, i)
            sp.wait_ge(g_x, B)
            load_input(0)
            sp.wait_ge(d_ct[1], 16)
            for i in range(NR):
                sp.wait_ge(m_em, i + 1)
                load_weights(1, i)
            sp.wait_ge(d_ct[2], 16)
            sp.wait_ge(d_ct[3], 16)
            with sp.Fori(2, NG) as g:
                for i in range(NR):
                    sp.wait_ge(m_em, (g - 1) * NR + i + 1)
                    load_weights(g, i)
                    if i == 4:
                        store(g - 2)
                        load_input(g - 1)
            store(NG - 2)
            load_input(NG - 1)
            store(NG - 1)
            sp.wait_ge(d_out, 16 * NG)

        @block.gpsimd
        def _(pool):
            nc.gpsimd.memset(neg_half[:], -0.5).then_inc(consts, 1)
            nc.gpsimd.memset(ident[:], 0.0).then_inc(consts, 1)
            nc.gpsimd.memset(eps[:], EPS).then_inc(consts, 1)
            pool.wait_ge(consts, 3)
            nc.gpsimd.affine_select(out=ident[:], in_=ident[:], compare_op=ALU.not_equal, fill=1.0, base=0,
                                    pattern=[[-1, P]], channel_multiplier=1).then_inc(consts, 1)

            def norm(n, rms=False):
                pool.wait_ge(n_st, n + 1)
                nc.gpsimd.tensor_tensor(vare[:], mv[:, :, 1], eps[:, 0:GB], ALU.add).then_inc(n_ve, 1)
                if rms:
                    nc.gpsimd.tensor_tensor(mean2[:], mv[:, :, 0], mv[:, :, 0], ALU.mult).then_inc(n_m2, 1)
                    pool.wait_ge(n_m2, 2 * (n - 2 * NG) + 1)
                    pool.wait_ge(n_ve, n + 1)
                    nc.gpsimd.tensor_tensor(vare[:], vare[:], mean2[:], ALU.add).then_inc(n_m2, 1)
                    pool.wait_ge(n_m2, 2 * (n - 2 * NG) + 2)
                pool.wait_ge(n_ve, n + 1)
                nc.gpsimd.tensor_tensor(rstd[:], vare[:], neg_half[:, 0:GB], ALU.pow).then_inc(n_rs, 1)

            norm(0)
            for c, i in ((c, i) for c in range(2) for i in range(3)):
                lo, raw, hi = pair_part(c, i)
                pool.wait_ge(w_hi1, 3 * c + i + 1)
                nc.gpsimd.tensor_tensor(lo, raw, hi.bitcast(F32), ALU.subtract).then_inc(w_lo1p, 1)

            def residual_bias(r, g, gb):
                pool.wait_ge(d_gate, 16 * (r + 1))
                for b in range(GB):
                    nc.gpsimd.tensor_tensor(gb[:], gate[:, b], obias[:], ALU.mult).then_inc(r_gb, 1)
                    xs = xres[:, bass.ds(g * GB + b, 1), :].rearrange("p a d -> p (a d)")
                    pool.wait_ge(r_gb, GB * r + b + 1)
                    nc.gpsimd.tensor_tensor(xs, xs, gb[:], ALU.add).then_inc(r_b, 1)
                    if b < GB - 1:
                        pool.wait_ge(r_b, GB * r + b + 1)

            def normalise(n, h):
                pool.wait_ge(a_ri, n + 1)
                nc.gpsimd.tensor_tensor(p1[:, h % 2], p1[:, h % 2],
                                        rinv[:, h % 2].unsqueeze(2).broadcast_to([P, GB, T]),
                                        ALU.mult).then_inc(a_pn, 1)

            def attention1(g, first):
                for h in range(H):
                    if h >= 1 or not first:
                        normalise(g * H + h - 1, (h - 1) % 2)
                    if h == 0 and not first:
                        residual_bias(g - 1, g - 1, gb1)
                    job = background_norm(g, h, first)
                    if job and job.part == 0:
                        norm(job.n)

            attention1(0, True)
            with pool.Fori(1, NG) as g:
                attention1(g, False)
            pool.wait_ge(w_hi2, 1)
            nc.gpsimd.tensor_tensor(w1_lo[:, 0:NF // 2], w1_raw[:, 0:NF // 2], w1_hi[:, 0:NF // 2].bitcast(F32),
                                    ALU.subtract).then_inc(w_lo2, 1)
            normalise(NG * H - 1, 1)
            residual_bias(NG - 1, NG - 1, gb1)
            norm(2 * NG - 1)

            pool.wait_ge(a_op, NG * H)
            nc.gpsimd.memset(mask_f[:], 0.0).then_inc(g_mask, 1)
            pool.wait_ge(g_mask, 1)
            nc.gpsimd.affine_select(out=mask_f[:], in_=mask_f[:], compare_op=ALU.is_ge, fill=-1e30, base=0,
                                    pattern=[[-1, T]], channel_multiplier=1).then_inc(g_mask, 1)

            for g in range(NG):
                pool.wait_ge(d_b2, 16)
                residual_bias(NG + g, g, gb2)
                if g < NG - 1:
                    norm(2 * NG + g, True)

            def experts_constants():
                pool.wait_ge(f_dp, NG * NF)
                nc.gpsimd.memset(before[:], 1.0).then_inc(m_sel, 1)
                pool.wait_ge(m_sel, 1)
                nc.gpsimd.affine_select(out=before[:], in_=before[:], compare_op=ALU.is_gt, fill=0.0, base=0,
                                        pattern=[[1, E], [-1, E]], channel_multiplier=0).then_inc(m_sel, 1)

            def step(s):
                n, new_seq = s.n, s.new() and s.kv == 0
                if new_seq:
                    pool.wait_ge(g_kb, s.seq + 1)
                    nc.gpsimd.tensor_tensor(kr[:], kr[:], kb[:], ALU.add).then_inc(g_ka, 1)
                if s.new():
                    pool.wait_ge(g_qb, n + 1)
                    nc.gpsimd.tensor_tensor(qr[:, s.u % 2], qr[:, s.u % 2], rb[:], ALU.add).then_inc(g_qr, 1)
                if s.live(3):
                    pool.wait_ge(g_ri, n - 2)
                    nc.gpsimd.tensor_tensor(p2[:, (s.u - 3) % 2], p2[:, (s.u - 3) % 2],
                                            rinv[:, (s.u - 3) % 2].unsqueeze(2).broadcast_to([P, REP, T]),
                                            ALU.mult).then_inc(g_pn, 1)
                if s.new():
                    pool.wait_ge(g_ss, n + 1)
                    if s.had(2):
                        pool.wait_ge(g_rq, n - 1)
                    nc.gpsimd.tensor_tensor(q_ve[:, s.u % 2], q_ms[:, s.u % 2], eps[:, 0:REP], ALU.add).then_inc(g_qv, 1)
                    pool.wait_ge(g_qv, n + 1)
                    if s.had(4):
                        pool.wait_ge(g_ex, n - 3)
                    nc.gpsimd.tensor_tensor(rq[:, s.u % 4], q_ve[:, s.u % 2], neg_half[:, 0:REP], ALU.pow).then_inc(g_rq, 1)
                if new_seq:
                    pool.wait_ge(g_ks, s.seq + 1)
                    if s.had(4):
                        pool.wait_ge(g_rk, s.seq)
                    nc.gpsimd.tensor_tensor(k_ve[:], k_ms[:], eps[:, 0:HKV], ALU.add).then_inc(g_kv, 1)
                    pool.wait_ge(g_kv, s.seq + 1)
                    nc.gpsimd.tensor_tensor(rk[:], k_ve[:], neg_half[:, 0:HKV], ALU.pow).then_inc(g_rk, 1)
                if s.first and s.u == 9:
                    experts_constants()
                if s.u == 8:
                    norm(3 * NG + s.g - 1, True)

            attention2(pool, step)
            norm(4 * NG - 1, True)

        @block.scalar
        def _(act):
            def logits_copy(r, src):
                act.wait_ge(t_lp, r + 1)
                nc.scalar.activation(lt[:], src[0:E, :], ACT.Copy).then_inc(t_lt, 1)

            def router_exp(r):
                act.wait_ge(t_v0, 2 * r + 2)
                of_group = probs[:, bass.ds(r * GB, GB), :]
                nc.scalar.activation(of_group, of_group, ACT.Exp).then_inc(t_ex, 1)

            def cur(c, g):
                for k in range(KD):
                    nc.scalar.activation(cur_hi[:, k], act_t[:, k, bass.ds(g * GT, GT)], ACT.Copy).then_inc(c_hi, 1)

            def split_pair(c):
                hs, cs = slice(2 * c, 2 * c + 2), slice(2 * DH * c, 2 * DH * (c + 1))
                act.wait_ge(d_pair[c], 48)
                if c == 4:
                    act.wait_ge(ada_p, 2)
                    act.wait_ge(ada_s, 9)
                    act.wait_ge(d_gout, 16)
                nc.scalar.activation(wqk_hi[:, hs], wqk_raw[:, hs], ACT.Copy).then_inc(w_hi1, 1)
                nc.scalar.activation(wv_hi[:, :, cs], wv_raw[:, :, cs], ACT.Copy).then_inc(w_hi1, 1)
                nc.scalar.activation(wo_hi[:, hs], wo_raw[:, hs], ACT.Copy).then_inc(w_hi1, 1)

            act.wait_ge(d_first, 48)
            nc.scalar.activation(bqkv[:, 0], bqkv[:, 0], ACT.Copy, scale=SCALE).then_inc(bq_s, 1)
            split_pair(0)

            def exps(n, h):
                act.wait_ge(a_mx, n + 1)
                if not isinstance(n, int) or n >= 2:
                    act.wait_ge(a_tp, n - 1)
                for b in range(GB):
                    last = nc.scalar.activation(p1[:, h % 2, b], bank[3][:, b * T:(b + 1) * T], ACT.Exp,
                                                bias=nmax[:, h % 2, b:b + 1], accum_out=rsum[:, h % 2, b:b + 1])
                last.then_inc(a_ex, 1)

            def o_hi(n, h):
                act.wait_ge(a_pvp, n + 1)
                if not isinstance(n, int) or n >= 2:
                    act.wait_ge(a_op, n - 1)
                nc.scalar.activation(o1_hi[:, h % 2], bank[5][:], ACT.Identity,
                                     bias=bqkv[:, 2, h:h + 1]).then_inc(a_oh, 1)

            def attention1(g, first):
                for h in range(H):
                    n = g * H + h
                    if h == 0:
                        act.wait_ge(n_ev, 2 * (g + 1))
                        if not first:
                            act.wait_ge(a_vp, n)
                        cur(g, g)
                    if h >= 1 or not first:
                        exps(n - 1, (h - 1) % 2)
                    act.wait_ge(a_qp, n + 1)
                    if h >= 2 or not first:
                        act.wait_ge(a_sp, n - 1)
                    nc.scalar.activation(q1[:, h % 2], bank[0][:], ACT.Identity, scale=SCALE,
                                         bias=bqkv[:, 0, h:h + 1]).then_inc(a_q, 1)
                    if first and h == 0:
                        split_pair(1)
                    if h >= 2 or not first:
                        o_hi(n - 2, (h - 2) % H)
                    act.wait_ge(a_vp, n + 1)
                    if h >= 4 or not first:
                        act.wait_ge(a_pvp, n - h % 2 - 2)
                    nc.scalar.activation(v1[:, h // 2 % 2, h % 2 * 2:h % 2 * 2 + 2],
                                         bank[2][:].rearrange("p (b d) -> p b d", b=2), ACT.Copy).then_inc(a_v, 1)
                    if first and h % 2 == 0 and 0 < h < H - 2:
                        split_pair(h // 2 + 1)

            attention1(0, True)
            with act.Fori(1, NG) as g:
                attention1(g, False)
            def split2(weights, half):
                hi, raw, d = ((w1_hi, w1_raw, d_w1), (w2_hi, w2_raw, d_w2))[weights]
                fs = slice(half * NF // 2, (half + 1) * NF // 2)
                act.wait_ge(d, 16)
                nc.scalar.activation(hi[:, fs], raw[:, fs], ACT.Copy).then_inc(w_hi2, 1)

            def split3(c):
                act.wait_ge(d_wkv, 16)
                nc.scalar.activation(wkv_hi[:, :, bass.ds(c * 256, 256)], wkv_raw[:, :, bass.ds(c * 256, 256)],
                                     ACT.Copy).then_inc(w_hi3, 1)
                act.wait_ge(d_wq, 16)
                nc.scalar.activation(wq_hi[:, :, bass.ds(c * 512, 512)], wq_raw[:, :, bass.ds(c * 512, 512)],
                                     ACT.Copy).then_inc(w_hi3, 1)

            def split_out(c):
                act.wait_ge(d_oproj, 16)
                nc.scalar.activation(wo2_hi[:, bass.ds(c * 4, 4)], wo2_raw[:, bass.ds(c * 4, 4)],
                                     ACT.Copy).then_inc(w_ohi3, 1)

            n = NG * H
            act.wait_ge(a_kp, n)
            split2(0, 0)
            act.wait_ge(n_ev, 2 * (NG + 1))
            act.wait_ge(a_vp, n)
            cur(NG, 0)
            exps(n - 1, 1)
            split2(0, 1)
            o_hi(n - 2, H - 2)
            split2(1, 0)

            def h_round(m, f, first):
                act.wait_ge(f_g, m + 1)
                if f >= 2 or not first:
                    act.wait_ge(f_dp, m - 1)
                nc.scalar.activation(h_hi[:, f % 2], hf[:, f % 2], ACT.Copy).then_inc(f_h, 1)

            def ffn1(g, first):
                for f in range(NF):
                    m = g * NF + f
                    if f == 0 and not first:
                        act.wait_ge(n_ev, 2 * (NG + g + 1))
                        act.wait_ge(f_up, m)
                        cur(NG + g, g)
                    if f == 1 and first:
                        o_hi(n - 1, H - 1)
                    if f >= 1 or not first:
                        h_round(m - 1, (f - 1) % NF, first)
                    act.wait_ge(f_up, m + 1)
                    if f == 0 and first:
                        act.wait_ge(a_sp, n)
                    if f >= 2 or not first:
                        act.wait_ge(f_l, m - 1)
                    nc.scalar.activation(hf[:, f % 2], bank[f % 2][:], ACT.Gelu, bias=b1[:, f:f + 1]).then_inc(f_g, 1)
                    if f == 1 and first:
                        split2(1, 1)
                    if f == 4 and not first:
                        split_out(g - 1)
                    if f == 6:
                        if first:
                            act.wait_ge(a_op, n)
                        split3(g)

            ffn1(0, True)
            with act.Fori(1, NG) as g:
                ffn1(g, False)

            def gate_silu(n, i):
                act.wait_ge(m_gp, n + 1)
                nc.scalar.activation(sg[:, i % 2], bank[i % 2][:], ACT.Silu).then_inc(m_sg, 1)

            def combination_out(r):
                act.wait_ge(t_ctp, r + 1)
                nc.scalar.activation(ct[r][:], bank[4][0:E, :], ACT.Copy).then_inc(t_ct, 1)
                act.wait_ge(t_ct, r + 1)
                act.dma_start(ct_dram[r], ct[r][:]).then_inc(d_ct[r], 16)

            def step(s):
                n, new_seq = s.n, s.new() and s.kv == 0
                if s.u == 0:
                    act.wait_ge(n_ev, 2 * (2 * NG + s.g + 1))
                    if s.first:
                        act.wait_ge(f_up, NG * NF)
                        act.wait_ge(c_lo, KD * 2 * NG)
                    else:
                        act.wait_ge(g_qp, n)
                    cur(2 * NG + s.g, s.g)
                    if s.first:
                        h_round(NG * NF - 1, NF - 1, False)
                if s.live(3):
                    act.wait_ge(g_nb, n - 2)
                    if s.had(5):
                        act.wait_ge(g_tp, n - 4)
                    for j in range(REP):
                        last = nc.scalar.activation(p2[:, (s.u - 3) % 2, j], bank[3][:, j * T:(j + 1) * T], ACT.Exp,
                                                    scale=rq[:, (s.u - 3) % 4, j:j + 1],
                                                    bias=nb[:, (s.u - 3) % 2, j:j + 1],
                                                    accum_out=rsum[:, (s.u - 3) % 2, j:j + 1])
                    last.then_inc(g_ex, 1)
                if new_seq:
                    act.wait_ge(g_kb, s.seq + 1)
                    if s.had(4):
                        act.wait_ge(g_ks, s.seq)
                    nc.scalar.activation(ksq[:], bank[1][:], ACT.Square, scale=SCALE).then_inc(g_ksq, 1)
                if s.new():
                    act.wait_ge(g_qb, n + 1)
                    if s.had(1):
                        act.wait_ge(g_ss, n)
                    nc.scalar.activation(sq[:], bank[0][:], ACT.Square, scale=SCALE).then_inc(g_sq, 1)
                if s.u == 13 and not s.first:
                    router_exp(s.g - 1)
                if s.live(5):
                    act.wait_ge(g_pvp, n - 4)
                    if s.had(6):
                        act.wait_ge(g_op, n - 5)
                    nc.scalar.activation(o2_hi[:], bank[6][:], ACT.Copy).then_inc(g_oh, 1)
                if s.live(1):
                    act.wait_ge(g_qtp, n)
                    if s.had(3):
                        act.wait_ge(g_sp, n - 2)
                    nc.scalar.activation(q_t[:, (s.u - 1) % 2], bank[4][:], ACT.Copy).then_inc(g_qt, 1)
                if s.u == 11 and not s.first:
                    logits_copy(s.g - 1, bank[2])
                if s.live(4):
                    act.wait_ge(g_tp, n - 3)
                    if s.had(5):
                        act.wait_ge(g_pvp, n - 4)
                    nc.scalar.activation(pt_hi[:], bank[5][:], ACT.Copy).then_inc(g_ph, 1)
                if new_seq:
                    act.wait_ge(g_vp, s.seq + 1)
                    if s.first and s.u == 0:
                        act.wait_ge(f_dp, NG * NF)
                    if s.had(8):
                        act.wait_ge(g_pvp, 4 * (s.seq - 1))
                    nc.scalar.activation(v_hi[:, s.b % 2], bank[2][:], ACT.Copy).then_inc(g_vh, 1)
                if s.new() and s.kv == 1:
                    act.wait_ge(g_ktp, s.seq + 1)
                    if s.had(8):
                        act.wait_ge(g_sp, 4 * (s.seq - 1))
                    nc.scalar.activation(k_t[:, s.b % 2], bank[1][:], ACT.Copy).then_inc(g_kt, 1)
                if s.first and s.u == 3:
                    split_out(NG - 1)
                if s.first and s.u >= WG_STEP:
                    act.wait_ge(d_wg, 16)
                    nc.scalar.activation(wg_hi[:, s.u - WG_STEP], wg_raw[:, s.u - WG_STEP], ACT.Copy).then_inc(w_hi4, 1)
                if s.u == 4 * GB + 1:
                    act.wait_ge(n_ev, 2 * (3 * NG + 1))
                    act.wait_ge(g_qp, NG * 4 * GB)
                    act.wait_ge(g_vp, B)
                    cur(3 * NG, 0)
                if s.u == 4 * GB + 2:
                    combination_out(0)
                if late_chunk(s.u):
                    which, _, tiles = late_chunk(s.u)
                    act.wait_ge((d_wu, d_wd)[which], 16)
                    hi, raw = ((wu_hi, wu_raw), (wd_hi, wd_raw))[which]
                    nc.scalar.activation(hi[:, tiles], raw[:, tiles], ACT.Copy).then_inc(w_hi4, 1)
                if s.u == 4 * GB + 5:
                    gate_silu(0, 0)

            attention2(act, step)

            def e_round(n, i, first):
                act.wait_ge(m_em, n + 1)
                if i >= 2 or not first:
                    act.wait_ge(m_dp, n - back(i) + 1)
                nc.scalar.activation(e_hi[:, i % 2], em[:, i % 2], ACT.Copy).then_inc(m_h, 1)

            def experts(g, first):
                for i in range(NR):
                    n = g * NR + i
                    if i == 0 and not first:
                        act.wait_ge(n_ev, 2 * (3 * NG + g + 1))
                        act.wait_ge(m_up, n)
                        cur(3 * NG + g, g)
                    if i >= 1 or not first:
                        e_round(n - 1, (i - 1) % NR, first)
                    if i >= 2 or not first:
                        act.wait_ge(m_em, n - back(i) + 1)
                    if i >= 1 or not first:
                        gate_silu(n, i)
                    if first and i in (5, 8, 10):
                        combination_out((5, 8, 10).index(i) + 1)
                    if i == 5 and first:
                        logits_copy(NG - 1, bank[5])
                    if i == 7 and first:
                        router_exp(NG - 1)

            experts(0, True)
            with act.Fori(1, NG) as g:
                experts(g, False)
            e_round(NG * NR - 1, NR - 1, False)

        @block.vector
        def _(dve):
            def norm_stats(g):
                for b in range(GB):
                    last = nc.vector.bn_stats(bn[:, b], xres[:, bass.ds(g * GB + b, 1), :].rearrange("p a d -> p (a d)"))
                last.then_inc(n_bn, 1)

            def norm_sums():
                for b in range(GB):
                    last = nc.vector.bn_aggr(mv[:, b], bn[:, b])
                last.then_inc(n_st, 1)

            def norm_apply(n, g):
                dve.wait_ge(n_rs, n + 1)
                for b in range(GB):
                    last = nc.vector.tensor_scalar(xn[:, b], xres[:, bass.ds(g * GB + b, 1), :].rearrange("p a d -> p (a d)"),
                                                   mv[:, b, 0:1], rstd[:, b:b + 1], ALU.subtract, ALU.mult)
                last.then_inc(n_xn, 1)

            def norm_apply_rms(n, g):
                dve.wait_ge(n_rs, n + 1)
                for b in range(GB):
                    last = nc.vector.tensor_scalar(xn[:, b], xres[:, bass.ds(g * GB + b, 1), :].rearrange("p a d -> p (a d)"),
                                                   rstd[:, b:b + 1], None, ALU.mult)
                last.then_inc(n_xn, 1)

            def norm_weight(n, g, k, kind, src):
                dve.wait_ge(n_tp, 2 * n + k + 1)
                nc.vector.tensor_scalar(span(act_t, k, g), src[:], norm_w[:, kind, k:k + 1], None,
                                        ALU.mult).then_inc(n_ev, 1)

            def norm_ada(n, g, k, kind, src):
                dve.wait_ge(n_tp, 2 * n + k + 1)
                for b in range(GB):
                    last = nc.vector.tensor_scalar(span(act_t, k, g, b, 1), src[:, b * T:(b + 1) * T],
                                                   ada_t[:, 2 * kind + 1, k, bass.ds(g * GB + b, 1)],
                                                   ada_t[:, 2 * kind, k, bass.ds(g * GB + b, 1)], ALU.mult, ALU.add)
                last.then_inc(n_ev, 1)

            def routing_part(r, part, src=None):
                p = probs[:, bass.ds(r * GB, GB), :]
                wide = [P, GB, E]
                if part == 0:
                    lg = src[:, 0:GB * E].rearrange("p (b e) -> p b e", b=GB)
                    dve.wait_ge(t_ltp, r + 1)
                    nc.vector.tensor_reduce(r4[:, 0], lg, X, ALU.max).then_inc(t_v0, 1)
                    dve.wait_ge(t_v0, 2 * r + 1)
                    nc.vector.tensor_tensor(p, lg, r4[:, 0].unsqueeze(2).broadcast_to(wide), ALU.subtract).then_inc(t_v0, 1)
                    return
                done = [(0, 4, 7)[part - 1]]

                def after():
                    dve.wait_ge(t_v, r * RV + done[0])

                def inc(i):
                    done[0] += 1
                    i.then_inc(t_v, 1)

                if part == 1:
                    dve.wait_ge(t_ex, r + 1)
                    inc(nc.vector.tensor_reduce(r4[:, 1], p, X, ALU.add))
                    after()
                    inc(nc.vector.reciprocal(r4[:, 2], r4[:, 1]))
                    after()
                    inc(nc.vector.tensor_tensor(p, p, r4[:, 2].unsqueeze(2).broadcast_to(wide), ALU.mult))
                    after()
                    pj = p.unsqueeze(2).broadcast_to([P, GB, E, E])
                    pe_ = p.unsqueeze(3).broadcast_to([P, GB, E, E])
                    nc.vector.tensor_tensor(gt[:], pj, pe_, ALU.is_gt)
                    inc(nc.vector.tensor_tensor(eq[:], pj, pe_, ALU.is_equal))
                if part == 2:
                    after()
                    inc(nc.vector.tensor_tensor(eq[:].rearrange("p b e j -> p b (e j)"), eq[:].rearrange("p b e j -> p b (e j)"),
                                                before[:].rearrange("p e j -> p (e j)").unsqueeze(1)
                                                .broadcast_to([P, GB, E * E]), ALU.mult))
                    after()
                    inc(nc.vector.tensor_tensor(gt[:], gt[:], eq[:], ALU.add))
                    after()
                    inc(nc.vector.tensor_reduce(pick[:], gt[:], X, ALU.add))
                if part == 3:
                    picked = comb[:, bass.ds(r * GB, GB), :]
                    after()
                    inc(nc.vector.scalar_tensor_tensor(out=p, in0=pick[:], scalar=2.0, in1=p,
                                                       op0=ALU.is_lt, op1=ALU.mult))
                    after()
                    inc(nc.vector.tensor_reduce(r4[:, 3], p, X, ALU.add))
                    after()
                    inc(nc.vector.tensor_scalar(r4[:, 0], r4[:, 3], 1e-9, None, ALU.add))
                    after()
                    inc(nc.vector.reciprocal(r4[:, 1], r4[:, 0]))
                    after()
                    assert done[0] == RV
                    nc.vector.tensor_tensor(picked, p, r4[:, 1].unsqueeze(2).broadcast_to(wide),
                                            ALU.mult).then_inc(t_cb, 1)

            def cur_rest(c, g):
                for k in range(KD):
                    dve.wait_ge(c_hi, KD * c + k + 1)
                    nc.vector.tensor_tensor(cur_lo[:, k], act_t[:, k, bass.ds(g * GT, GT)], cur_hi[:, k].bitcast(F32),
                                            ALU.subtract).then_inc(c_lo, 1)

            def residual_scale(r, j):
                dve.wait_ge(r_b, GB * (r + 1))
                nc.vector.tensor_tensor(gate[:, 2 * j:2 * j + 2], bank[6 + j][:].rearrange("p (b d) -> p b d", b=2),
                                        gate[:, 2 * j:2 * j + 2], ALU.mult).then_inc(r_mul, 1)

            def residual_add(r, g):
                for j in range(2):
                    xs = xres[:, bass.ds(g * GB + 2 * j, 2), :]
                    dve.wait_ge(r_mul, 2 * r + j + 1)
                    nc.vector.tensor_tensor(xs, xs, gate[:, 2 * j:2 * j + 2], ALU.add).then_inc(r_x, 1)

            def ada_vectors(chunks):
                for i, c in chunks:
                    for k in range(KD):
                        nc.vector.tensor_scalar(ada_t[:, i, k], bank[7][:, (i * KD + k) * B:(i * KD + k + 1) * B],
                                                ada_bt[:, c * KD + k:c * KD + k + 1], float(i % 2),
                                                ALU.add, ALU.add).then_inc(ada_s, 1)

            def split_part(c, i):
                lo, raw, hi = pair_part(c, i)
                dve.wait_ge(w_hi1, 3 * c + i + 1)
                nc.vector.tensor_tensor(lo, raw, hi.bitcast(F32), ALU.subtract).then_inc(w_lo1, 1)

            dve.wait_ge(d_x[0], 16)
            norm_stats(0)
            dve.wait_ge(n_bn, 1)
            norm_sums()
            norm_apply(0, 0)
            dve.wait_ge(ada_p, 1)
            dve.wait_ge(d_first, 48)
            ada_vectors(((0, 0), (1, 1)))
            dve.wait_ge(ada_s, 4)
            for k in range(KD):
                norm_ada(0, 0, k, 0, bank[k])

            def row_max(n, h):
                dve.wait_ge(a_sp, n + 1)
                nc.vector.tensor_reduce(nmax[:, h % 2], bank[3][:].rearrange("p (b s) -> p b s", b=GB), X, ALU.max,
                                        negate=True).then_inc(a_mx, 1)

            def p_t(n):
                dve.wait_ge(a_tp, n + 1)
                if not isinstance(n, int) or n >= 1:
                    dve.wait_ge(a_pvp, n)
                nc.vector.tensor_copy(pt1[:], bank[4][:]).then_inc(a_pt, 1)

            def row_inverse(n, h):
                dve.wait_ge(a_ex, n + 1)
                nc.vector.reciprocal(rinv[:, h % 2], rsum[:, h % 2]).then_inc(a_ri, 1)

            def o_lo(n, h):
                dve.wait_ge(a_oh, n + 1)
                nc.vector.scalar_tensor_tensor(out=o1_lo[:, h % 2], in0=bank[5][:], scalar=bqkv[:, 2, h:h + 1],
                                               in1=o1_hi[:, h % 2].bitcast(F32), op0=ALU.add,
                                               op1=ALU.subtract).then_inc(a_ol, 1)

            def attention1(g, first):
                for h in range(H):
                    n = g * H + h
                    job = background_norm(g, h, first)
                    past = background_norm(g, h - 1, first)
                    if h == 0:
                        cur_rest(g, g)
                    if past and past.part >= 2:
                        norm_ada(past.n, past.g, past.part - 2, past.kind, bank[4])
                    if job and job.part == 0:
                        if first:
                            dve.wait_ge(d_x[job.g], 16)
                        else:
                            dve.wait_ge(r_x, 2 * g)
                    if h >= 1 or not first:
                        row_max(n - 1, (h - 1) % 2)
                    if job and job.part == 0:
                        norm_stats(job.g)
                        dve.wait_ge(n_bn, job.n + 1)
                    if h >= 2 or not first:
                        p_t(n - 2)
                    if job and job.part == 0:
                        norm_sums()
                    if h >= 1 or not first:
                        row_inverse(n - 1, (h - 1) % 2)
                    dve.wait_ge(a_kp, n + 1)
                    if h >= 2 or not first:
                        dve.wait_ge(a_sp, n - 1)
                    nc.vector.tensor_scalar(k1[:, h % 2], bank[1][:], bqkv[:, 1, h:h + 1], None, ALU.add).then_inc(a_k, 1)
                    if first and h == 2:
                        dve.wait_ge(ada_p, 2)
                        dve.wait_ge(d_small, 16 * 4)
                        ada_vectors(((2, 3), (3, 4)))
                        nc.vector.tensor_tensor(gates[:], bank[6][0:B, :].rearrange("b (c d) -> b c d", c=2), ada_bg[:],
                                                ALU.add).then_inc(ada_s, 1)
                    if h >= 2 or not first:
                        o_lo(n - 2, (h - 2) % H)
                    if h == 1 and not first:
                        dve.wait_ge(a_op, n - 1)
                        residual_scale(g - 1, 0)
                        residual_scale(g - 1, 1)
                    if h == 2 and not first:
                        residual_add(g - 1, g - 1)
                    if job and job.part == 1:
                        norm_apply(job.n, job.g)
                    if first and h % 2 == 0 and 0 < h < H - 2:
                        for i in range(3):
                            split_part(h // 2 + 1, i)

            attention1(0, True)
            with dve.Fori(1, NG) as g:
                attention1(g, False)
            def split2(weights, half):
                lo, raw, hi = ((w1_lo, w1_raw, w1_hi), (w2_lo, w2_raw, w2_hi))[weights]
                fs = slice(half * NF // 2, (half + 1) * NF // 2)
                dve.wait_ge(w_hi2, 2 * weights + half + 1)
                dve.wait_ge(w_lo2, 1)
                nc.vector.tensor_tensor(lo[:, fs], raw[:, fs], hi[:, fs].bitcast(F32), ALU.subtract).then_inc(w_lo2, 1)

            def split3(c):
                for i, (lo, hi, raw, w) in enumerate(((wkv_lo, wkv_hi, wkv_raw, 256), (wq_lo, wq_hi, wq_raw, 512))):
                    cols = bass.ds(c * w, w)
                    dve.wait_ge(w_hi3, 2 * c + i + 1)
                    nc.vector.tensor_tensor(lo[:, :, cols], raw[:, :, cols], hi[:, :, cols].bitcast(F32),
                                            ALU.subtract).then_inc(w_lo3, 1)

            def split_out(c):
                tiles = bass.ds(c * 4, 4)
                dve.wait_ge(w_ohi3, c + 1)
                nc.vector.tensor_tensor(wo2_lo[:, tiles], wo2_raw[:, tiles], wo2_hi[:, tiles].bitcast(F32),
                                        ALU.subtract).then_inc(w_olo3, 1)

            n = NG * H
            row_max(n - 1, 1)
            cur_rest(NG, 0)
            p_t(n - 2)
            row_inverse(n - 1, 1)
            o_lo(n - 2, H - 2)
            split2(0, 1)
            p_t(n - 1)
            split2(1, 0)
            o_lo(n - 1, H - 1)

            def h_rest(m, f, first):
                dve.wait_ge(f_h, m + 1)
                if f >= 2 or not first:
                    dve.wait_ge(f_dp, m - 1)
                elif f == 0:
                    dve.wait_ge(a_pvp, n - 2)
                nc.vector.tensor_tensor(h_lo[:, f % 2], hf[:, f % 2], h_hi[:, f % 2].bitcast(F32),
                                        ALU.subtract).then_inc(f_l, 1)

            def ffn1(g, first):
                done = NG - 1 if first else g - 1
                for f in range(NF):
                    m = g * NF + f
                    if f == 0 and not first:
                        cur_rest(NG + g, g)
                    if f == 4:
                        dve.wait_ge(n_bn, 2 * NG + g)
                    if f == 2:
                        if first:
                            dve.wait_ge(a_op, n)
                        else:
                            dve.wait_ge(f_dp, m - 2)
                        residual_scale(NG + g - 1, 0)
                        residual_scale(NG + g - 1, 1)
                    if f >= 1 or not first:
                        h_rest(m - 1, (f - 1) % NF, first)
                    if f == 1 and first:
                        split2(1, 1)
                    if f == 2:
                        residual_add(NG + g - 1, done)
                        dve.wait_ge(r_x, 2 * (NG + g))
                    if f == 4:
                        norm_sums()
                        if not first:
                            split_out(g - 1)
                    if f == 3:
                        norm_stats(done)
                    if f == 5 and first:
                        norm_apply(2 * NG - 1, done)
                    if f == 5 and not first:
                        norm_apply_rms(2 * NG + g - 1, done)
                    if f == 6:
                        split3(g)
                        if first:
                            dve.wait_ge(d_rope, 32)
                            for i in range(4):
                                nc.vector.scalar_tensor_tensor(out=rope[:, i], in0=rope[:, i], scalar=SCALE if i < 2 else 1.0,
                                                               in1=cos_sin[:, i % 2], op0=ALU.mult,
                                                               op1=ALU.mult).then_inc(g_tab, 1)
                            dve.wait_ge(g_mask, 2)
                            nc.vector.tensor_copy(mask[:].rearrange("p (j s) -> p j s", j=REP),
                                                  mask_f[:].unsqueeze(1).broadcast_to([P, REP, T])).then_inc(g_tab, 1)
                            nc.vector.tensor_copy(ident_b[:], ident[:]).then_inc(g_tab, 1)
                    if f == 7:
                        for k in range(KD):
                            if first:
                                norm_ada(2 * NG - 1, done, k, 1, bank[2 + k])
                            else:
                                norm_weight(2 * NG + g - 1, done, k, 0, bank[2 + k])

            ffn1(0, True)
            with dve.Fori(1, NG) as g:
                ffn1(g, False)
            dve.wait_ge(g_tab, 6)

            def rotate(out_cos, out_sin, src, table, cos_free, sin_free, done):
                heads = src.rearrange("p (h d) -> p h d", d=DH)
                for sem_, value in cos_free:
                    dve.wait_ge(sem_, value)
                nc.vector.tensor_tensor(out_cos.rearrange("p (h d) -> p h d", d=DH), heads,
                                        rope[:, table].unsqueeze(1).broadcast_to([P, 4, DH]), ALU.mult)
                for sem_, value in sin_free:
                    dve.wait_ge(sem_, value)
                nc.vector.tensor_tensor(out_sin.rearrange("p (h c d) -> p h c d", c=2, d=DH // 2),
                                        src.rearrange("p (h c d) -> p h c d", c=2, d=DH // 2)[:, :, ::-1, :],
                                        rope[:, table + 1].rearrange("p (c d) -> p c d", c=2).unsqueeze(1)
                                        .broadcast_to([P, 4, 2, DH // 2]), ALU.mult).then_inc(done, 1)

            def step(s):
                n, new_seq, prev = s.n, s.new() and s.kv == 0, 3 * NG + s.g - 1
                done = NG - 1 if s.first else s.g - 1
                if s.u == 0:
                    cur_rest(2 * NG + s.g, s.g)
                if s.first and s.u == 0:
                    dve.wait_ge(r_b, GB * 2 * NG)
                    h_rest(NG * NF - 1, NF - 1, False)
                if s.first and s.u == 2:
                    dve.wait_ge(f_dp, NG * NF)
                    residual_scale(2 * NG - 1, 0)
                    residual_scale(2 * NG - 1, 1)
                if s.first and s.u == 5:
                    residual_add(2 * NG - 1, NG - 1)
                if s.first and s.u == 14:
                    dve.wait_ge(m_sel, 2)
                if s.u == 7:
                    if s.first:
                        dve.wait_ge(r_x, 4 * NG)
                    else:
                        dve.wait_ge(g_x, GB * s.g)
                if s.live(3):
                    dve.wait_ge(g_sp, n - 2)
                    nc.vector.tensor_reduce(nmax[:, (s.u - 3) % 2], bank[3][:].rearrange("p (j s) -> p j s", j=REP), X,
                                            ALU.max, negate=True).then_inc(g_mx, 1)
                    dve.wait_ge(g_rq, n - 2)
                    dve.wait_ge(g_mx, n - 2)
                    nc.vector.tensor_tensor(nb[:, (s.u - 3) % 2], nmax[:, (s.u - 3) % 2], rq[:, (s.u - 3) % 4],
                                            ALU.mult).then_inc(g_nb, 1)
                if s.u == 7:
                    norm_stats(done)
                if new_seq:
                    free = [(g_ktp, s.seq)] if s.had(4) else []
                    rotate(kr[:], kb[:], bank[1][:], 2, [(g_kp, s.seq + 1)] + free, free, g_kb)
                if s.u == 7:
                    dve.wait_ge(n_bn, prev + 1)
                if s.new() and s.kv == 1:
                    dve.wait_ge(g_rk, s.seq + 1)
                    dve.wait_ge(g_ka, s.seq + 1)
                    kh = kr[:].rearrange("p (h d) -> p h d", d=DH)
                    nc.vector.tensor_tensor(kh, kh, rk[:].unsqueeze(2).broadcast_to([P, HKV, DH]),
                                            ALU.mult).then_inc(g_kr, 1)
                if s.u == 12 and not s.first:
                    routing_part(s.g - 1, 0, bank[2])
                if s.new():
                    rotate(qr[:, s.u % 2], rb[:], bank[0][:], 0,
                           [(g_qp, n + 1)] + ([(g_qtp, n - 1)] if s.had(2) else []),
                           [(g_qr, n)] if s.had(1) else [], g_qb)
                if s.live(3):
                    dve.wait_ge(g_ex, n - 2)
                    nc.vector.reciprocal(rinv[:, (s.u - 3) % 2], rsum[:, (s.u - 3) % 2]).then_inc(g_ri, 1)
                if s.u == 7:
                    norm_sums()
                if new_seq:
                    dve.wait_ge(g_ksq, s.seq + 1)
                    nc.vector.tensor_reduce(k_ms[:], ksq[:].rearrange("p (h d) -> p h d", d=DH), X,
                                            ALU.add).then_inc(g_ks, 1)
                if s.new():
                    dve.wait_ge(g_sq, n + 1)
                    if s.had(2):
                        dve.wait_ge(g_rq, n - 1)
                    nc.vector.tensor_reduce(q_ms[:, s.u % 2], sq[:].rearrange("p (h d) -> p h d", d=DH), X,
                                            ALU.add).then_inc(g_ss, 1)
                if s.live(5):
                    dve.wait_ge(g_oh, n - 4)
                    nc.vector.tensor_tensor(o2_lo[:], bank[6][:], o2_hi[:].bitcast(F32), ALU.subtract).then_inc(g_ol, 1)
                if s.kv == 1 and s.had(9):
                    dve.wait_ge(g_op, 4 * (s.seq - 1))
                    xs = xres[:, bass.ds(s.seq - 2, 1), :].rearrange("p a d -> p (a d)")
                    nc.vector.tensor_tensor(xs, xs, bank[7][:, 0:D], ALU.add).then_inc(g_x, 1)
                if s.live(4):
                    dve.wait_ge(g_ph, n - 3)
                    nc.vector.tensor_tensor(pt_lo[:], bank[5][:], pt_hi[:].bitcast(F32), ALU.subtract).then_inc(g_pl, 1)
                if new_seq:
                    dve.wait_ge(g_vh, s.seq + 1)
                    nc.vector.tensor_tensor(v_lo[:, s.b % 2], bank[2][:], v_hi[:, s.b % 2].bitcast(F32),
                                            ALU.subtract).then_inc(g_vl, 1)
                if s.u == 9:
                    norm_apply_rms(prev, done)
                if s.u == 10:
                    for k in range(KD):
                        norm_weight(prev, done, k, 0 if s.first else 1, bank[1 + k])
                if s.u == 16:
                    routing_part(0, 1)
                if s.u == 17:
                    routing_part(0, 2)
                    routing_part(0, 3)
                if s.first and s.u == 3:
                    split_out(NG - 1)
                if s.first and s.u >= WG_STEP:
                    t = s.u - WG_STEP
                    dve.wait_ge(w_hi4, t + 1)
                    nc.vector.tensor_tensor(wg_lo[:, t], wg_raw[:, t], wg_hi[:, t].bitcast(F32),
                                            ALU.subtract).then_inc(w_lo4, 1)
                if s.u == 4 * GB + 1:
                    cur_rest(3 * NG, 0)
                if late_chunk(s.u):
                    which, c, tiles = late_chunk(s.u)
                    lo, raw, hi = ((wu_lo, wu_raw, wu_hi), (wd_lo, wd_raw, wd_hi))[which]
                    dve.wait_ge(w_hi4, NR + 3 * which + c + 1)
                    nc.vector.tensor_tensor(lo[:, tiles], raw[:, tiles], hi[:, tiles].bitcast(F32),
                                            ALU.subtract).then_inc(w_lo4, 1)

            attention2(dve, step)
            def e_rest(n, i):
                dve.wait_ge(m_h, n + 1)
                nc.vector.tensor_tensor(e_lo[:, i % 2], em[:, i % 2], e_hi[:, i % 2].bitcast(F32),
                                        ALU.subtract).then_inc(m_l, 1)

            def experts(g, first):
                last_norm = 4 * NG - 1
                for i in range(NR):
                    n = g * NR + i
                    if i == 0:
                        if not first:
                            cur_rest(3 * NG + g, g)
                    if i >= 1 or not first:
                        e_rest(n - 1, (i - 1) % NR)
                    dve.wait_ge(m_sg, n + 1)
                    dve.wait_ge(m_up, n + 1)
                    nc.vector.tensor_tensor(sg[:, i % 2], sg[:, i % 2], bank[2 + i % 2][:], ALU.mult).then_inc(m_su, 1)
                    if i == 1 and not first:
                        result(g - 1)
                    dve.wait_ge(d_cw[i], 16 * len(segments(i)) * (g + 1))
                    dve.wait_ge(m_su, n + 1)
                    if i >= 2 or not first:
                        dve.wait_ge(m_l, n - back(i) + 1)
                    nc.vector.tensor_tensor(em[:, i % 2], sg[:, i % 2], cw[i][:], ALU.mult).then_inc(m_em, 1)
                    if i == 3 and not first:
                        result_input(g - 1)
                    if first and i == 1:
                        dve.wait_ge(g_x, B)
                        norm_stats(NG - 1)
                        dve.wait_ge(n_bn, 4 * NG)
                        norm_sums()
                    if first and i == 2:
                        norm_apply_rms(last_norm, NG - 1)
                    if first and i in (3, 4):
                        norm_weight(last_norm, NG - 1, i - 3, 1, bank[5])
                    if first and 1 <= i <= 3 * (NG - 2):
                        routing_part(1 + (i - 1) // 3, 1 + (i - 1) % 3)
                    if first and i == 6:
                        routing_part(NG - 1, 0, bank[5])
                    if first and i == 8:
                        routing_part(NG - 1, 1)
                    if first and i == 9:
                        routing_part(NG - 1, 2)
                        routing_part(NG - 1, 3)

            def result(g):
                dve.wait_ge(m_dp, NR * (g + 1))
                if not isinstance(g, int) or g >= 1:
                    dve.wait_ge(d_out, 16 * g)
                for j in range(2):
                    nc.vector.tensor_tensor(y[:, 2 * j:2 * j + 2], bank[6 + j][:].rearrange("p (b d) -> p b d", b=2),
                                            xres[:, bass.ds(g * GB + 2 * j, 2), :], ALU.add).then_inc(m_y, 1)

            def result_input(g):
                dve.wait_ge(d_xin, 16 * (g + 1))
                dve.wait_ge(m_y, 4 * g + 2)
                for j in range(2):
                    nc.vector.tensor_tensor(y[:, 2 * j:2 * j + 2], y[:, 2 * j:2 * j + 2], x0[:, 2 * j:2 * j + 2],
                                            ALU.add).then_inc(m_y, 1)

            experts(0, True)
            with dve.Fori(1, NG) as g:
                experts(g, False)
            e_rest(NG * NR - 1, NR - 1)
            result(NG - 1)
            result_input(NG - 1)

        @block.tensor
        def _(pe):
            def norm_transposes(n, k, dst):
                for b in range(GB):
                    last = pe.transpose(dst[:, b * T:(b + 1) * T], xn[:, b, k * P:(k + 1) * P], ident[:])
                last.then_inc(n_tp, 1)

            def ada_columns(chunks):
                for i, c in chunks:
                    for k in range(KD):
                        for j in range(KD):
                            last = pe.matmul(bank[7][:, (i * KD + k) * B:(i * KD + k + 1) * B],
                                             ada_w[:, j, c * D + k * P:c * D + (k + 1) * P], cond_t[:, j],
                                             start=(j == 0), stop=(j == KD - 1))
                return last

            pe.wait_ge(d_first, 48)
            pe.wait_ge(d_ada1, 16)
            ada_columns(((0, 0), (1, 1))).then_inc(ada_p, 1)
            pe.wait_ge(consts, 4)
            pe.wait_ge(n_xn, 1)
            for k in range(KD):
                norm_transposes(0, k, bank[k])

            def input_tile(c, k):
                if c is not None:
                    pe.wait_ge(c_lo, KD * c + k + 1)

            def project(dst, h, c, new=None):
                for k in range(KD):
                    input_tile(new, k)
                    for i, (l, r) in enumerate(split_products(wqk_hi[:, h, c, k], wqk_lo[:, h, c, k],
                                                              cur_hi[:, k], cur_lo[:, k])):
                        last = pe.matmul(dst, l, r, start=(k == 0 and i == 0), stop=(k == KD - 1 and i == 2))
                return last

            def scores(n, h):
                pe.wait_ge(a_k, n + 1)
                pe.wait_ge(a_q, n + 1)
                if not isinstance(n, int) or n >= 1:
                    pe.wait_ge(a_ex, n)
                for b in range(GB):
                    bs = slice(b * T, (b + 1) * T)
                    last = pe.matmul(bank[3][:, bs], q1[:, h % 2, bs], k1[:, h % 2, bs], start=True, stop=True)
                last.then_inc(a_sp, 1)

            def p_transposes(n, h):
                pe.wait_ge(a_pn, n + 1)
                if not isinstance(n, int) or n >= 1:
                    pe.wait_ge(a_pt, n)
                for b in range(GB):
                    last = pe.transpose(bank[4][:, b * T:(b + 1) * T], p1[:, h % 2, b], ident[:])
                last.then_inc(a_tp, 1)

            def values_product(n, h):
                pe.wait_ge(a_pt, n + 1)
                pe.wait_ge(a_v, n - h % 2 + 2)
                if not isinstance(n, int) or n >= 1:
                    pe.wait_ge(a_ol, n)
                for b in range(GB):
                    bs = slice(b * T, (b + 1) * T)
                    last = pe.matmul(bank[5][:, bs], v1[:, h // 2 % 2, b, h % 2 * DH:h % 2 * DH + DH], pt1[:, bs],
                                     start=True, stop=True)
                last.then_inc(a_pvp, 1)

            def down(banks, lhs_hi, lhs_lo, rhs_hi, rhs_lo, first, last_one):
                for b in range(GB):
                    bs = slice(b * T, (b + 1) * T)
                    for i, (l, r) in enumerate(split_products(lhs_hi[:, bs], lhs_lo[:, bs], rhs_hi, rhs_lo)):
                        last = pe.matmul(bank[banks[b // 2]][:, b % 2 * D:b % 2 * D + D], l, r,
                                         start=(first and b % 2 == 0 and i == 0), stop=(last_one and i == 2),
                                         skip_group_check=True)
                return last

            def out_product(n, h):
                pe.wait_ge(a_ol, n + 1)
                down((6, 7), o1_hi[:, h % 2], o1_lo[:, h % 2], wo_hi[:, h], wo_lo[:, h],
                     h == 0, h == H - 1).then_inc(a_op, 1)

            def attention1(g, first):
                for h in range(H):
                    n = g * H + h
                    job = background_norm(g, h, first)
                    past = background_norm(g, h - 1, first)
                    if h == 0:
                        if not first:
                            p_transposes(n - 2, 0)
                    if first and h % 2 == 0:
                        pe.wait_ge(*lo1(h // 2, 0))
                    if h >= 1 or not first:
                        pe.wait_ge(a_q, n)
                    project(bank[0][:], h, 0, g if h == 0 else None).then_inc(a_qp, 1)
                    ps = slice(h // 2 * 2 * DH, (h // 2 + 1) * 2 * DH)

                    def pair_values(j):
                        bs = slice((h % 2 * 2 + j) * T, (h % 2 * 2 + j + 1) * T)
                        for k in range(KD):
                            for i, (l, r) in enumerate(split_products(cur_hi[:, k, bs], cur_lo[:, k, bs],
                                                                      wv_hi[:, k, ps], wv_lo[:, k, ps])):
                                last = pe.matmul(bank[2][:, j * 2 * DH:(j + 1) * 2 * DH], l, r,
                                                 start=(k == 0 and i == 0), stop=(k == KD - 1 and i == 2))
                        return last

                    late = past and past.part >= 2
                    if late:
                        if first and h % 2 == 0:
                            pe.wait_ge(*lo1(h // 2, 1))
                        pe.wait_ge(a_v, n)
                        pair_values(0)
                        pe.wait_ge(n_ev, 2 * past.n + past.part - 1)
                        p_transposes(n - 2, h % 2)
                    if h >= 1 and (h >= 2 or not first) and not late:
                        p_transposes(n - 2, h % 2)
                    if h >= 1 or not first:
                        pe.wait_ge(a_k, n)
                    project(bank[1][:], h, 1).then_inc(a_kp, 1)
                    if h >= 2 or not first:
                        values_product(n - 2, (h - 2) % H)
                    if not late:
                        if first and h % 2 == 0:
                            pe.wait_ge(*lo1(h // 2, 1))
                        if h >= 1 or not first:
                            pe.wait_ge(a_v, n)
                        pair_values(0)
                    pair_values(1).then_inc(a_vp, 1)
                    scores(n, h)
                    if first and h == 1:
                        pe.wait_ge(d_ada2, 16)
                        ada_columns(((2, 3), (3, 4)))
                        for i, c in enumerate((2, 5)):
                            for j in range(KD):
                                last = pe.matmul(bank[6][0:B, i * D:(i + 1) * D], cond_t[:, j],
                                                 ada_w[:, j, c * D:(c + 1) * D], start=(j == 0), stop=(j == KD - 1))
                        last.then_inc(ada_p, 1)
                    if h >= 2 or not first:
                        if first and h % 2 == 0:
                            pe.wait_ge(*lo1(h // 2 - 1, 2))
                        if first and h == 2:
                            pe.wait_ge(ada_s, 9)
                        if h == 2 and not first:
                            pe.wait_ge(r_mul, 2 * g)
                        out_product(n - 2, (h - 2) % H)
                    if job and job.part >= 2:
                        if job.part == 2:
                            pe.wait_ge(n_xn, job.n + 1)
                        pe.wait_ge(a_pt, n - 1)
                        norm_transposes(job.n, job.part - 2, bank[4])

            attention1(0, True)
            with pe.Fori(1, NG) as g:
                attention1(g, False)
            def ffn_up(m, f, first, new=None):
                if f >= 2 or not first:
                    pe.wait_ge(f_g, m - 1)
                for k in range(KD):
                    input_tile(new, k)
                    for i, (l, r) in enumerate(split_products(w1_hi[:, f, k], w1_lo[:, f, k], cur_hi[:, k], cur_lo[:, k])):
                        last = pe.matmul(bank[f % 2][:], l, r, start=(k == 0 and i == 0), stop=(k == KD - 1 and i == 2))
                last.then_inc(f_up, 1)

            def ffn_down(m, f):
                pe.wait_ge(f_l, m + 1)
                down((6, 7), h_hi[:, f % 2], h_lo[:, f % 2], w2_hi[:, f], w2_lo[:, f], f == 0, f == NF - 1).then_inc(f_dp, 1)

            n = NG * H
            p_transposes(n - 2, H - 2)
            values_product(n - 2, H - 2)
            pe.wait_ge(w_lo2, 1)
            pe.wait_ge(a_q, n)
            ffn_up(0, 0, True, NG)
            out_product(n - 2, H - 2)
            p_transposes(n - 1, H - 1)
            values_product(n - 1, H - 1)
            pe.wait_ge(a_k, n)
            ffn_up(1, 1, True)
            out_product(n - 1, H - 1)

            def ffn1(g, first):
                for f in range(2 if first else 0, NF):
                    m = g * NF + f
                    if f == 0:
                        ffn_down(m - 2, NF - 2)
                    if f == 4 and first:
                        pe.wait_ge(w_lo2, 2)
                    ffn_up(m, f, first, NG + g if f == 0 else None)
                    if f == 6 and first:
                        pe.wait_ge(w_lo2, 4)
                    if f == 3:
                        if first:
                            pe.wait_ge(w_lo2, 3)
                        pe.wait_ge(r_mul, 2 * (NG + g))
                        ffn_down(m - 3, 0)
                    if f == 1 or f >= 3:
                        ffn_down(m - 2, (f - 2) % NF)
                    if f == 6:
                        pe.wait_ge(n_xn, 2 * NG + g)
                        if first:
                            pe.wait_ge(a_v, n)
                            pe.wait_ge(a_ex, n)
                        pe.wait_ge(n_ev, 2 * (2 * NG + g - 1))
                        for k in range(KD):
                            norm_transposes(2 * NG + g - 1, k, bank[2 + k])

            ffn1(0, True)
            with pe.Fori(1, NG) as g:
                ffn1(g, False)

            def token_product(dst, seq, w_hi, w_lo, cols, new=None):
                bs = slice(seq * T, (seq + 1) * T)
                for k in range(KD):
                    input_tile(new, k)
                    for i, (l, r) in enumerate(split_products(cur_hi[:, k, bs], cur_lo[:, k, bs],
                                                              w_hi[:, k, cols], w_lo[:, k, cols])):
                        last = pe.matmul(dst, l, r, start=(k == 0 and i == 0), stop=(k == KD - 1 and i == 2))
                return last

            def router_product(r, dst):
                pe.wait_ge(d_rw, 16)
                pe.wait_ge(n_ev, 2 * (3 * NG + r + 1))
                for k in range(KD):
                    last = pe.matmul(dst[0:E, :], rw[:, k], act_t[:, k, bass.ds(r * GT, GT)], start=(k == 0), stop=(k == KD - 1))
                last.then_inc(t_lp, 1)

            def router_transposes(r, dst):
                for b in range(GB):
                    last = pe.transpose(dst[:, b * E:(b + 1) * E], lt[:, b * T:(b + 1) * T], ident[0:E, 0:E])
                last.then_inc(t_ltp, 1)

            def combination_transposes(g):
                pe.wait_ge(t_cb, g + 1)
                for b in range(GB):
                    last = pe.transpose(bank[4][0:E, b * T:(b + 1) * T], comb[:, g * GB + b, :], ident[:])
                last.then_inc(t_ctp, 1)

            def inner_product(g, i, u, first, new=None):
                dst, w_hi, w_lo, done, read = ((bank[i % 2], wg_hi, wg_lo, m_gp, m_sg),
                                               (bank[2 + i % 2], wu_hi, wu_lo, m_up, m_su))[u]
                if i >= 2 or not first:
                    pe.wait_ge(read, g * NR + i - back(i) + 1)
                if first and u == 1 and i % 4 == 0:
                    pe.wait_ge(w_lo4, NR + i // 4 + 1)
                for k in range(KD):
                    input_tile(new, k)
                    for j, (l, r) in enumerate(split_products(w_hi[:, i, k], w_lo[:, i, k], cur_hi[:, k], cur_lo[:, k])):
                        last = pe.matmul(dst[:], l, r, start=(k == 0 and j == 0), stop=(k == KD - 1 and j == 2))
                last.then_inc(done, 1)

            def step(s):
                n, new_seq = s.n, s.new() and s.kv == 0
                def keys_queries():
                    if new_seq:
                        if s.had(4):
                            pe.wait_ge(g_kt, s.seq)
                        if s.u == 12:
                            pe.wait_ge(n_ev, 2 * (3 * NG + s.g))
                        token_product(bank[1][:], s.b, wkv_hi, wkv_lo, slice(0, HKV * DH),
                                      2 * NG + s.g if s.u == 0 else None).then_inc(g_kp, 1)
                    if s.new():
                        if s.had(1):
                            pe.wait_ge(g_qb, n)
                            pe.wait_ge(g_sq, n)
                        if s.u == 12 and not s.first:
                            pe.wait_ge(t_lt, s.g)
                        token_product(bank[0][:], s.b, wq_hi, wq_lo,
                                      slice(s.kv * REP * DH, (s.kv + 1) * REP * DH)).then_inc(g_qp, 1)
                    if s.u == 12 and not s.first:
                        router_transposes(s.g - 1, bank[2])

                def output_product():
                    if not s.live(6):
                        return
                    kv = (s.u - 6) % HKV
                    if s.first and s.u == 6:
                        pe.wait_ge(w_olo3, NG)
                    pe.wait_ge(g_ol, n - 5)
                    if kv == 0 and s.had(10):
                        pe.wait_ge(g_x, s.seq - 1)
                    for j in range(REP):
                        js = slice(j * T, (j + 1) * T)
                        for i, (l, r) in enumerate(split_products(o2_hi[:, js], o2_lo[:, js],
                                                                  wo2_hi[:, kv * REP + j], wo2_lo[:, kv * REP + j])):
                            last = pe.matmul(bank[7][:, 0:D], l, r, start=(kv == 0 and j == 0 and i == 0),
                                             stop=(kv == HKV - 1 and j == REP - 1 and i == 2))
                    last.then_inc(g_op, 1)

                def values():
                    if not new_seq:
                        return
                    if s.had(4):
                        pe.wait_ge(g_vl, s.seq)
                    if s.u == 12 and not s.first:
                        pe.wait_ge(t_v0, 2 * s.g)
                    token_product(bank[2][:], s.b, wkv_hi, wkv_lo, slice(HKV * DH, 2 * HKV * DH)).then_inc(g_vp, 1)

                def weighted_values():
                    if not s.live(5):
                        return
                    kv, slot = (s.u - 5) % HKV, (s.u - 5) // HKV % 2
                    pe.wait_ge(g_pl, n - 4)
                    pe.wait_ge(g_vl, s.g * GB + (s.u - 5) // HKV + 1)
                    if s.had(6):
                        pe.wait_ge(g_ol, n - 5)
                    else:
                        pe.wait_ge(r_mul, 2 * 2 * NG)
                    ks = slice(kv * DH, (kv + 1) * DH)
                    for i, (l, r) in enumerate(split_products(v_hi[:, slot, ks], v_lo[:, slot, ks], pt_hi[:], pt_lo[:])):
                        last = pe.matmul(bank[6][:], l, r, start=(i == 0), stop=(i == 2))
                    last.then_inc(g_pvp, 1)

                if s.u == 0 and not s.first:
                    output_product()
                    weighted_values()
                    keys_queries()
                    values()
                else:
                    if s.u == 0:
                        ffn_down(NG * NF - 2, NF - 2)
                        pe.wait_ge(w_lo3, 8)
                        pe.wait_ge(f_g, NG * NF)
                        pe.wait_ge(n_ev, 2 * (3 * NG - 1))
                    keys_queries()
                    output_product()
                    if s.u == 12:
                        weighted_values()
                        values()
                    else:
                        values()
                        if s.first and s.u == 0:
                            ffn_down(NG * NF - 1, NF - 1)
                        weighted_values()
                if s.u == 11 and not s.first:
                    router_product(s.g - 1, bank[2])
                if s.live(1):
                    pe.wait_ge(g_qr, n)
                    if s.had(2):
                        pe.wait_ge(g_qt, n - 1)
                    for j in range(REP):
                        last = pe.transpose(bank[4][:, j * T:(j + 1) * T],
                                            qr[:, (s.u - 1) % 2, j * DH:(j + 1) * DH], ident[:])
                    last.then_inc(g_qtp, 1)
                if s.live(4):
                    pe.wait_ge(g_pn, n - 3)
                    if s.had(5):
                        pe.wait_ge(g_pl, n - 4)
                    for j in range(REP):
                        last = pe.transpose(bank[5][:, j * T:(j + 1) * T], p2[:, (s.u - 4) % 2, j], ident[:])
                    last.then_inc(g_tp, 1)
                if s.new() and s.kv == 1:
                    pe.wait_ge(g_kr, s.seq + 1)
                    for j in range(HKV):
                        last = pe.transpose(bank[1][:, j * T:(j + 1) * T], kr[:, j * DH:(j + 1) * DH], ident[:])
                    last.then_inc(g_ktp, 1)
                if s.u == 10:
                    pe.wait_ge(n_xn, 3 * NG + s.g)
                    pe.wait_ge(g_kt, s.g * GB + 3)
                    pe.wait_ge(g_vl, s.g * GB + 3)
                    for k in range(KD):
                        norm_transposes(3 * NG + s.g - 1, k, bank[1 + k])
                if s.live(2):
                    kv, slot = (s.u - 2) % HKV, (s.u - 2) // HKV % 2
                    pe.wait_ge(g_qt, n - 1)
                    pe.wait_ge(g_kt, s.g * GB + (s.u - 2) // HKV + 1)
                    if s.had(3):
                        pe.wait_ge(g_ex, n - 2)
                    pe.matmul(bank[3][:], ident_b[:], mask[:], start=True, stop=False, skip_group_check=True)
                    for j in range(REP):
                        js = slice(j * T, (j + 1) * T)
                        last = pe.matmul(bank[3][:, js], q_t[:, s.u % 2, js], k_t[:, slot, kv * T:(kv + 1) * T],
                                         start=False, stop=(j == REP - 1), skip_group_check=True)
                    last.then_inc(g_sp, 1)
                if s.u == 4 * GB + 2:
                    pe.wait_ge(g_qt, NG * 4 * GB)
                    combination_transposes(0)
                    pe.wait_ge(w_lo4, NR)
                    pe.wait_ge(g_qb, NG * 4 * GB)
                    pe.wait_ge(g_sq, NG * 4 * GB)
                    inner_product(0, 0, 0, True, 3 * NG)
                if s.u == 4 * GB + 3:
                    pe.wait_ge(g_vl, B)
                    inner_product(0, 0, 1, True)
                if s.u == 4 * GB + 4:
                    pe.wait_ge(g_kt, B)
                    inner_product(0, 1, 0, True)
                if s.u == 4 * GB + 5:
                    pe.wait_ge(g_ex, NG * 4 * GB)
                    inner_product(0, 1, 1, True)

            attention2(pe, step)

            def expert_down(n, i):
                pe.wait_ge(m_l, n + 1)
                down((6, 7), e_hi[:, i % 2], e_lo[:, i % 2], wd_hi[:, i], wd_lo[:, i], i == 0, i == NR - 1).then_inc(m_dp, 1)

            def experts(g, first):
                for i in range(NR):
                    n = g * NR + i
                    if i == 0:
                        if first:
                            pe.wait_ge(g_pl, NG * 4 * GB)
                            pe.wait_ge(g_ol, NG * 4 * GB)
                            pe.wait_ge(g_x, B)
                        else:
                            expert_down(n - 2, NR - 2)
                    if i >= 2 or not first:
                        inner_product(g, i, 0, first, 3 * NG + g if i == 0 else None)
                        inner_product(g, i, 1, first)
                    if first and i >= 2 and (i - 2) % 4 == 0:
                        pe.wait_ge(w_lo4, NR + 3 + (i - 2) // 4 + 1)
                    if i == 3 and not first:
                        pe.wait_ge(m_y, 4 * g - 2)
                        expert_down(n - 3, 0)
                    if i >= (2 if first else 3) or (i == 1 and not first):
                        expert_down(n - 2, (i - 2) % NR)
                    if first and i in (5, 8, 10):
                        r = (5, 8, 10).index(i) + 1
                        pe.wait_ge(t_ct, r)
                        combination_transposes(r)
                    if first and i in (3, 4):
                        if i == 3:
                            pe.wait_ge(n_xn, 4 * NG)
                        else:
                            pe.wait_ge(n_ev, 2 * 4 * NG - 1)
                        norm_transposes(4 * NG - 1, i - 3, bank[5])
                    if first and i == 5:
                        router_product(NG - 1, bank[5])
                    if first and i == 6:
                        pe.wait_ge(t_lt, NG)
                        router_transposes(NG - 1, bank[5])
                    if first and i == 9:
                        pe.wait_ge(t_v0, 2 * NG)

            experts(0, True)
            with pe.Fori(1, NG) as g:
                experts(g, False)
            expert_down(NG * NR - 2, NR - 2)
            expert_down(NG * NR - 1, NR - 1)


def layout(a):
    import numpy as np
    freqs = (1.0 / np.float32(1000000.0) ** (np.arange(0, DH, 2, dtype=np.float32) / np.float32(DH))).astype(np.float32)
    angle = np.outer(np.arange(T, dtype=np.float32), freqs).astype(np.float32)
    cos, sin = np.cos(angle), np.sin(angle)
    cos_sin = np.stack([np.concatenate([cos, cos], 1), np.concatenate([-sin, sin], 1)], 1).astype(np.float32)
    qw, kw = a["L0_ffn_q_norm_w"], a["L0_ffn_k_norm_w"]
    rows = lambda w: w.T.reshape(KD, P, -1).transpose(1, 0, 2)
    tiles = lambda w: w.reshape(E * I, D).T.reshape(KD, P, NR, P).transpose(1, 2, 0, 3)
    qkv = a["L0_cond_qkv_w"].reshape(KD, P, 3, H, DH)
    return {
        "x": a["x"],
        "cond_t": a["cond_2048"].T.reshape(KD, P, B).transpose(1, 0, 2),
        "ada_w": a["L0_cond_ada_w"].reshape(KD, P, 6 * D).transpose(1, 0, 2),
        "ada_bt": a["L0_cond_ada_b"].reshape(12, P).T,
        "ada_bg": np.broadcast_to(a["L0_cond_ada_b"].reshape(6, D)[[2, 5]], (B, 2, D)),
        "wqk": qkv[:, :, 0:2].transpose(1, 3, 2, 0, 4),
        "wv": qkv[:, :, 2].reshape(KD, P, H * DH).transpose(1, 0, 2),
        "wo": a["L0_cond_out_w"].reshape(H, DH, D).transpose(1, 0, 2),
        "bqkv": a["L0_cond_qkv_b"].reshape(3, H, DH).transpose(2, 0, 1),
        "out_b": a["L0_cond_out_b"],
        "w1": a["L0_cond_ffn_w1"].reshape(KD, P, NF, P).transpose(1, 2, 0, 3),
        "b1": a["L0_cond_ffn_b1"].reshape(NF, P).T,
        "w2": a["L0_cond_ffn_w2"].reshape(NF, P, D).transpose(1, 0, 2),
        "b2": a["L0_cond_ffn_b2"],
        "wq": rows(a["L0_ffn_q_w"]),
        "wkv": rows(np.concatenate([a["L0_ffn_k_w"], a["L0_ffn_v_w"]], 0)),
        "wo2": a["L0_ffn_o_w"].T.reshape(H, DH, D).transpose(1, 0, 2),
        "qk_norm": np.stack([qw, np.roll(qw, DH // 2), kw, np.roll(kw, DH // 2)]),
        "cos_sin": cos_sin,
        "rw": rows(a["L0_ffn_gate_w"]),
        "wg": tiles(a["L0_ffn_wg"]),
        "wu": tiles(a["L0_ffn_wu"]),
        "wd": a["L0_ffn_wd"].transpose(0, 2, 1).reshape(NR, P, D).transpose(1, 0, 2),
        "norm_w": np.stack([a["L0_ffn_attn_norm_w"], a["L0_ffn_ffn_norm_w"]]).reshape(2, KD, P).transpose(2, 0, 1),
    }


def kernel(**inputs):
    import numpy as np
    import concourse.bacc as bacc
    from concourse.bass_utils import run_bass_kernel_spmd

    nc = bacc.Bacc("TRN2", target_bir_lowering=False, num_devices=1)
    arrays, args = {}, {}
    for name, a in layout({k: np.asarray(v) for k, v in inputs.items()}).items():
        a = np.ascontiguousarray(a)
        arrays[f"in_{name}"] = a
        args[name] = nc.dram_tensor(f"in_{name}", a.shape, mybir.dt.from_np(a.dtype), kind="ExternalInput").ap()
    out = nc.dram_tensor("out_y", (B, T, D), F32, kind="ExternalOutput").ap()
    program(nc, args, out)
    r = run_bass_kernel_spmd(nc, [arrays], core_ids=[0])
    return r.results[0]["out_y"]
```
